# Optimizing a Trainium2 kernel written in Bass

```python
import numpy as np
import jax
import jax.numpy as jnp

def _softmax(x, axis=-1):
    return jax.nn.softmax(x, axis=axis)

def _gelu(x):
    return jax.nn.gelu(x, approximate=True)

def _silu(x):
    return jax.nn.silu(x)

def _sigmoid(x):
    return jax.nn.sigmoid(x)

def _layernorm(x, axis=-1, eps=1e-05):
    m = jnp.mean(x, axis=axis, keepdims=True)
    v = jnp.var(x, axis=axis, keepdims=True)
    return (x - m) / jnp.sqrt(v + eps)

def _scatter_add(tgt, idx, src, axis=0):
    return tgt.at[idx].add(src)

def _segment_sum(src, seg, n):
    return jax.ops.segment_sum(src, seg, n)
kernel_name = 'mk_flamingo_gated_d2_seqx_r8_0c19dd'

def setup_inputs(seed: int=0):
    np.random.seed(seed)
    _w = jnp.asarray

    def _rec_inputs():
        import jax
        import jax.numpy as jnp
        _rk = jax.random.key(seed)
        x = -0.0003929 + 0.9999 * jax.random.normal(jax.random.fold_in(_rk, 1), (16, 64, 256), jnp.float32)
        _lenS = 64 - jax.random.randint(jax.random.fold_in(_rk, 7), (16,), 0, max(1, 64 // 4) + 1, jnp.int32)
        _lenS2 = 64 - jax.random.randint(jax.random.fold_in(_rk, 8), (16,), 0, max(1, 64 // 4) + 1, jnp.int32)
        _ctx_1024P = jax.random.normal(jax.random.fold_in(_rk, 11), (16, 16, 128), jnp.float32)
        _ctx_1024c = jax.random.dirichlet(jax.random.fold_in(_rk, 511), 0.3 * jnp.ones((16,), jnp.float32), (16, 64))
        _ctx_1024t = jnp.einsum('bsk,bkd->bsd', _ctx_1024c, _ctx_1024P)
        _ctx_1024t = _ctx_1024t * jax.lax.rsqrt(jnp.mean(jnp.square(_ctx_1024t)) + 1e-12) * 0.953939
        ctx_1024 = 0.000227908 + 0.99994 * (_ctx_1024t + 0.3 * jax.random.normal(jax.random.fold_in(_rk, 611), (16, 64, 128), jnp.float32))
        _validS = jnp.arange(64)[None, :] < _lenS[:, None]
        _validS2 = jnp.arange(64)[None, :] < _lenS2[:, None]
        _causal = jnp.tril(jnp.ones((64, 64), dtype=bool))
        mask_BxS2_bf1 = jnp.ones((16, 64), dtype=bool)
        _g = jax.random.normal(jax.random.fold_in(_rk, 9001), (2, 2), jnp.float32)
        _g = jnp.sign(_g) * jnp.maximum(jnp.abs(_g), 1.0) + (_g == 0) * 1.0
        g_xattn = _g[0]
        g_ffn = _g[1]
        return (x, ctx_1024, mask_BxS2_bf1, g_xattn, g_ffn)
    x, ctx_1024, mask_BxS2_bf1, g_xattn, g_ffn = _rec_inputs()

    def _L0_xattn_setup():
        import jax, jax.numpy as jnp
        import numpy as np
        EPS = 1e-05

        def rmsnorm(x, g, eps=EPS):
            var = jnp.mean(jnp.square(x), axis=-1, keepdims=True)
            return x * jax.lax.rsqrt(var + eps) * g
        key = jax.random.key(seed)
        ks = jax.random.split(key, 8)
        B, Sq, Skv = (2, 512, 64)
        dim, cdim, H, D = (256, 128, 16, 128)
        inner = H * D
        s = lambda f: 1.0 / np.sqrt(f)
        return {'hidden_states': jax.random.normal(ks[0], (B, Sq, dim), jnp.float32), 'encoder_hidden_states': jax.random.normal(ks[1], (B, Skv, cdim), jnp.float32), 'Wq': jax.random.normal(ks[2], (dim, inner), jnp.float32) * s(dim), 'Wk': jax.random.normal(ks[3], (cdim, inner), jnp.float32) * s(cdim), 'Wv': jax.random.normal(ks[4], (cdim, inner), jnp.float32) * s(cdim), 'Wo': jax.random.normal(ks[5], (inner, dim), jnp.float32) * s(inner), 'gq': jnp.ones((D,), jnp.float32), 'gk': jnp.ones((D,), jnp.float32)}
    _L0_xattn_all = _L0_xattn_setup()
    _L0_xattn_in = {k: v for k, v in _L0_xattn_all.items() if k in ('Wq', 'Wk', 'Wv', 'Wo', 'gq', 'gk')}
    del _L0_xattn_all

    def _L0_ffn_setup():
        import jax, jax.numpy as jnp
        import numpy as np
        EPS = 1e-07
        CURVATURE = 1.0
        MAX_NORM_RATIO = 0.99
        B, L, N, K = (4, 256, 256, 256)

        def _ternary_init(key, n, k):
            rand = jax.random.normal(key, (n, k), dtype=jnp.float32)
            threshold = 0.5 * jnp.mean(jnp.abs(rand))
            return jnp.where(rand > threshold, 1.0, jnp.where(rand < -threshold, -1.0, 0.0)).astype(jnp.float32)
        key = jax.random.key(seed)
        kx, kw = jax.random.split(key)
        x = jax.random.normal(kx, (B, L, N), dtype=jnp.float32)
        weight = _ternary_init(kw, N, K)
        scale = jnp.full((K,), 1.0 / np.sqrt(N), dtype=jnp.float32)
        return {'x': x, 'weight': weight, 'scale': scale}
    _L0_ffn_all = _L0_ffn_setup()
    _L0_ffn_in = {k: v for k, v in _L0_ffn_all.items() if k in ('weight', 'scale')}
    del _L0_ffn_all

    def _L1_xattn_setup():
        import jax, jax.numpy as jnp
        import numpy as np
        N_HEADS = 16
        N_KV_HEADS = 8
        HEAD_DIM = 128
        D_TEXT = 256
        D_VISION = 128
        GROUPS = N_HEADS // N_KV_HEADS
        key = jax.random.key(seed)
        ks = jax.random.split(key, 6)
        B, T_text, T_vis = (4, 256, 72)
        text_hidden = jax.random.normal(ks[0], (B, T_text, D_TEXT), dtype=jnp.float32)
        vision_tokens = jax.random.normal(ks[1], (B, T_vis, D_VISION), dtype=jnp.float32)
        vision_mask = jnp.ones((B, T_vis), dtype=bool)
        s = 0.02
        Wq = jax.random.normal(ks[2], (D_TEXT, N_HEADS * HEAD_DIM), dtype=jnp.float32) * s
        Wk = jax.random.normal(ks[3], (D_VISION, N_KV_HEADS * HEAD_DIM), dtype=jnp.float32) * s
        Wv = jax.random.normal(ks[4], (D_VISION, N_KV_HEADS * HEAD_DIM), dtype=jnp.float32) * s
        Wo = jax.random.normal(ks[5], (N_HEADS * HEAD_DIM, D_TEXT), dtype=jnp.float32) * s
        return {'text_hidden': text_hidden, 'vision_tokens': vision_tokens, 'vision_mask': vision_mask, 'Wq': Wq, 'Wk': Wk, 'Wv': Wv, 'Wo': Wo}
    _L1_xattn_all = _L1_xattn_setup()
    _L1_xattn_in = {k: v for k, v in _L1_xattn_all.items() if k in ('Wq', 'Wk', 'Wv', 'Wo')}
    del _L1_xattn_all

    def _L1_ffn_setup():
        import jax, jax.numpy as jnp
        import numpy as np
        B, S, HID = (2, 256, 256)
        NUM_HEADS = 16
        HEAD_DIM = HID // NUM_HEADS
        NUM_EXPERTS = 8
        TOP_K = 2
        INTER = 512
        EPS = 1e-05

        def _rmsnorm(x, w, eps=EPS):
            return x * jax.lax.rsqrt(jnp.mean(x * x, axis=-1, keepdims=True) + eps) * w

        def _moe(x_flat, Wr, Wg, Wu, Wd):
            T = x_flat.shape[0]
            logits = x_flat @ Wr.T
            top_logits, top_idx = jax.lax.top_k(logits, TOP_K)
            probs = jax.nn.softmax(top_logits, axis=-1)
            cw = jnp.zeros((T, NUM_EXPERTS), x_flat.dtype)
            cw = cw.at[jnp.arange(T)[:, None], top_idx].add(probs)
            hg = jnp.einsum('eih,th->eti', Wg, x_flat)
            hu = jnp.einsum('eih,th->eti', Wu, x_flat)
            y = jnp.einsum('ehi,eti->eth', Wd, jax.nn.silu(hg) * hu)
            return jnp.einsum('eth,te->th', y, cw)
        key = jax.random.key(seed)
        ks = jax.random.split(key, 12)
        sd_h = 1.0 / np.sqrt(HID)
        sd_i = 1.0 / np.sqrt(INTER)
        return {'x': jax.random.normal(ks[0], (B, S, HID), jnp.float32), 'Wq': jax.random.normal(ks[1], (HID, HID), jnp.float32) * sd_h, 'Wk': jax.random.normal(ks[2], (HID, HID), jnp.float32) * sd_h, 'Wv': jax.random.normal(ks[3], (HID, HID), jnp.float32) * sd_h, 'Wo': jax.random.normal(ks[4], (HID, HID), jnp.float32) * sd_h, 'w_ln1': jnp.ones((HID,), jnp.float32), 'w_ln2': jnp.ones((HID,), jnp.float32), 'Wr': jax.random.normal(ks[5], (NUM_EXPERTS, HID), jnp.float32) * sd_h, 'Wg': jax.random.normal(ks[6], (NUM_EXPERTS, INTER, HID), jnp.float32) * sd_h, 'Wu': jax.random.normal(ks[7], (NUM_EXPERTS, INTER, HID), jnp.float32) * sd_h, 'Wd': jax.random.normal(ks[8], (NUM_EXPERTS, HID, INTER), jnp.float32) * sd_i}
    _L1_ffn_all = _L1_ffn_setup()
    _L1_ffn_in = {k: v for k, v in _L1_ffn_all.items() if k in ('Wq', 'Wk', 'Wv', 'Wo', 'w_ln1', 'w_ln2', 'Wr', 'Wg', 'Wu', 'Wd')}
    del _L1_ffn_all
    return {'x': x, 'ctx_1024': ctx_1024, 'mask_BxS2_bf1': mask_BxS2_bf1, 'g_xattn': g_xattn, 'g_ffn': g_ffn, 'L0_xattn_Wq': _L0_xattn_in['Wq'], 'L0_xattn_Wk': _L0_xattn_in['Wk'], 'L0_xattn_Wv': _L0_xattn_in['Wv'], 'L0_xattn_Wo': _L0_xattn_in['Wo'], 'L0_xattn_gq': _L0_xattn_in['gq'], 'L0_xattn_gk': _L0_xattn_in['gk'], 'L0_ffn_weight': _L0_ffn_in['weight'], 'L0_ffn_scale': _L0_ffn_in['scale'], 'L1_xattn_Wq': _L1_xattn_in['Wq'], 'L1_xattn_Wk': _L1_xattn_in['Wk'], 'L1_xattn_Wv': _L1_xattn_in['Wv'], 'L1_xattn_Wo': _L1_xattn_in['Wo'], 'L1_ffn_Wq': _L1_ffn_in['Wq'], 'L1_ffn_Wk': _L1_ffn_in['Wk'], 'L1_ffn_Wv': _L1_ffn_in['Wv'], 'L1_ffn_Wo': _L1_ffn_in['Wo'], 'L1_ffn_w_ln1': _L1_ffn_in['w_ln1'], 'L1_ffn_w_ln2': _L1_ffn_in['w_ln2'], 'L1_ffn_Wr': _L1_ffn_in['Wr'], 'L1_ffn_Wg': _L1_ffn_in['Wg'], 'L1_ffn_Wu': _L1_ffn_in['Wu'], 'L1_ffn_Wd': _L1_ffn_in['Wd']}

def reference(x, ctx_1024, mask_BxS2_bf1, g_xattn, g_ffn, L0_xattn_Wq, L0_xattn_Wk, L0_xattn_Wv, L0_xattn_Wo, L0_xattn_gq, L0_xattn_gk, L0_ffn_weight, L0_ffn_scale, L1_xattn_Wq, L1_xattn_Wk, L1_xattn_Wv, L1_xattn_Wo, L1_ffn_Wq, L1_ffn_Wk, L1_ffn_Wv, L1_ffn_Wo, L1_ffn_w_ln1, L1_ffn_w_ln2, L1_ffn_Wr, L1_ffn_Wg, L1_ffn_Wu, L1_ffn_Wd):
    import jax
    import jax.numpy as jnp

    def _L0_xattn_ref(hidden_states, encoder_hidden_states, Wq, Wk, Wv, Wo, gq, gk):
        import jax, jax.numpy as jnp
        import numpy as np
        EPS = 1e-05

        def rmsnorm(x, g, eps=EPS):
            var = jnp.mean(jnp.square(x), axis=-1, keepdims=True)
            return x * jax.lax.rsqrt(var + eps) * g
        B, Sq, _ = hidden_states.shape
        Skv = encoder_hidden_states.shape[1]
        D = gq.shape[0]
        H = Wq.shape[1] // D
        scale = 1.0 / np.sqrt(D)
        q = (hidden_states @ Wq).reshape(B, Sq, H, D)
        k = (encoder_hidden_states @ Wk).reshape(B, Skv, H, D)
        v = (encoder_hidden_states @ Wv).reshape(B, Skv, H, D)
        q = rmsnorm(q, gq)
        k = rmsnorm(k, gk)
        scores = jnp.einsum('bqhd,bkhd->bhqk', q, k) * scale
        attn = jax.nn.softmax(scores, axis=-1)
        out = jnp.einsum('bhqk,bkhd->bqhd', attn, v)
        out = out.reshape(B, Sq, H * D)
        return out @ Wo

    def _L0_ffn_ref(x, weight, scale):
        import jax, jax.numpy as jnp
        import numpy as np
        EPS = 1e-07
        CURVATURE = 1.0
        MAX_NORM_RATIO = 0.99
        B, L, N, K = (4, 256, 256, 256)

        def _ternary_init(key, n, k):
            rand = jax.random.normal(key, (n, k), dtype=jnp.float32)
            threshold = 0.5 * jnp.mean(jnp.abs(rand))
            return jnp.where(rand > threshold, 1.0, jnp.where(rand < -threshold, -1.0, 0.0)).astype(jnp.float32)
        sqrt_c = jnp.sqrt(jnp.float32(CURVATURE))
        out = jnp.einsum('bln,nk->blk', x, weight) * scale
        v_norm = jnp.maximum(jnp.linalg.norm(out, axis=-1, keepdims=True), EPS)
        scaled_norm = sqrt_c * v_norm
        out = out * (jnp.tanh(scaled_norm) / (scaled_norm + EPS))
        max_norm = MAX_NORM_RATIO / sqrt_c
        o_norm = jnp.maximum(jnp.linalg.norm(out, axis=-1, keepdims=True), EPS)
        out = out * jnp.minimum(max_norm / o_norm, 1.0)
        return out.astype(x.dtype)

    def _L1_xattn_ref(text_hidden, vision_tokens, vision_mask, Wq, Wk, Wv, Wo):
        import jax, jax.numpy as jnp
        import numpy as np
        N_HEADS = 16
        N_KV_HEADS = 8
        HEAD_DIM = 128
        D_TEXT = 256
        D_VISION = 128
        GROUPS = N_HEADS // N_KV_HEADS
        B, T_text, _ = text_hidden.shape
        T_vis = vision_tokens.shape[1]
        scale = jnp.float32(np.sqrt(HEAD_DIM))
        q = (text_hidden @ Wq).reshape(B, T_text, N_HEADS, HEAD_DIM).transpose(0, 2, 1, 3)
        k = (vision_tokens @ Wk).reshape(B, T_vis, N_KV_HEADS, HEAD_DIM).transpose(0, 2, 1, 3)
        v = (vision_tokens @ Wv).reshape(B, T_vis, N_KV_HEADS, HEAD_DIM).transpose(0, 2, 1, 3)
        k = jnp.repeat(k, GROUPS, axis=1)
        v = jnp.repeat(v, GROUPS, axis=1)
        scores = jnp.einsum('bhtd,bhsd->bhts', q, k) / scale
        mask = vision_mask[:, None, None, :]
        scores = jnp.where(mask, scores, -jnp.inf)
        attn = jax.nn.softmax(scores, axis=-1)
        attn = jnp.nan_to_num(attn, nan=0.0)
        out = jnp.einsum('bhts,bhsd->bhtd', attn, v)
        out = out.transpose(0, 2, 1, 3).reshape(B, T_text, N_HEADS * HEAD_DIM)
        return out @ Wo

    def _L1_ffn_ref(x, Wq, Wk, Wv, Wo, w_ln1, w_ln2, Wr, Wg, Wu, Wd):
        import jax, jax.numpy as jnp
        import numpy as np
        B, S, HID = (2, 256, 256)
        NUM_HEADS = 16
        HEAD_DIM = HID // NUM_HEADS
        NUM_EXPERTS = 8
        TOP_K = 2
        INTER = 512
        EPS = 1e-05

        def _rmsnorm(x, w, eps=EPS):
            return x * jax.lax.rsqrt(jnp.mean(x * x, axis=-1, keepdims=True) + eps) * w

        def _moe(x_flat, Wr, Wg, Wu, Wd):
            T = x_flat.shape[0]
            logits = x_flat @ Wr.T
            top_logits, top_idx = jax.lax.top_k(logits, TOP_K)
            probs = jax.nn.softmax(top_logits, axis=-1)
            cw = jnp.zeros((T, NUM_EXPERTS), x_flat.dtype)
            cw = cw.at[jnp.arange(T)[:, None], top_idx].add(probs)
            hg = jnp.einsum('eih,th->eti', Wg, x_flat)
            hu = jnp.einsum('eih,th->eti', Wu, x_flat)
            y = jnp.einsum('ehi,eti->eth', Wd, jax.nn.silu(hg) * hu)
            return jnp.einsum('eth,te->th', y, cw)
        b, s, hid = x.shape
        residual = x
        xn = _rmsnorm(x, w_ln1)
        q = (xn @ Wq.T).reshape(b, s, NUM_HEADS, HEAD_DIM)
        k = (xn @ Wk.T).reshape(b, s, NUM_HEADS, HEAD_DIM)
        v = (xn @ Wv.T).reshape(b, s, NUM_HEADS, HEAD_DIM)
        scale = 1.0 / np.sqrt(HEAD_DIM)
        attn = jnp.einsum('bqhd,bkhd->bhqk', q, k) * scale
        causal = jnp.tril(jnp.ones((s, s), bool))
        attn = jnp.where(causal[None, None], attn, -jnp.inf)
        attn = jax.nn.softmax(attn, axis=-1)
        h = jnp.einsum('bhqk,bkhd->bqhd', attn, v).reshape(b, s, hid)
        x = residual + h @ Wo.T
        residual = x
        xn = _rmsnorm(x, w_ln2)
        moe_out = _moe(xn.reshape(-1, hid), Wr, Wg, Wu, Wd).reshape(b, s, hid)
        return residual + moe_out
    x = x + jnp.tanh(g_xattn[0]) * _L0_xattn_ref(_layernorm(x, axis=-1), ctx_1024, L0_xattn_Wq, L0_xattn_Wk, L0_xattn_Wv, L0_xattn_Wo, L0_xattn_gq, L0_xattn_gk)
    x = x + jnp.tanh(g_ffn[0]) * _L0_ffn_ref(_layernorm(x, axis=-1), L0_ffn_weight, L0_ffn_scale)
    x = x + jnp.tanh(g_xattn[1]) * _L1_xattn_ref(_layernorm(x, axis=-1), ctx_1024, mask_BxS2_bf1, L1_xattn_Wq, L1_xattn_Wk, L1_xattn_Wv, L1_xattn_Wo)
    x = x + jnp.tanh(g_ffn[1]) * _L1_ffn_ref(_layernorm(x, axis=-1), L1_ffn_Wq, L1_ffn_Wk, L1_ffn_Wv, L1_ffn_Wo, L1_ffn_w_ln1, L1_ffn_w_ln2, L1_ffn_Wr, L1_ffn_Wg, L1_ffn_Wu, L1_ffn_Wd)
    return x

_drawn_inputs = setup_inputs


def setup_inputs(seed=0):
    import zlib

    import numpy as np

    out = dict(_drawn_inputs(seed))
    spreads = {'g_ffn': (-1.0, 0.2),
     'L0_xattn_gq': (1.0, 0.2),
     'L0_xattn_gk': (1.0, 0.2),
     'L0_ffn_scale': (0.0625, 0.2),
     'L1_ffn_w_ln1': (1.0, 0.2),
     'L1_ffn_w_ln2': (1.0, 0.2)}
    factors = {'L1_xattn_Wq': 5.297}
    for name, (base, spread) in spreads.items():
        noise = np.random.default_rng([zlib.crc32(name.encode()), seed]).standard_normal(out[name].shape)
        drawn = base * np.exp(spread * noise) if base else spread * noise
        out[name] = jnp.asarray(drawn.astype(out[name].dtype))
    for name, factor in factors.items():
        out[name] = (out[name] * factor).astype(out[name].dtype)
    return out
```

```python
from contextlib import ExitStack

import concourse.bass as bass
from concourse import mybir

F32 = mybir.dt.float32
F32R = mybir.dt.float32r
I32 = mybir.dt.int32
U32 = mybir.dt.uint32
U8 = mybir.dt.uint8
ALU = mybir.AluOpType
ACT = mybir.ActivationFunctionType
AX = mybir.AxisListType

P = 128
NB, SQ, DM = 16, 64, 256
CD, HD = 128, 128
NH, NKV = 16, 8
NT = NB * SQ // P
KC = DM // P
HALF = NB * SQ // 2
PAIRS = NH // 2
UNITS = 2 * PAIRS
NE, INTER = 8, 512
IC = INTER // P
AH, AD = 16, 16
BANK = 512
BIG = 1e30
SMALL = 9 * 16


def build(nc, a):
    with ExitStack() as ctx:
        def sb(name, shape, dt=F32):
            return ctx.enter_context(nc.sbuf_tensor(name, shape, dt))

        def sem(name):
            return ctx.enter_context(nc.semaphore(name))

        x_res = sb("x_res", [P, NT, DM])
        ctxT = sb("ctxT", [P, NB * SQ])
        ctx_tok = sb("ctx_tok", [P, NT, CD])
        reg_a = sb("reg_a", [P, 4096])
        reg_b = sb("reg_b", [P, 2048])
        reg_c = sb("reg_c", [P, 6144])
        reg_d = sb("reg_d", [P, 4096])
        reg_e = sb("reg_e", [P, 4096])
        norm_buf = sb("norm_buf", [P, NT, DM])
        qT = sb("qT", [P, 2048])
        kT = sb("kT", [P, 2048])
        probs = sb("probs", [P, NB, SQ])
        probsT = sb("probsT", [P, 4, 2, P])
        ident = sb("ident", [P, P])
        swap = sb("swap", [P, P])
        causal = sb("causal", [P, SQ])
        head_mask = sb("head_mask", [P, 8])
        mask_add = sb("mask_add", [P, NB, SQ], mybir.dt.bfloat16)
        mask_any = sb("mask_any", [P, NB])
        gates = sb("gates", [P, 4])
        tgates = sb("tgates", [P, 4])
        gq_gk = sb("gq_gk", [P, 2])
        gqk = sb("gqk", [P, 1])
        ffn_scale = sb("ffn_scale", [P, DM])
        w_ln = sb("w_ln", [P, 2, KC])
        bn6 = sb("bn6", [P, NT, 6])
        mean_var = sb("mean_var", [P, NT, 2])
        var_eps = sb("var_eps", [P, NT])
        rstd = sb("rstd", [P, NT])
        neg_half = sb("neg_half", [P, 8])
        eps8 = sb("eps8", [P, 8])
        pos_half = sb("pos_half", [P, 8])
        sumsq = sb("sumsq", [P, 4, 4])
        sumsq_eps = sb("sumsq_eps", [P, 4, 4])
        rnorm = sb("rnorm", [P, 4, 4])
        smax = sb("smax", [P, 2, 8])
        ssum = sb("ssum", [P, 2, 8])
        srec = sb("srec", [P, 2, 8])
        row_max, row_sum, row_rec = (sb(n, [P, 2, AH]) for n in ("row_max", "row_sum", "row_rec"))
        iota8 = sb("iota8", [P, NE])
        logits = sb("logits", [P, NT, NE])
        top8 = sb("top8", [P, NT, 8])
        top8_at = sb("top8_at", [P, NT, 8], U32)
        top_at = sb("top_at", [P, NT, 2])
        chosen = sb("chosen", [P, 2, NE, NT])
        cw = sb("cw", [P, NE * NT])
        cw_now = sb("cw_now", [P, NT])
        wr_raw = sb("wr_raw", [P, KC, NE])
        tiny = sb("tiny", [P, 12, NT])

        xT_h = sb("xT_h", [P, KC, NB * SQ], F32R)
        xT_l = sb("xT_l", [P, KC, NB * SQ], F32R)
        w_r = sb("w_r", [P, 6144], F32R)
        wr_r = sb("wr_r", [P, 2, KC, NE], F32R)
        wr_h, wr_l = wr_r[:, 0, :, :], wr_r[:, 1, :, :]
        act_r = sb("act_r", [P, 8192], F32R)

        wq_raw = reg_a[:, :]
        wk_raw = reg_b[:, :]
        wf_raw = reg_b[:, 0:512]
        wo_raw = reg_c[:, 0:4096]
        wv_raw = reg_c[:, 4096:6144]
        wk1T = reg_c[:, 4096:5120]
        wv1T = reg_c[:, 5120:6144]
        vo0, m1, vo1 = reg_d, reg_d, reg_e
        nb_flat = norm_buf[:, :, :].rearrange("p t d -> p (t d)")
        squares = reg_e[:, 1024:2048].rearrange("p (s g d) -> p s g d", s=2, g=4)
        raw = nb_flat.rearrange("p (s g d) -> p s g d", s=4, g=4)
        qT_v = qT[:, :].rearrange("p (t b h q) -> p t b h q", t=NT, b=2, h=2)
        kT_v = kT[:, :].rearrange("p (t b h q) -> p t b h q", t=NT, b=2, h=2)
        wq_h, wq_l = w_r[:, 0:512].rearrange("p (k n) -> p k n", k=KC), w_r[:, 512:1024].rearrange("p (k n) -> p k n", k=KC)
        wk_h, wk_l = w_r[:, 1024:1280], w_r[:, 1280:1536]
        vo_h, vo_l = w_r[:, 1536:2048].rearrange("p (h n) -> p h n", h=2), w_r[:, 2048:2560].rearrange("p (h n) -> p h n", h=2)
        ctxT_h, ctxT_l = w_r[:, 2560:3584], w_r[:, 3584:4608]
        wf_h, wf_l = w_r[:, 4608:5120].rearrange("p (k n) -> p k n", k=KC), w_r[:, 5120:5632].rearrange("p (k n) -> p k n", k=KC)
        ac_h = act_r[:, 0:2048].rearrange("p (h t n) -> p h t n", h=2, t=NT)
        ac_l = act_r[:, 2048:4096].rearrange("p (h t n) -> p h t n", h=2, t=NT)

        mask_u8 = reg_e[:, 0:256].bitcast(U8)
        x1 = reg_a[:, 0:2048].rearrange("p (t d) -> p t d", t=NT)
        attn_raw = reg_a[:, 2048:4096]
        gu_raw, dn_raw = reg_c[:, 0:2048], reg_c[:, 2048:3072]
        silu_buf = qT[:, 0:1024].rearrange("p (s n) -> p s n", s=2)
        prod_buf = reg_b[:, :].rearrange("p (s n) -> p s n", s=IC)
        ffn_out = qT[:, :].rearrange("p (t d) -> p t d", t=NT)
        nb = norm_buf
        qT2 = qT[:, :].rearrange("p (k n) -> p k n", k=KC)
        kT2 = kT[:, :].rearrange("p (k n) -> p k n", k=KC)
        kexp = reg_e[:, :].rearrange("p (s b k n) -> p s b k n", s=2, b=2, k=KC)
        vexp = reg_d[:, :].rearrange("p (b n) -> p b n", b=NB)
        vexp_v = reg_d[:, :].rearrange("p (b g r d) -> p b g r d", b=NB, g=8, r=2)
        v_sb = reg_c[:, 3072:5120].rearrange("p (t n) -> p t n", t=NT)
        probs2 = reg_b[:, :].rearrange("p (s n) -> p s n", s=2)
        pt2 = [probs[:, :, :].rearrange("p b k -> p (b k)"), probsT[:, :, :, :].rearrange("p j b n -> p (j b n)")]
        aw_h = w_r[:, 0:2048].rearrange("p (w k n) -> p w k n", w=4, k=KC)
        aw_l = w_r[:, 2048:4096].rearrange("p (w k n) -> p w k n", w=4, k=KC)
        hT_h = act_r[:, 0:2048].rearrange("p (t k n) -> p t k n", t=NT, k=KC)
        hT_l = act_r[:, 2048:4096].rearrange("p (t k n) -> p t k n", t=NT, k=KC)
        gu_h = w_r[:, 0:2048].rearrange("p (i m k n) -> p i m k n", i=IC, m=2, k=KC)
        gu_l = w_r[:, 2048:4096].rearrange("p (i m k n) -> p i m k n", i=IC, m=2, k=KC)
        dn_h = w_r[:, 4096:5120].rearrange("p (i n) -> p i n", i=IC)
        dn_l = w_r[:, 5120:6144].rearrange("p (i n) -> p i n", i=IC)
        hx_h = act_r[:, 0:4096].rearrange("p (s i n) -> p s i n", s=2, i=IC)
        hx_l = act_r[:, 4096:8192].rearrange("p (s i n) -> p s i n", s=2, i=IC)

        psum = [ctx.enter_context(nc.psum_tensor(f"bank{i}", [P, BANK], F32)) for i in range(8)]
        Y = psum[0:4]
        R = psum[4:8]

        def y_tile(t):
            return Y[t // 2][:, DM * (t % 2):DM * (t % 2 + 1)]

        def f(ap):
            return ap.bitcast(F32)

        ld = {n: sem("ld_" + n) for n in (
            "x0", "x1", "ident", "ctx", "ctx_tok", "small", "wv0", "wo0", "wq0", "wk0", "wf",
            "wq1", "wk1", "wv1", "wo1", "attn", "wr", "gu", "dn")}
        stored = sem("stored")
        S = {n: sem(n) for n in (
            "stats", "var_eps", "rstd", "normed",
            "xT_mm", "xT_high", "xT_low",
            "halves", "zeroed", "gates", "gqk", "mask_add", "mask_any", "ctx_high", "ctx_low",
            "vo0_mm", "vo0", "m1_mm", "m1", "vo1_mm", "vo1",
            "wf_high", "wf_low", "ffn_mm", "ffn_sumsq", "ffn_len0", "ffn_len", "ffn_tanh",
            "aw_high", "aw_low", "qk2_mm", "q2", "k2", "v2_mm", "v2", "vs_mm", "vs_a", "vs_v",
            "kexp_v", "kexp_p", "s2_mm", "s2_free", "s2_sub", "s2_exp", "s2_rec", "s2_prob", "pt2_mm", "pt2_a", "pt2_v",
            "av2_mm", "h2", "hT_mm", "hT_high", "hT_low", "wo2_mm", "x2",
            "wr_high", "wr_low", "route_mm", "top_gap", "top_exp",
            "gu_high", "gu_low", "dn_high", "dn_low", "gu_mm", "silu", "prod", "act_high", "act_low", "y_mm", "y_added",
            "cw_now", "out_ready", "dve_step", "pool_step")}
        LAYER = ("wk_low", "proj", "squares", "sumsq", "sumsq_eps", "rnorm", "scaled", "qk_mm", "qk",
                 "scores", "masked", "smax", "sub", "exp", "ssum", "srec0", "srec", "prob",
                 "pt_mm", "pt_a", "pt_v", "av_mm", "ac_high", "ac_low", "o_mm", "w_high", "w_low", "vo_high", "vo_low")
        L0 = {k: sem("a0_" + k) for k in LAYER}
        L1 = {k: sem("a1_" + k) for k in LAYER if k not in ("wk_low", "squares", "sumsq", "sumsq_eps", "rnorm", "scaled", "qk_mm")}

        class Chain:
            def __init__(self, eng, s):
                self.eng, self.s, self.n = eng, s, 0

            def __call__(self, ins):
                ins.then_inc(self.s, 1)
                self.n += 1
                self.eng.wait_ge(self.s, self.n)

        def v_parts(bank):
            return bank[:, :].rearrange("p (t g r d) -> p t g r d", t=2, g=8, r=2)

        def xT_half(part, k, hf):
            return part[:, k, HALF * hf:HALF * (hf + 1)]

        block = ctx.enter_context(nc.Block())

        @block.sync
        def _(sp):
            def load(name, dst, src):
                sp.dma_start(dst, src).then_inc(ld[name], 16)

            xv = a["x"].rearrange("(t p) d -> p t d", p=P)
            load("x0", x_res[:, 0:4, :], xv[:, 0:4, :])
            load("x1", x_res[:, 4:8, :], xv[:, 4:8, :])
            load("ident", ident[:, :], a["c_ident"])
            load("wv0", wv_raw, a["wv0T"])
            load("wo0", wo_raw, a["wo0"])
            load("wq0", wq_raw, a["wq0"])
            load("wk0", wk_raw, a["wk0"])
            sp.wait_ge(S["vo0_mm"], 8)
            load("wo1", wo_raw, a["wo1"])
            load("wk1", wk1T, a["wk1T"])
            load("wv1", wv1T, a["wv1T"])
            sp.wait_ge(L0["w_low"], PAIRS)
            load("wq1", wq_raw, a["wq1T"])
            load("wf", wf_raw, a["wf"])
            sp.wait_ge(S["m1_mm"], 8)
            load("attn", attn_raw, a["wattn"])
            sp.wait_ge(S["vo1_mm"], 8)
            load("gu", gu_raw, a["gu"][0])
            load("dn", dn_raw, a["dn"][0])
            with sp.Fori(1, NE) as e:
                sp.wait_ge(S["gu_low"], e * IC)
                load("gu", gu_raw, a["gu"][bass.ds(e, 1)].rearrange("e p n -> (e p) n"))
                sp.wait_ge(S["dn_low"], e)
                load("dn", dn_raw, a["dn"][bass.ds(e, 1)].rearrange("e p n -> (e p) n"))
            ov = a["out"].rearrange("(t p) d -> p t d", p=P)
            for hf in range(2):
                sp.wait_ge(S["out_ready"], hf + 1)
                sp.dma_start(ov[:, 4 * hf:4 * hf + 4, :], norm_buf[:, 4 * hf:4 * hf + 4, :]).then_inc(stored, 16)
            sp.wait_ge(stored, 32)

        class Unit:
            def __init__(self, i, c):
                self.i, self.c = i, c

            def at(self, off):
                return Unit(self.i, self.c + off)

            def there(self):
                return not isinstance(self.i, int) or 0 <= 2 * self.i + self.c < UNITS

            def count(self, per, k):
                return self.i * (2 * per) + (self.c * per + k)

            def after_zero(self, per, k):
                return not isinstance(self.i, int) or self.count(per, k) > 0

            def half(self):
                return self.c % 2

            def first(self):
                return isinstance(self.i, int) and 2 * self.i + self.c in (0, 1)

        def pair_there(j):
            return not isinstance(j, int) or 0 <= j < PAIRS

        def pipeline(eng, step, lead):
            if lead == 3:
                step(Unit(-2, 1))
            for i in (-1, 0, 1):
                for c in (0, 1):
                    step(Unit(i, c))
            with eng.Fori(2, PAIRS - 2) as i:
                for c in (0, 1):
                    step(Unit(i, c))
            for i in (PAIRS - 2, PAIRS - 1, PAIRS):
                for c in (0, 1):
                    step(Unit(i, c))

        @block.tensor
        def _(pe):
            def split_mm(out, lh, ll, rh, rl, start, stop):
                pe.matmul(out, lh, rh, start=start, stop=False, skip_group_check=True)
                pe.matmul(out, lh, rl, start=False, stop=False, skip_group_check=True)
                return pe.matmul(out, ll, rh, start=False, stop=stop, skip_group_check=True)

            def x_transposes(norm, turn):
                for hf in range(2):
                    for k in range(KC):
                        for t in range(4):
                            pe.wait_ge(S["normed"], 8 * norm + 4 * hf + t + 1)
                            ins = pe.transpose(R[2 * hf + k][:, P * t:P * (t + 1)],
                                               nb[:, 4 * hf + t, P * k:P * (k + 1)], ident[:, :])
                        ins.then_inc(S["xT_mm"], 1)

            pe.wait_ge(ld["wv0"], 16)
            pe.wait_ge(ld["wo0"], 16)
            for g in range(PAIRS):
                if g >= 4:
                    pe.wait_ge(S["vo0"], g - 3)
                for hh in range(2):
                    h = 2 * g + hh
                    ins = pe.matmul(Y[g % 4][:, DM * hh:DM * (hh + 1)], wv_raw[:, CD * h:CD * (h + 1)],
                                    wo_raw[:, DM * h:DM * (h + 1)], start=True, stop=True)
                ins.then_inc(S["vo0_mm"], 1)
            pe.wait_ge(ld["ident"], 16)
            x_transposes(0, 0)

            def probs_T(L, n, bank):
                pe.wait_ge(L["prob"], n.count(1, 1))
                for j in range(4):
                    b = 8 * n.half() + 2 * j
                    ins = pe.transpose(bank[:, P * j:P * (j + 1)],
                                       probs[:, b:b + 2, :].rearrange("p b k -> p (b k)"), ident[:, :])
                ins.then_inc(L["pt_mm"], 1)

            def attend(L, n, part, bank):
                pe.wait_ge(L["pt_a"], n.count(1, 1))
                pe.wait_ge(L["pt_v"], n.count(1, 1))
                for jj in range(2):
                    j = 2 * part + jj
                    ins = pe.matmul(bank[:, 256 * jj:256 * (jj + 1)], ctx_tok[:, 4 * n.half() + j, :],
                                    probsT[:, j, :, :].rearrange("p b (h q) -> p h b q", h=2), start=True, stop=True)
                ins.then_inc(L["av_mm"], 1)

            def project_out(L, n, tiles):
                pe.wait_ge(L["ac_low"], n.count(2, 2))
                pe.wait_ge(L["vo_low"], n.i + (n.c // 2 + 1))
                for j in tiles:
                    t = 4 * n.half() + j
                    for hh in range(2):
                        ins = split_mm(y_tile(t), ac_h[:, hh, t, :], ac_l[:, hh, t, :], vo_h[:, hh, :], vo_l[:, hh, :],
                                       start=n.first() and t % 2 == 0 and hh == 0, stop=False)
                if tiles[-1] == 3:
                    ins.then_inc(L["o_mm"], 1)

            def project_qk(u, j, bank):
                t = 4 * u.half() + j
                if j == 0:
                    pe.wait_ge(L0["w_low"], u.i + (u.c // 2 + 1))
                    pe.wait_ge(L0["wk_low"], u.i + (u.c // 2 + 1))
                for k in range(KC):
                    split_mm(bank[:, 0:256], xT_h[:, k, P * t:P * (t + 1)], xT_l[:, k, P * t:P * (t + 1)],
                             wq_h[:, k, :], wq_l[:, k, :], k == 0, k == KC - 1)
                split_mm(bank[:, 256:512], ctxT_h[:, P * t:P * (t + 1)], ctxT_l[:, P * t:P * (t + 1)],
                         wk_h, wk_l, True, True).then_inc(L0["proj"], 1)

            def qk_T(u, j, bank):
                pe.wait_ge(L0["scaled"], u.count(4, j + 1))
                for g in range(4):
                    ins = pe.transpose(bank[:, P * g:P * (g + 1)], raw[:, j, g, :], ident[:, :])
                ins.then_inc(L0["qk_mm"], 1)

            def step0(n):
                u1, u2, u3, um = n.at(1), n.at(2), n.at(3), n.at(-1)
                if u1.there():
                    pe.wait_ge(L0["qk"], u1.count(4, 4))
                    for j in range(4):
                        for b in range(2):
                            for hh in range(2):
                                t = 4 * u1.half() + j
                                ins = pe.matmul(R[0][64 * hh:64 * (hh + 1), 64 * (2 * j + b):64 * (2 * j + b + 1)],
                                                qT_v[:, t, b, hh, :], kT_v[:, t, b, hh, :], start=True, stop=True)
                    ins.then_inc(L0["scores"], 1)
                if u2.there():
                    if um.there():
                        pe.wait_ge(L0["ac_low"], um.count(2, 2))
                    qk_T(u2, 0, R[1])
                    pe.wait_ge(L0["squares"], u2.count(4, 3))
                    qk_T(u2, 1, R[2])
                    pe.wait_ge(L0["squares"], u2.count(4, 4))
                if n.there():
                    probs_T(L0, n, R[3])
                if u3.there():
                    if u1.there():
                        pe.wait_ge(L0["sub"], u1.count(1, 1))
                    project_qk(u3, 0, R[0])
                if u2.there():
                    pe.wait_ge(L0["qk"], u2.count(4, 1))
                    qk_T(u2, 2, R[1])
                    pe.wait_ge(L0["qk"], u2.count(4, 2))
                if n.there():
                    if um.there():
                        pe.wait_ge(L0["ac_low"], um.count(2, 2))
                    attend(L0, n, 0, R[2])
                if u3.there():
                    project_qk(u3, 1, R[3])
                if um.there():
                    project_out(L0, um, (0, 1))
                if u2.there():
                    if u3.there():
                        pe.wait_ge(L0["squares"], u3.count(4, 1))
                    else:
                        pe.wait_ge(L0["sub"], u1.count(1, 1))
                    qk_T(u2, 3, R[0])
                    pe.wait_ge(L0["qk"], u2.count(4, 3))
                if n.there():
                    attend(L0, n, 1, R[1])
                if u3.there():
                    if n.there():
                        pe.wait_ge(L0["ac_low"], n.count(2, 1))
                    project_qk(u3, 2, R[2])
                if um.there():
                    project_out(L0, um, (2,))
                if u3.there():
                    pe.wait_ge(L0["squares"], u3.count(4, 2))
                    project_qk(u3, 3, R[3])
                if um.there():
                    project_out(L0, um, (3,))

            pe.wait_ge(S["xT_low"], 4)
            pe.wait_ge(S["ctx_low"], 1)
            pe.wait_ge(ld["ctx_tok"], 16)
            pipeline(pe, step0, 3)

            pe.wait_ge(ld["wq1"], 16)
            pe.wait_ge(ld["wk1"], 16)
            pe.wait_ge(ld["wv1"], 16)
            pe.wait_ge(ld["wo1"], 16)
            for g in range(PAIRS):
                if g >= 4:
                    pe.wait_ge(S["m1"], g - 3)
                for k in range(KC):
                    for hh in range(2):
                        o = P * (2 * k + hh)
                        w = DM * (2 * g + hh) + P * k
                        ins = pe.matmul(R[g % 4][:, o:o + P], wq_raw[:, w:w + P], wk1T[:, CD * g:CD * (g + 1)],
                                        start=True, stop=True)
                ins.then_inc(S["m1_mm"], 1)
            for g in range(PAIRS):
                if g < 4:
                    pe.wait_ge(S["m1"], g + 5)
                else:
                    pe.wait_ge(S["vo1"], g - 3)
                for hh in range(2):
                    h = 2 * g + hh
                    ins = pe.matmul(R[g % 4][:, DM * hh:DM * (hh + 1)], wv1T[:, CD * g:CD * (g + 1)],
                                    wo_raw[:, DM * h:DM * (h + 1)], start=True, stop=True)
                ins.then_inc(S["vo1_mm"], 1)

            pe.wait_ge(S["vo1"], 8)
            x_transposes(1, 1)
            pe.wait_ge(S["xT_low"], 8)
            pe.wait_ge(S["wf_low"], 1)
            for t in range(NT):
                for k in range(KC):
                    ins = split_mm(y_tile(t), xT_h[:, k, P * t:P * (t + 1)], xT_l[:, k, P * t:P * (t + 1)],
                                   wf_h[:, k, :], wf_l[:, k, :], k == 0, k == KC - 1)
                ins.then_inc(S["ffn_mm"], 1)
            x_transposes(2, 2)

            def project_t(u, hh, bank):
                if hh == 0:
                    pe.wait_ge(L1["w_low"], u.i + (u.c // 2 + 1))
                for k in range(KC):
                    ins = split_mm(bank[:, :], wq_h[:, k, P * hh:P * (hh + 1)], wq_l[:, k, P * hh:P * (hh + 1)],
                                   xT_half(xT_h, k, u.half()), xT_half(xT_l, k, u.half()), k == 0, k == KC - 1)
                ins.then_inc(L1["proj"], 1)

            def step1(n):
                u1, u2, um = n.at(1), n.at(2), n.at(-1)
                B = [R[(2 * n.half() + k) % 4] for k in range(4)]
                if u1.there():
                    pe.wait_ge(L1["qk"], u1.count(2, 2))
                    for j in range(4):
                        for b in range(2):
                            t = 4 * u1.half() + j
                            ins = pe.matmul(B[0][:, 64 * (2 * j + b):64 * (2 * j + b + 1)],
                                            qT_v[:, t, b, :, :].rearrange("p h q -> p (h q)"),
                                            ctxT[:, SQ * (2 * t + b):SQ * (2 * t + b + 1)], start=True, stop=True)
                    ins.then_inc(L1["scores"], 1)
                if u2.there():
                    project_t(u2, 0, B[1])
                if n.there():
                    if um.there():
                        pe.wait_ge(L1["ac_low"], um.count(2, 1))
                    probs_T(L1, n, B[2])
                if um.there():
                    project_out(L1, um, (0, 1))
                if u2.there():
                    project_t(u2, 1, B[3])
                if n.there():
                    if u1.there():
                        pe.wait_ge(L1["masked"], u1.count(1, 1))
                    attend(L1, n, 0, B[0])
                    if u2.there():
                        pe.wait_ge(L1["qk"], u2.count(2, 1))
                    attend(L1, n, 1, B[1])
                if um.there():
                    project_out(L1, um, (2, 3))

            pe.wait_ge(S["xT_low"], 12)
            pipeline(pe, step1, 2)

            x_transposes(4, 3)
            pe.wait_ge(S["xT_low"], 16)
            pe.wait_ge(S["aw_low"], 1)
            use = 0
            for w, what in ((0, "q2"), (1, "k2")):
                for oc in range(KC):
                    for hf in range(2):
                        if use >= 4:
                            pe.wait_ge(S["q2"], use - 3)
                        for k in range(KC):
                            ins = split_mm(R[use % 4][:, :], aw_h[:, w, k, P * oc:P * (oc + 1)],
                                           aw_l[:, w, k, P * oc:P * (oc + 1)],
                                           xT_half(xT_h, k, hf), xT_half(xT_l, k, hf), k == 0, k == KC - 1)
                        ins.then_inc(S["qk2_mm"], 1)
                        use += 1
            for g in range(4):
                pe.wait_ge(S["k2"], g + 1)
                for tt in range(2):
                    c = P * (2 * g + tt)
                    for k in range(KC):
                        ins = split_mm(R[g][:, DM * tt:DM * (tt + 1)], xT_h[:, k, c:c + P], xT_l[:, k, c:c + P],
                                       aw_h[:, 2, k, :], aw_l[:, 2, k, :], k == 0, k == KC - 1)
                ins.then_inc(S["v2_mm"], 1)
            for g in range(4):
                pe.wait_ge(S["v2"], g + 1)
                pe.matmul(R[g][:, :], swap[:, :], v_sb[:, 2 * g:2 * g + 2, :].rearrange("p t n -> p (t n)"),
                          start=True, stop=True).then_inc(S["vs_mm"], 1)
            pe.wait_ge(S["vs_a"], 4)
            pe.wait_ge(S["vs_v"], 4)

            def self_scores(t):
                pe.wait_ge(S["kexp_v"], t + 1)
                pe.wait_ge(S["kexp_p"], t + 1)
                if t >= 2:
                    pe.wait_ge(S["s2_free"], t - 1)
                for oc in range(KC):
                    for b in range(2):
                        c = SQ * (2 * t + b)
                        ins = pe.matmul(Y[2 * (t % 2) + oc][64 * b:64 * (b + 1), :], qT2[:, oc, c:c + SQ],
                                        kexp[:, t % 2, b, oc, :], start=True, stop=True)
                ins.then_inc(S["s2_mm"], 1)

            def self_out(t):
                pe.wait_ge(S["h2"], t + 1)
                if t >= 1:
                    pe.wait_ge(S["x2"], t)
                for k in range(KC):
                    ins = pe.transpose(R[3][:, P * k:P * (k + 1)], nb[:, t, P * k:P * (k + 1)], ident[:, :])
                ins.then_inc(S["hT_mm"], 1)

            def self_proj(t):
                pe.wait_ge(S["hT_low"], t + 1)
                for k in range(KC):
                    ins = split_mm(R[3][:, DM:2 * DM], hT_h[:, t, k, :], hT_l[:, t, k, :],
                                   aw_h[:, 3, k, :], aw_l[:, 3, k, :], k == 0, k == KC - 1)
                ins.then_inc(S["wo2_mm"], 1)

            self_scores(0)
            for t in range(NT + 1):
                if t + 1 < NT:
                    self_scores(t + 1)
                if t >= 1:
                    self_out(t - 1)
                if t < NT:
                    pe.wait_ge(S["s2_prob"], t + 1)
                    if t >= 1:
                        pe.wait_ge(S["pt2_a"], t)
                        pe.wait_ge(S["pt2_v"], t)
                    for g in range(8):
                        ins = pe.transpose(R[g // 4][:, P * (g % 4):P * (g % 4 + 1)],
                                           probs2[:, t % 2, P * g:P * (g + 1)], ident[:, :])
                    ins.then_inc(S["pt2_mm"], 1)
                if t >= 1:
                    self_proj(t - 1)
                if t < NT:
                    pe.wait_ge(S["pt2_a"], t + 1)
                    pe.wait_ge(S["pt2_v"], t + 1)
                    for b in range(2):
                        for g in range(8):
                            ins = pe.matmul(R[2][64 * b:64 * (b + 1), 32 * g:32 * (g + 1)],
                                            pt2[t % 2][:, P * g + 64 * b:P * g + 64 * (b + 1)],
                                            vexp[:, 2 * t + b, 32 * g:32 * (g + 1)], start=True, stop=True)
                    ins.then_inc(S["av2_mm"], 1)

            pe.wait_ge(S["x2"], NT)
            x_transposes(5, 4)
            pe.wait_ge(S["xT_low"], 20)
            pe.wait_ge(S["wr_low"], 1)
            for t in range(NT):
                for k in range(KC):
                    ins = split_mm(Y[3][:, NE * t:NE * (t + 1)], xT_h[:, k, P * t:P * (t + 1)],
                                   xT_l[:, k, P * t:P * (t + 1)], wr_h[:, k, :], wr_l[:, k, :], k == 0, k == KC - 1)
            ins.then_inc(S["route_mm"], 1)

            def gate_up(u):
                for ic in range(IC):
                    pe.wait_ge(S["gu_low"], u.i * IC + (u.c // 2 * IC + ic + 1))
                    if u.after_zero(4, ic - 1):
                        pe.wait_ge(S["prod"], u.count(4, ic - 1))
                    for m in range(2):
                        for k in range(KC):
                            ins = split_mm(R[2 * (ic % 2) + m][:, :], gu_h[:, ic, m, k, :], gu_l[:, ic, m, k, :],
                                           xT_half(xT_h, k, u.half()), xT_half(xT_l, k, u.half()), k == 0, k == KC - 1)
                        ins.then_inc(S["gu_mm"], 1)

            def down(u):
                pe.wait_ge(S["dn_low"], u.i + 1)
                pe.wait_ge(S["act_low"], u.count(4, 4))
                if u.after_zero(4, -4):
                    pe.wait_ge(S["y_added"], u.count(4, -4))
                for j in range(4):
                    t = 4 * u.half() + j
                    for ic in range(IC):
                        ins = split_mm(y_tile(t), hx_h[:, u.half(), ic, P * j:P * (j + 1)],
                                       hx_l[:, u.half(), ic, P * j:P * (j + 1)], dn_h[:, ic, :], dn_l[:, ic, :],
                                       ic == 0, ic == IC - 1)
                    ins.then_inc(S["y_mm"], 1)

            gate_up(Unit(0, 0))
            pe.wait_ge(S["top_gap"], 1)
            for c in range(2):
                gate_up(Unit(0, c + 1))
                down(Unit(0, c))
            with pe.Fori(1, NE - 1) as e:
                for c in range(2):
                    gate_up(Unit(e, c + 1))
                    down(Unit(e, c))
            gate_up(Unit(NE - 1, 1))
            down(Unit(NE - 1, 0))
            down(Unit(NE - 1, 1))

        @block.scalar
        def _(act):
            def copy(out, in_, scale=None):
                if scale is None:
                    return act.activation(out, in_, ACT.Copy)
                return act.activation(out, in_, ACT.Copy, scale=scale)

            def load(name, dst, src):
                act.dma_start(dst, src).then_inc(ld[name], 16)

            def x_high(turn, w=None):
                for hf in range(2):
                    for k in range(KC):
                        act.wait_ge(S["xT_mm"], 4 * turn + 2 * hf + k + 1)
                        copy(xT_half(xT_h, k, hf), R[2 * hf + k][:, :],
                             None if w is None else w_ln[:, w, k:k + 1]).then_inc(S["xT_high"], 1)

            load("ctx", ctxT[:, :], a["ctxT"])
            load("ctx_tok", ctx_tok[:, :, :], a["ctx"].rearrange("(t p) c -> p t c", p=P))
            for dst, src in ((gates[:, :], a["gates"].unsqueeze(0).broadcast_to([P, 4])),
                             (gq_gk[:, :], a["gqk"]), (causal[:, :], a["c_causal"]), (head_mask[:, :], a["c_heads"]),
                             (iota8[:, :], a["c_iota"]), (swap[:, :], a["c_swap"]), (w_ln[:, :, :], a["w_ln"]),
                             (ffn_scale[:, :], a["ffn_scale"].unsqueeze(0).broadcast_to([P, DM])),
                             (mask_u8[:, :], a["mask"].unsqueeze(0).broadcast_to([P, NB * SQ]))):
                load("small", dst, src)
            load("wr", wr_raw[:, :, :], a["wr"])
            act.wait_ge(ld["small"], SMALL)
            act.activation(tgates[:, :], gates[:, :], ACT.Tanh).then_inc(S["gates"], 1)
            act.wait_ge(ld["ctx"], 16)
            copy(ctxT_h, ctxT[:, :]).then_inc(S["ctx_high"], 1)
            for g in range(PAIRS):
                act.wait_ge(S["vo0_mm"], g + 1)
                copy(vo0[:, 512 * g:512 * (g + 1)], Y[g % 4][:, :]).then_inc(S["vo0"], 1)
            x_high(0)

            def vo_high(L, src, n):
                if n.c == 1 and pair_there(n.i):
                    if not isinstance(n.i, int) or n.i > 0:
                        act.wait_ge(L["o_mm"], n.i * 2)
                    copy(vo_h.rearrange("p h n -> p (h n)"), src[:, bass.ds(n.i * 512, 512)]).then_inc(L["vo_high"], 1)

            def split_exp(L, u1):
                act.wait_ge(L["sub"], u1.count(1, 1))
                p = probs[:, 8 * u1.half():8 * u1.half() + 8, :]
                act.activation(p, p, ACT.Exp, scale=float(HD) ** -0.5).then_inc(L["exp"], 1)

            def probs_T(L, n, bank):
                act.wait_ge(L["pt_mm"], n.count(1, 1))
                copy(probsT[0:64, :, 0, :], bank[0:64, :].rearrange("p (j n) -> p j n", j=4)).then_inc(L["pt_a"], 1)

            def attended(L, n, part, bank):
                act.wait_ge(L["av_mm"], n.count(2, part + 1))
                t = 4 * n.half() + 2 * part
                copy(ac_h[:, :, t:t + 2, :].rearrange("p h t n -> p t h n"),
                     bank[:, :].rearrange("p (t h n) -> p t h n", t=2, h=2)).then_inc(L["ac_high"], 1)

            def w_high0(j):
                copy(w_r[:, 0:512], wq_raw[:, bass.ds(j * 512, 512)])
                copy(wk_h, wk_raw[:, bass.ds(j * 256, 256)]).then_inc(L0["w_high"], 1)

            def step0(n):
                u1, u2, u3, um = n.at(1), n.at(2), n.at(3), n.at(-1)
                vo_high(L0, vo0, n)

                def take(j, bank):
                    act.wait_ge(L0["proj"], u3.count(4, j + 1))
                    copy(raw[:, j, :, :].rearrange("p g d -> p (g d)"), bank[:, :])
                    if u3.after_zero(4, j - 1):
                        act.wait_ge(L0["sumsq"], u3.count(4, j - 1))
                    act.activation(squares[:, j % 2, :, :].rearrange("p g d -> p (g d)"), bank[:, :],
                                   ACT.Square, scale=float(HD) ** -0.5).then_inc(L0["squares"], 1)

                def qk_out(j, bank):
                    act.wait_ge(L0["qk_mm"], u2.count(4, j + 1))
                    t = 4 * u2.half() + j
                    for g, dst, scale in ((0, qT_v, gqk[:, 0:1]), (1, kT_v, None)):
                        ins = copy(dst[:, t, :, :, :].rearrange("p b h q -> p h b q"),
                                   bank[:, 256 * g:256 * (g + 1)].rearrange("p (h b q) -> p h b q", h=2, b=2), scale)
                    ins.then_inc(L0["qk"], 1)

                if u2.there():
                    qk_out(0, R[1])
                    qk_out(1, R[2])
                if n.there():
                    probs_T(L0, n, R[3])
                if u1.there():
                    split_exp(L0, u1)
                if u3.there():
                    take(0, R[0])
                if u2.there():
                    qk_out(2, R[1])
                if n.there():
                    attended(L0, n, 0, R[2])
                if u3.there():
                    take(1, R[3])
                if u2.there():
                    qk_out(3, R[0])
                if n.there():
                    attended(L0, n, 1, R[1])
                if u3.there():
                    take(2, R[2])
                    take(3, R[3])
                if n.c == 0 and pair_there(n.i + 2):
                    w_high0(n.i + 2)

            act.wait_ge(ld["wq0"], 16)
            act.wait_ge(ld["wk0"], 16)
            act.wait_ge(S["gqk"], 1)
            act.wait_ge(S["vo0"], PAIRS)
            w_high0(0)
            pipeline(act, step0, 3)

            act.wait_ge(ld["wf"], 16)
            copy(w_r[:, 4608:5120], wf_raw).then_inc(S["wf_high"], 1)
            act.wait_ge(L0["vo_low"], PAIRS)
            for g in range(PAIRS):
                act.wait_ge(S["m1_mm"], g + 1)
                copy(m1[:, 512 * g:512 * (g + 1)], R[g % 4][:, :]).then_inc(S["m1"], 1)
            for g in range(PAIRS):
                act.wait_ge(S["vo1_mm"], g + 1)
                copy(vo1[:, 512 * g:512 * (g + 1)], R[g % 4][:, :]).then_inc(S["vo1"], 1)
            x_high(1)
            act.wait_ge(S["ffn_len"], 1)
            act.activation(tiny[:, 2, :], tiny[:, 1, :], ACT.Tanh).then_inc(S["ffn_tanh"], 1)
            x_high(2)

            def w_high1(j):
                copy(w_r[:, 0:512], m1[:, bass.ds(j * 512, 512)]).then_inc(L1["w_high"], 1)

            def step1(n):
                u1, u2, um = n.at(1), n.at(2), n.at(-1)
                B = [R[(2 * n.half() + k) % 4] for k in range(4)]
                vo_high(L1, vo1, n)

                def t_out(hh, bank):
                    act.wait_ge(L1["proj"], u2.count(2, hh + 1))
                    t = 4 * u2.half()
                    copy(qT_v[:, t:t + 4, :, hh, :].rearrange("p t b q -> p (t b) q"),
                         bank[:, :].rearrange("p (tb q) -> p tb q", q=SQ)).then_inc(L1["qk"], 1)

                if u2.there():
                    t_out(0, B[1])
                if u1.there():
                    split_exp(L1, u1)
                if n.there():
                    probs_T(L1, n, B[2])
                if u2.there():
                    t_out(1, B[3])
                if n.c == 1 and pair_there(n.i + 2):
                    act.wait_ge(L1["proj"], u2.count(2, 2))
                    w_high1(n.i + 2)
                if n.there():
                    attended(L1, n, 0, B[0])
                    attended(L1, n, 1, B[1])

            act.wait_ge(S["vo1"], PAIRS)
            w_high1(0)
            pipeline(act, step1, 2)

            act.wait_ge(ld["attn"], 16)
            act.wait_ge(L1["o_mm"], UNITS)
            copy(w_r[:, 0:2048], attn_raw).then_inc(S["aw_high"], 1)
            x_high(3, 0)
            for use in range(4):
                act.wait_ge(S["qk2_mm"], use + 1)
                copy(qT2[:, use // 2, HALF * (use % 2):HALF * (use % 2 + 1)], R[use][:, :]).then_inc(S["q2"], 1)
            for g in range(4):
                act.wait_ge(S["v2_mm"], g + 1)
                copy(v_sb[:, 2 * g:2 * g + 2, :].rearrange("p t n -> p (t n)"), R[g][:, :]).then_inc(S["v2"], 1)
            act.wait_ge(S["zeroed"], 3)
            for g in range(4):
                act.wait_ge(S["vs_mm"], g + 1)
                copy(vexp_v[0:64, 4 * g + 1:4 * g + 4:2, :, 0, :], v_parts(R[g])[0:64, :, :, 0, :]).then_inc(S["vs_a"], 1)

            def self_exp(t):
                act.wait_ge(S["s2_sub"], t + 1)
                act.activation(probs2[:, t % 2, :], probs2[:, t % 2, :], ACT.Exp,
                               scale=float(AD) ** -0.5).then_inc(S["s2_exp"], 1)

            self_exp(0)
            for t in range(NT + 1):
                if t + 1 < NT:
                    self_exp(t + 1)
                if t >= 1:
                    act.wait_ge(S["hT_mm"], t)
                    copy(hT_h[:, t - 1, :, :].rearrange("p k n -> p (k n)"), R[3][:, 0:DM]).then_inc(S["hT_high"], 1)
                if t < NT:
                    act.wait_ge(S["pt2_mm"], t + 1)
                    copy(pt2[t % 2][:, 0:512], R[0][:, :]).then_inc(S["pt2_a"], 1)
                    act.wait_ge(S["av2_mm"], t + 1)
                    copy(nb[:, t, :], R[2][:, 0:DM]).then_inc(S["h2"], 1)

            act.wait_ge(ld["wr"], 16)
            copy(wr_h.rearrange("p k n -> p (k n)"), wr_raw[:, :, :].rearrange("p k n -> p (k n)")).then_inc(S["wr_high"], 1)
            act.wait_ge(ld["gu"], 16)
            act.wait_ge(S["wo2_mm"], NT)
            for ic in range(IC):
                copy(w_r[:, 512 * ic:512 * (ic + 1)], gu_raw[:, 512 * ic:512 * (ic + 1)]).then_inc(S["gu_high"], 1)
            x_high(4, 1)
            act.wait_ge(S["top_gap"], 1)
            act.activation(tiny[:, 1, :], tiny[:, 0, :], ACT.Exp).then_inc(S["top_exp"], 1)

            def expert_unit(u, splits, downs):
                def silu(ic):
                    act.wait_ge(S["gu_mm"], u.count(8, 2 * ic + 1))
                    if u.after_zero(4, ic - 1):
                        act.wait_ge(S["prod"], u.count(4, ic - 1))
                    act.activation(silu_buf[:, ic % 2, :], R[2 * (ic % 2)][:, :], ACT.Silu).then_inc(S["silu"], 1)

                def high(ic):
                    act.wait_ge(S["prod"], u.count(4, ic + 1))
                    copy(hx_h[:, u.half(), ic, :], prod_buf[:, ic, :]).then_inc(S["act_high"], 1)
                    if splits:
                        act.wait_ge(S["gu_mm"], u.count(8, 2 * ic + 2))
                        if ic == 0:
                            act.wait_ge(ld["gu"], u.i * 16 + 32)
                        copy(w_r[:, 512 * ic:512 * (ic + 1)], gu_raw[:, 512 * ic:512 * (ic + 1)]).then_inc(S["gu_high"], 1)

                for ic in range(IC):
                    silu(ic)
                    if ic >= 1:
                        high(ic - 1)
                high(IC - 1)

            def down_high(e):
                act.wait_ge(ld["dn"], e * 16 + 16)
                if not isinstance(e, int) or e > 0:
                    act.wait_ge(S["y_mm"], e * 8)
                copy(w_r[:, 4096:5120], dn_raw).then_inc(S["dn_high"], 1)

            expert_unit(Unit(0, 0), False, False)
            down_high(0)
            expert_unit(Unit(0, 1), True, False)
            with act.Fori(1, NE - 1) as e:
                expert_unit(Unit(e, 0), False, False)
                down_high(e)
                expert_unit(Unit(e, 1), True, False)
            expert_unit(Unit(NE - 1, 0), False, False)
            down_high(NE - 1)
            expert_unit(Unit(NE - 1, 1), False, False)

        @block.vector
        def _(dve):
            link = Chain(dve, S["dve_step"])

            def norm(k, src, dst, rms=False, before_stats=None):
                for hf in range(2):
                    if before_stats:
                        before_stats(hf)
                    for t in range(4 * hf, 4 * hf + 4):
                        ins = dve.bn_stats(bn6[:, t, :], src[:, t, :])
                    link(ins)
                    for t in range(4 * hf, 4 * hf + 4):
                        ins = dve.bn_aggr(mean_var[:, t, :], bn6[:, t, :])
                    if rms:
                        link(ins)
                        m, v = mean_var[:, 4 * hf:4 * hf + 4, 0], mean_var[:, 4 * hf:4 * hf + 4, 1]
                        link(dve.tensor_tensor(m, m, m, ALU.mult))
                        ins = dve.tensor_tensor(v, v, m, ALU.add)
                    ins.then_inc(S["stats"], 1)
                for hf in range(2):
                    dve.wait_ge(S["rstd"], 2 * k + hf + 1)
                    for t in range(4 * hf, 4 * hf + 4):
                        if rms:
                            ins = dve.tensor_scalar(dst[:, t, :], src[:, t, :], rstd[:, t:t + 1], None, ALU.mult)
                        else:
                            ins = dve.tensor_scalar(dst[:, t, :], src[:, t, :], mean_var[:, t, 0:1], rstd[:, t:t + 1],
                                                    ALU.subtract, ALU.mult)
                        ins.then_inc(S["normed"], 1)

            def x_low(turn, w=None):
                for hf in range(2):
                    for k in range(KC):
                        dve.wait_ge(S["xT_high"], 4 * turn + 2 * hf + k + 1)
                        bank = R[2 * hf + k][:, :]
                        if w is None:
                            ins = dve.tensor_tensor(xT_half(xT_l, k, hf), bank, f(xT_half(xT_h, k, hf)), ALU.subtract)
                        else:
                            ins = dve.scalar_tensor_tensor(out=xT_half(xT_l, k, hf), in0=bank, scalar=w_ln[:, w, k:k + 1],
                                                           in1=f(xT_half(xT_h, k, hf)), op0=ALU.mult, op1=ALU.subtract)
                        ins.then_inc(S["xT_low"], 1)

            def add_gated(L, g):
                def go(hf):
                    if hf == 0:
                        dve.wait_ge(L["o_mm"], UNITS)
                    for t in range(4 * hf, 4 * hf + 4):
                        ins = dve.scalar_tensor_tensor(out=x_res[:, t, :], in0=y_tile(t), scalar=tgates[:, g:g + 1],
                                                       in1=x_res[:, t, :], op0=ALU.mult, op1=ALU.add)
                    link(ins)
                return go

            norm(0, x_res, nb, before_stats=lambda hf: dve.wait_ge(ld[f"x{hf}"], 16))
            dve.wait_ge(ld["small"], SMALL)
            dve.tensor_tensor(gqk[:, :], gq_gk[:, 0:1], gq_gk[:, 1:2], ALU.mult).then_inc(S["gqk"], 1)
            dve.tensor_reduce(mask_any[:, :], mask_u8[:, :].rearrange("p (b k) -> p b k", b=NB), AX.X,
                              ALU.max).then_inc(S["mask_any"], 1)
            dve.tensor_scalar(mask_add[:, :, :].rearrange("p b k -> p (b k)"), mask_u8[:, :], 1.0, BIG, ALU.subtract,
                              ALU.mult).then_inc(S["mask_add"], 1)
            dve.wait_ge(S["ctx_high"], 1)
            dve.tensor_tensor(ctxT_l, ctxT[:, :], f(ctxT_h), ALU.subtract).then_inc(S["ctx_low"], 1)
            x_low(0)
            dve.wait_ge(S["zeroed"], 1)

            def sub_max(L, u1, src):
                c = u1.half()
                dve.tensor_reduce(smax[:, c, :], src, AX.X, ALU.max).then_inc(L["smax"], 1)
                dve.wait_ge(L["smax"], u1.count(1, 1))
                dve.tensor_tensor(probs[:, 8 * c:8 * c + 8, :], src,
                                  smax[:, c, :].unsqueeze(2).broadcast_to([P, 8, SQ]), ALU.subtract).then_inc(L["sub"], 1)

            def sum_exp(L, u1):
                c = u1.half()
                dve.wait_ge(L["exp"], u1.count(1, 1))
                dve.tensor_reduce(ssum[:, c, :], probs[:, 8 * c:8 * c + 8, :], AX.X, ALU.add).then_inc(L["ssum"], 1)
                dve.wait_ge(L["ssum"], u1.count(1, 1))

            def probs_T(L, n, bank):
                dve.wait_ge(L["pt_mm"], n.count(1, 1))
                dve.tensor_copy(probsT[64:128, :, 1, :],
                                bank[64:128, :].rearrange("p (j n) -> p j n", j=4)).then_inc(L["pt_v"], 1)

            def attended(L, n, part, bank):
                dve.wait_ge(L["ac_high"], n.count(2, part + 1))
                t = 4 * n.half() + 2 * part
                dve.tensor_tensor(ac_l[:, :, t:t + 2, :].rearrange("p h t n -> p t h n"),
                                  bank[:, :].rearrange("p (t h n) -> p t h n", t=2, h=2),
                                  f(ac_h[:, :, t:t + 2, :]).rearrange("p h t n -> p t h n"),
                                  ALU.subtract).then_inc(L["ac_low"], 1)

            def wk_low(j):
                dve.wait_ge(L0["w_high"], j + 1)
                dve.tensor_tensor(wk_l, wk_raw[:, bass.ds(j * 256, 256)], f(wk_h), ALU.subtract).then_inc(L0["wk_low"], 1)

            def step0(n):
                u1, u2, u3 = n.at(1), n.at(2), n.at(3)

                def sum_squares(u, j):
                    dve.wait_ge(L0["squares"], u.count(4, j + 1))
                    dve.tensor_reduce(sumsq[:, j, :], squares[:, j % 2, :, :], AX.X, ALU.add).then_inc(L0["sumsq"], 1)

                def scale(u, j):
                    dve.wait_ge(L0["rnorm"], u.count(2, j // 2 + 1))
                    dve.tensor_tensor(raw[:, j, :, :], raw[:, j, :, :],
                                      rnorm[:, j, :].unsqueeze(2).broadcast_to([P, 4, HD]),
                                      ALU.mult).then_inc(L0["scaled"], 1)

                if u1.there():
                    dve.wait_ge(L0["scores"], u1.count(1, 1))
                    sub_max(L0, u1, R[0][:, :].rearrange("p (b k) -> p b k", b=8))
                if n.c == 1 and pair_there(n.i):
                    dve.wait_ge(L0["vo_high"], n.i + 1)
                    dve.tensor_tensor(vo_l.rearrange("p h n -> p (h n)"), vo0[:, bass.ds(n.i * 512, 512)],
                                      f(vo_h.rearrange("p h n -> p (h n)")), ALU.subtract).then_inc(L0["vo_low"], 1)
                if u2.there():
                    scale(u2, 2)
                    scale(u2, 3)
                if n.there():
                    probs_T(L0, n, R[3])
                if u1.there():
                    sum_exp(L0, u1)
                    dve.reciprocal(srec[:, u1.half(), :], ssum[:, u1.half(), :]).then_inc(L0["srec"], 1)
                if u3.there():
                    sum_squares(u3, 0)
                if n.there():
                    attended(L0, n, 0, R[2])
                if u3.there():
                    sum_squares(u3, 1)
                if n.there():
                    attended(L0, n, 1, R[1])
                if u3.there():
                    scale(u3, 0)
                    scale(u3, 1)
                    sum_squares(u3, 2)
                    sum_squares(u3, 3)
                if n.c == 0 and pair_there(n.i + 2):
                    wk_low(n.i + 2)

            wk_low(0)
            pipeline(dve, step0, 3)

            dve.wait_ge(S["gates"], 1)
            norm(1, x_res, nb, before_stats=add_gated(L0, 0))
            dve.wait_ge(S["wf_high"], 1)
            dve.tensor_tensor(w_r[:, 5120:5632], wf_raw, f(w_r[:, 4608:5120]), ALU.subtract).then_inc(S["wf_low"], 1)
            x_low(1)
            sq_scratch = kT[:, 0:DM]
            for t in range(NT):
                dve.wait_ge(S["ffn_mm"], t // 2 * 2 + 2)
                link(dve.tensor_tensor(ffn_out[:, t, :], y_tile(t), ffn_scale[:, :], ALU.mult))
                dve.tensor_tensor_reduce(out=sq_scratch, in0=ffn_out[:, t, :], in1=ffn_out[:, t, :], scale=1.0, scalar=0.0,
                                         op0=ALU.mult, op1=ALU.add, accum_out=tiny[:, 0, t:t + 1]
                                         ).then_inc(S["ffn_sumsq"], 1)
                dve.wait_ge(S["ffn_sumsq"], t + 1)
            dve.wait_ge(S["ffn_len0"], 1)
            dve.tensor_scalar(tiny[:, 1, :], tiny[:, 3, :], 1e-7, None, ALU.max).then_inc(S["ffn_len"], 1)
            dve.wait_ge(S["ffn_tanh"], 1)
            link(dve.tensor_scalar(tiny[:, 4, :], tiny[:, 1, :], 1e-7, None, ALU.add))
            link(dve.reciprocal(tiny[:, 5, :], tiny[:, 4, :]))
            link(dve.tensor_tensor(tiny[:, 6, :], tiny[:, 2, :], tiny[:, 5, :], ALU.mult))
            link(dve.tensor_tensor(tiny[:, 7, :], tiny[:, 6, :], tiny[:, 3, :], ALU.mult))
            link(dve.tensor_scalar(tiny[:, 7, :], tiny[:, 7, :], 1e-7, None, ALU.max))
            link(dve.reciprocal(tiny[:, 8, :], tiny[:, 7, :]))
            link(dve.tensor_scalar(tiny[:, 8, :], tiny[:, 8, :], 0.99, 1.0, ALU.mult, ALU.min))
            link(dve.tensor_tensor(tiny[:, 9, :], tiny[:, 6, :], tiny[:, 8, :], ALU.mult))
            link(dve.tensor_scalar(tiny[:, 10, :], tiny[:, 9, :], tgates[:, 2:3], None, ALU.mult))

            def add_ffn(hf):
                for t in range(4 * hf, 4 * hf + 4):
                    ins = dve.scalar_tensor_tensor(out=x_res[:, t, :], in0=ffn_out[:, t, :], scalar=tiny[:, 10, t:t + 1],
                                                   in1=x_res[:, t, :], op0=ALU.mult, op1=ALU.add)
                link(ins)

            norm(2, x_res, nb, before_stats=add_ffn)
            x_low(2)

            def step1(n):
                u1, u2 = n.at(1), n.at(2)
                B = [R[(2 * n.half() + k) % 4] for k in range(4)]
                if u1.there():
                    c = u1.half()
                    p = probs[:, 8 * c:8 * c + 8, :]
                    dve.wait_ge(L1["scores"], u1.count(1, 1))
                    dve.tensor_tensor(p, B[0][:, :].rearrange("p (b k) -> p b k", b=8), mask_add[:, 8 * c:8 * c + 8, :],
                                      ALU.add).then_inc(L1["masked"], 1)
                    dve.wait_ge(L1["masked"], u1.count(1, 1))
                    sub_max(L1, u1, p)
                if n.there():
                    probs_T(L1, n, B[2])
                if u1.there():
                    sum_exp(L1, u1)
                    dve.reciprocal(srec[:, c, :], ssum[:, c, :]).then_inc(L1["srec0"], 1)
                    dve.wait_ge(L1["srec0"], u1.count(1, 1))
                    dve.tensor_tensor(srec[:, c, :], srec[:, c, :], mask_any[:, 8 * c:8 * c + 8],
                                      ALU.mult).then_inc(L1["srec"], 1)
                if n.there():
                    attended(L1, n, 0, B[0])
                    attended(L1, n, 1, B[1])

            pipeline(dve, step1, 2)

            norm(3, x_res, x1, before_stats=add_gated(L1, 1))
            dve.wait_ge(S["normed"], 32)
            norm(4, x1, nb, rms=True)
            dve.wait_ge(S["aw_high"], 1)
            dve.tensor_tensor(w_r[:, 2048:4096], attn_raw, f(w_r[:, 0:2048]), ALU.subtract).then_inc(S["aw_low"], 1)
            x_low(3, 0)
            for use in range(4):
                dve.wait_ge(S["qk2_mm"], use + 5)
                dve.tensor_copy(kT2[:, use // 2, HALF * (use % 2):HALF * (use % 2 + 1)], R[use][:, :]).then_inc(S["k2"], 1)
            dve.wait_ge(S["zeroed"], 3)
            dve.wait_ge(S["v2"], 4)
            v_all = v_sb[:, :, :].rearrange("p t (g r d) -> p t g r d", g=8, r=2)
            dve.tensor_copy(vexp_v[0:64, 0:NB:2, :, 0, :], v_all[0:64, :, :, 0, :])
            dve.tensor_copy(vexp_v[64:128, 1:NB:2, :, 1, :], v_all[64:128, :, :, 1, :])
            for g in range(4):
                dve.wait_ge(S["vs_mm"], g + 1)
                dve.tensor_copy(vexp_v[64:128, 4 * g:4 * g + 3:2, :, 1, :],
                                v_parts(R[g])[64:128, :, :, 1, :]).then_inc(S["vs_v"], 1)

            def key_blocks(t):
                if t >= 2:
                    dve.wait_ge(S["s2_mm"], t - 1)
                for oc in range(KC):
                    c = SQ * 2 * t
                    ins = dve.tensor_tensor(kexp[:, t % 2, 0, oc, :].rearrange("p (h k) -> p h k", h=8),
                                            kT2[:, oc, c:c + SQ].unsqueeze(1).broadcast_to([P, 8, SQ]),
                                            head_mask[:, :].unsqueeze(2).broadcast_to([P, 8, SQ]), ALU.mult)
                ins.then_inc(S["kexp_v"], 1)

            def self_softmax(t):
                p = probs2[:, t % 2, :].rearrange("p (h k) -> p h k", k=SQ)
                dve.wait_ge(S["s2_mm"], t + 1)
                if t >= 2:
                    dve.wait_ge(S["pt2_mm"], t - 1)
                for oc in range(KC):
                    ins = dve.tensor_tensor(p[:, 8 * oc:8 * oc + 8, :],
                                            Y[2 * (t % 2) + oc][:, :].rearrange("p (h k) -> p h k", k=SQ),
                                            causal[:, :].unsqueeze(1).broadcast_to([P, 8, SQ]), ALU.add)
                ins.then_inc(S["s2_free"], 1)
                dve.wait_ge(S["s2_free"], t + 1)
                link(dve.tensor_reduce(row_max[:, t % 2, :], p, AX.X, ALU.max))
                dve.tensor_tensor(p, p, row_max[:, t % 2, :].unsqueeze(2).broadcast_to([P, AH, SQ]),
                                  ALU.subtract).then_inc(S["s2_sub"], 1)

            def self_sum(t):
                p = probs2[:, t % 2, :].rearrange("p (h k) -> p h k", k=SQ)
                dve.wait_ge(S["s2_exp"], t + 1)
                link(dve.tensor_reduce(row_sum[:, t % 2, :], p, AX.X, ALU.add))
                dve.reciprocal(row_rec[:, t % 2, :], row_sum[:, t % 2, :]).then_inc(S["s2_rec"], 1)

            dve.wait_ge(S["k2"], 4)
            key_blocks(0)
            key_blocks(1)
            self_softmax(0)
            self_sum(0)
            for t in range(NT + 1):
                if t + 1 < NT:
                    self_softmax(t + 1)
                if t >= 1:
                    dve.wait_ge(S["hT_high"], t)
                    dve.tensor_tensor(hT_l[:, t - 1, :, :].rearrange("p k n -> p (k n)"), R[3][:, 0:DM],
                                      f(hT_h[:, t - 1, :, :].rearrange("p k n -> p (k n)")),
                                      ALU.subtract).then_inc(S["hT_low"], 1)
                if t < NT:
                    dve.wait_ge(S["pt2_mm"], t + 1)
                    dve.tensor_copy(pt2[t % 2][:, 512:1024], R[1][:, :]).then_inc(S["pt2_v"], 1)
                if t + 1 < NT:
                    self_sum(t + 1)
                if t + 2 < NT:
                    key_blocks(t + 2)
                if t >= 1:
                    dve.wait_ge(S["wo2_mm"], t)
                    dve.tensor_tensor(x1[:, t - 1, :], R[3][:, DM:2 * DM], x1[:, t - 1, :],
                                      ALU.add).then_inc(S["x2"], 1)

            dve.wait_ge(S["x2"], NT)
            norm(5, x1, nb, rms=True)
            dve.wait_ge(S["wr_high"], 1)
            dve.tensor_tensor(wr_l, wr_raw[:, :, :], f(wr_h), ALU.subtract).then_inc(S["wr_low"], 1)
            x_low(4, 1)
            dve.wait_ge(S["route_mm"], 1)
            link(dve.tensor_copy(logits[:, :, :].rearrange("p t e -> p (t e)"), Y[3][:, 0:NT * NE]))
            for t in range(NT):
                ins = dve.max(top8[:, t, :], logits[:, t, :])
            link(ins)
            for t in range(NT):
                ins = dve.max_index(top8_at[:, t, :], top8[:, t, :], logits[:, t, :])
            link(ins)
            link(dve.tensor_copy(top_at[:, :, :], top8_at[:, :, 0:2]))
            dve.tensor_tensor(tiny[:, 0, :], top8[:, :, 1], top8[:, :, 0], ALU.subtract).then_inc(S["top_gap"], 1)
            dve.wait_ge(S["top_exp"], 1)
            link(dve.tensor_scalar(tiny[:, 2, :], tiny[:, 1, :], 1.0, None, ALU.add))
            link(dve.reciprocal(tiny[:, 3, :], tiny[:, 2, :]))
            link(dve.tensor_tensor(tiny[:, 4, :], tiny[:, 1, :], tiny[:, 3, :], ALU.mult))
            for j in range(2):
                link(dve.tensor_tensor(chosen[:, j, :, :], iota8[:, :].unsqueeze(2).broadcast_to([P, NE, NT]),
                                       top_at[:, :, j].unsqueeze(1).broadcast_to([P, NE, NT]), ALU.is_equal))
                link(dve.tensor_tensor(chosen[:, j, :, :], chosen[:, j, :, :],
                                       tiny[:, 3 + j, :].unsqueeze(1).broadcast_to([P, NE, NT]), ALU.mult))
            link(dve.tensor_tensor(cw[:, :].rearrange("p (e t) -> p e t", e=NE), chosen[:, 0, :, :], chosen[:, 1, :, :],
                                   ALU.add))

            def products(u):
                def product(ic):
                    dve.wait_ge(S["silu"], u.count(4, ic + 1))
                    dve.wait_ge(S["gu_mm"], u.count(8, 2 * ic + 2))
                    if u.after_zero(4, ic - 3):
                        dve.wait_ge(S["act_low"], u.count(4, ic - 3))
                    dve.tensor_tensor(prod_buf[:, ic, :], R[2 * (ic % 2) + 1][:, :], silu_buf[:, ic % 2, :],
                                      ALU.mult).then_inc(S["prod"], 1)

                def low(ic):
                    dve.wait_ge(S["act_high"], u.count(4, ic + 1))
                    dve.tensor_tensor(hx_l[:, u.half(), ic, :], prod_buf[:, ic, :], f(hx_h[:, u.half(), ic, :]),
                                      ALU.subtract).then_inc(S["act_low"], 1)

                for ic in range(IC):
                    product(ic)
                    if ic >= 1:
                        low(ic - 1)
                low(IC - 1)

            def add_expert(u):
                if u.half() == 0:
                    dve.tensor_copy(cw_now[:, :], cw[:, bass.ds(u.i * NT, NT)]).then_inc(S["cw_now"], 1)
                    dve.wait_ge(S["cw_now"], u.i + 1)
                for j in range(4):
                    t = 4 * u.half() + j
                    dve.wait_ge(S["y_mm"], u.count(4, j // 2 * 2 + 2))
                    dve.scalar_tensor_tensor(out=x1[:, t, :], in0=y_tile(t), scalar=cw_now[:, t:t + 1],
                                             in1=x1[:, t, :], op0=ALU.mult, op1=ALU.add).then_inc(S["y_added"], 1)

            products(Unit(0, 0))
            with dve.Fori(0, NE - 1) as e:
                for c in range(2):
                    products(Unit(e, c + 1))
                    add_expert(Unit(e, c))
            products(Unit(NE - 1, 1))
            add_expert(Unit(NE - 1, 0))
            add_expert(Unit(NE - 1, 1))
            dve.wait_ge(S["y_added"], 4 * UNITS)
            for hf in range(2):
                for t in range(4 * hf, 4 * hf + 4):
                    ins = dve.scalar_tensor_tensor(out=nb[:, t, :], in0=x1[:, t, :], scalar=tgates[:, 3:4],
                                                   in1=x_res[:, t, :], op0=ALU.mult, op1=ALU.add)
                ins.then_inc(S["out_ready"], 1)

        @block.gpsimd
        def _(pool):
            def rstd_of(k):
                for hf in range(2):
                    s = slice(4 * hf, 4 * hf + 4)
                    pool.wait_ge(S["stats"], 2 * k + hf + 1)
                    pool.tensor_scalar(var_eps[:, s], mean_var[:, s, 1], 1e-5, None, ALU.add).then_inc(S["var_eps"], 1)
                    pool.wait_ge(S["var_eps"], 2 * k + hf + 1)
                    pool.tensor_tensor(rstd[:, s], var_eps[:, s], neg_half[:, 0:4], ALU.pow).then_inc(S["rstd"], 1)

            pool.memset(neg_half[:, :], -0.5)
            pool.memset(eps8[:, :], 1e-5)
            pool.memset(pos_half[:, :], 0.5).then_inc(S["halves"], 1)
            pool.wait_ge(S["halves"], 1)
            rstd_of(0)
            pool.memset(probsT[:, :, :, :], 0.0).then_inc(S["zeroed"], 1)

            def probabilities(L, u1):
                c = u1.half()
                pool.wait_ge(L["srec"], u1.count(1, 1))
                p = probs[:, 8 * c:8 * c + 8, :]
                pool.tensor_tensor(p, p, srec[:, c, :].unsqueeze(2).broadcast_to([P, 8, SQ]),
                                   ALU.mult).then_inc(L["prob"], 1)

            def vo_low(L, src, n):
                if n.c == 1 and pair_there(n.i):
                    pool.wait_ge(L["vo_high"], n.i + 1)
                    pool.tensor_tensor(vo_l.rearrange("p h n -> p (h n)"), src[:, bass.ds(n.i * 512, 512)],
                                       f(vo_h.rearrange("p h n -> p (h n)")), ALU.subtract).then_inc(L["vo_low"], 1)

            def w_low0(j):
                pool.wait_ge(L0["w_high"], j + 1)
                pool.tensor_tensor(w_r[:, 512:1024], wq_raw[:, bass.ds(j * 512, 512)], f(w_r[:, 0:512]),
                                   ALU.subtract).then_inc(L0["w_low"], 1)

            def step0(n):
                u1, u3 = n.at(1), n.at(3)
                def norms(j):
                    pool.wait_ge(L0["sumsq"], u3.count(4, j + 2))
                    pool.tensor_tensor(sumsq_eps[:, j:j + 2, :].rearrange("p j g -> p (j g)"),
                                       sumsq[:, j:j + 2, :].rearrange("p j g -> p (j g)"), eps8[:, :],
                                       ALU.add).then_inc(L0["sumsq_eps"], 1)
                    pool.wait_ge(L0["sumsq_eps"], u3.count(2, j // 2 + 1))
                    pool.tensor_tensor(rnorm[:, j:j + 2, :].rearrange("p j g -> p (j g)"),
                                       sumsq_eps[:, j:j + 2, :].rearrange("p j g -> p (j g)"), neg_half[:, 0:8],
                                       ALU.pow).then_inc(L0["rnorm"], 1)

                if u1.there():
                    probabilities(L0, u1)
                if u3.there():
                    norms(0)
                if n.c == 0 and pair_there(n.i + 2):
                    w_low0(n.i + 2)
                if u3.there():
                    norms(2)

            w_low0(0)
            pipeline(pool, step0, 3)
            rstd_of(1)
            pool.wait_ge(S["ffn_sumsq"], NT)
            pool.tensor_tensor(tiny[:, 3, :], tiny[:, 0, :], pos_half[:, :], ALU.pow).then_inc(S["ffn_len0"], 1)
            rstd_of(2)

            def w_low1(j):
                pool.wait_ge(L1["w_high"], j + 1)
                pool.tensor_tensor(w_r[:, 512:1024], m1[:, bass.ds(j * 512, 512)], f(w_r[:, 0:512]),
                                   ALU.subtract).then_inc(L1["w_low"], 1)

            def step1(n):
                u1 = n.at(1)
                vo_low(L1, vo1, n)
                if u1.there():
                    probabilities(L1, u1)
                if n.c == 1 and pair_there(n.i + 2):
                    w_low1(n.i + 2)

            w_low1(0)
            pipeline(pool, step1, 2)
            pool.memset(reg_d[:, 0:2048], 0.0).then_inc(S["zeroed"], 1)
            pool.memset(reg_d[:, 2048:4096], 0.0).then_inc(S["zeroed"], 1)
            rstd_of(3)
            rstd_of(4)

            def key_blocks(t):
                if t == 0:
                    pool.wait_ge(S["k2"], 4)
                if t >= 2:
                    pool.wait_ge(S["s2_mm"], t - 1)
                for oc in range(KC):
                    c = SQ * (2 * t + 1)
                    ins = pool.tensor_tensor(kexp[:, t % 2, 1, oc, :].rearrange("p (h k) -> p h k", h=8),
                                             kT2[:, oc, c:c + SQ].unsqueeze(1).broadcast_to([P, 8, SQ]),
                                             head_mask[:, :].unsqueeze(2).broadcast_to([P, 8, SQ]), ALU.mult)
                ins.then_inc(S["kexp_p"], 1)

            key_blocks(0)
            key_blocks(1)
            for t in range(NT):
                pool.wait_ge(S["s2_rec"], t + 1)
                p = probs2[:, t % 2, :].rearrange("p (h k) -> p h k", k=SQ)
                pool.tensor_tensor(p, p, row_rec[:, t % 2, :].unsqueeze(2).broadcast_to([P, AH, SQ]),
                                   ALU.mult).then_inc(S["s2_prob"], 1)
                if t + 2 < NT:
                    key_blocks(t + 2)
            rstd_of(5)

            def gate_up_low(j, ic):
                pool.wait_ge(S["gu_high"], j * IC + (ic + 1))
                s = slice(512 * ic, 512 * (ic + 1))
                pool.tensor_tensor(w_r[:, 2048 + 512 * ic:2048 + 512 * (ic + 1)], gu_raw[:, s], f(w_r[:, s]),
                                   ALU.subtract).then_inc(S["gu_low"], 1)

            def down_low(e):
                pool.wait_ge(S["dn_high"], e + 1)
                pool.tensor_tensor(w_r[:, 5120:6144], dn_raw, f(w_r[:, 4096:5120]), ALU.subtract).then_inc(S["dn_low"], 1)

            for ic in range(IC):
                gate_up_low(0, ic)
            with pool.Fori(0, NE - 1) as e:
                down_low(e)
                for ic in range(IC):
                    gate_up_low(e + 1, ic)
            down_low(NE - 1)


def kernel(x, ctx_1024, mask_BxS2_bf1, g_xattn, g_ffn, L0_xattn_Wq, L0_xattn_Wk, L0_xattn_Wv, L0_xattn_Wo,
           L0_xattn_gq, L0_xattn_gk, L0_ffn_weight, L0_ffn_scale, L1_xattn_Wq, L1_xattn_Wk, L1_xattn_Wv, L1_xattn_Wo,
           L1_ffn_Wq, L1_ffn_Wk, L1_ffn_Wv, L1_ffn_Wo, L1_ffn_w_ln1, L1_ffn_w_ln2, L1_ffn_Wr, L1_ffn_Wg, L1_ffn_Wu,
           L1_ffn_Wd):
    import numpy as np
    import concourse.bacc as bacc
    from concourse import mybir as mb
    from concourse.bass_utils import run_bass_kernel_spmd

    def arr(v):
        return np.asarray(v)

    def rows(w, chunks):
        return arr(w).reshape(chunks, 128, -1).transpose(1, 0, 2)

    def inner_first(w, heads):
        return arr(w).reshape(arr(w).shape[0], heads, 128).transpose(2, 1, 0)

    x2 = arr(x).reshape(1024, 256)
    c2 = arr(ctx_1024).reshape(1024, 128)
    gu = np.stack([arr(L1_ffn_Wg), arr(L1_ffn_Wu)])
    gu = gu.reshape(2, 8, 4, 128, 2, 128).transpose(1, 5, 2, 0, 4, 3)
    dn = arr(L1_ffn_Wd).transpose(0, 2, 1).reshape(8, 4, 128, 256).transpose(0, 2, 1, 3)
    wattn = np.stack([arr(w).T.reshape(2, 128, 256) for w in (L1_ffn_Wq, L1_ffn_Wk, L1_ffn_Wv, L1_ffn_Wo)])
    key, q = np.arange(64)[None, :], np.arange(128)[:, None] % 64
    data = {
        "x": x2, "ctx": c2, "ctxT": c2.T, "mask": arr(mask_BxS2_bf1).reshape(-1).view(np.uint8),
        "gates": np.concatenate([arr(g_xattn), arr(g_ffn)]),
        "gqk": np.stack([arr(L0_xattn_gq), arr(L0_xattn_gk)], axis=1),
        "wq0": rows(L0_xattn_Wq, 2).reshape(128, 2, 8, 256).transpose(0, 2, 1, 3).reshape(128, 4096),
        "wk0": arr(L0_xattn_Wk), "wv0T": inner_first(L0_xattn_Wv, 16).reshape(128, 2048),
        "wo0": rows(L0_xattn_Wo, 16).reshape(128, 4096),
        "wf": rows(L0_ffn_weight, 2).reshape(128, 512), "ffn_scale": arr(L0_ffn_scale),
        "wq1T": inner_first(L1_xattn_Wq, 16).reshape(128, 4096), "wk1T": inner_first(L1_xattn_Wk, 8).reshape(128, 1024),
        "wv1T": inner_first(L1_xattn_Wv, 8).reshape(128, 1024), "wo1": rows(L1_xattn_Wo, 16).reshape(128, 4096),
        "wattn": wattn.transpose(2, 0, 1, 3).reshape(128, 2048),
        "w_ln": np.stack([arr(L1_ffn_w_ln1), arr(L1_ffn_w_ln2)]).reshape(2, 2, 128).transpose(2, 0, 1),
        "wr": arr(L1_ffn_Wr).T.reshape(2, 128, 8).transpose(1, 0, 2),
        "gu": gu.reshape(8, 128, 2048),
        "dn": dn.reshape(8, 128, 1024),
        "c_ident": np.eye(128, dtype=np.float32),
        "c_swap": np.roll(np.eye(128, dtype=np.float32), 64, axis=1),
        "c_causal": np.where(key <= q, 0.0, -1e30).astype(np.float32),
        "c_heads": (np.arange(128)[:, None] // 16 == np.arange(8)[None, :]).astype(np.float32),
        "c_iota": np.tile(np.arange(8, dtype=np.float32), (128, 1)),
    }
    nc = bacc.Bacc("TRN2", target_bir_lowering=False, num_devices=1)
    arrays, aps = {}, {}
    for name, v in data.items():
        v = np.ascontiguousarray(v)
        arrays["in_" + name] = v
        aps[name] = nc.dram_tensor("in_" + name, v.shape, mb.dt.from_np(v.dtype), kind="ExternalInput").ap()
    aps["out"] = nc.dram_tensor("out_x", (1024, 256), mb.dt.float32, kind="ExternalOutput").ap()
    build(nc, aps)
    r = run_bass_kernel_spmd(nc, [arrays], core_ids=[0])
    return r.results[0]["out_x"].reshape(16, 64, 256)
```

```python
from contextlib import ExitStack

import concourse.bass as bass
from concourse import mybir

F32 = mybir.dt.float32
F32R = mybir.dt.float32r
BF16 = mybir.dt.bfloat16
I32 = mybir.dt.int32
U32 = mybir.dt.uint32
U8 = mybir.dt.uint8
ALU = mybir.AluOpType
ACT = mybir.ActivationFunctionType
AX = mybir.AxisListType

P = 128
NB, SQ, DM = 16, 64, 256
CD, HD = 128, 128
NH, NKV = 16, 8
NT = NB * SQ // P
KC = DM // P
HALF = NB * SQ // 2
PAIRS = NH // 2
UNITS = 2 * PAIRS
NE, INTER = 8, 512
IC = INTER // P
AH, AD = 16, 16
BANK = 512
BIG = 1e30
EPS = 1e-5
SMALL = 9 * 16


def build(nc, a):
    with ExitStack() as ctx:
        def sb(name, shape, dt=F32):
            return ctx.enter_context(nc.sbuf_tensor(name, shape, dt))

        def sem(name):
            return ctx.enter_context(nc.semaphore(name))

        x_res = sb("x_res", [P, NT, DM])
        ctxT = sb("ctxT", [P, NB * SQ])
        ctx_tok = sb("ctx_tok", [P, NT, CD])
        reg_a = sb("reg_a", [P, 4096])
        reg_b = sb("reg_b", [P, 2048])
        reg_c = sb("reg_c", [P, 6144])
        reg_d = sb("reg_d", [P, 4096])
        reg_e = sb("reg_e", [P, 4096])
        norm_buf = sb("norm_buf", [P, NT, DM])
        qT = sb("qT", [P, 2048])
        kT = sb("kT", [P, 2048])
        probs = sb("probs", [P, NB, SQ])
        probsT = sb("probsT", [P, 4, 2, P])
        ident = sb("ident", [P, P])
        swap = sb("swap", [P, P])
        causal = sb("causal", [P, SQ], BF16)
        ident_b = sb("ident_b", [P, P], BF16)
        head_mask = sb("head_mask", [P, 8])
        mask_add = sb("mask_add", [P, NB, SQ], BF16)
        mask_any = sb("mask_any", [P, NB])
        gates = sb("gates", [P, 4])
        tgates = sb("tgates", [P, 4])
        gq_gk = sb("gq_gk", [P, 2])
        gqk = sb("gqk", [P, 1])
        ffn_scale = sb("ffn_scale", [P, DM])
        w_ln = sb("w_ln", [P, 2, KC])
        bn6 = sb("bn6", [P, NT, 6])
        mean_var = sb("mean_var", [P, NT, 2])
        var_eps = sb("var_eps", [P, NT])
        rstd = sb("rstd", [P, NT])
        rms_var, rms_rstd = sb("rms_var", [P, NT]), sb("rms_rstd", [P, NT])
        neg_half = sb("neg_half", [P, 8])
        eps8 = sb("eps8", [P, 8])
        pos_half = sb("pos_half", [P, 8])
        sumsq = sb("sumsq", [P, 4, 4])
        sumsq_eps = sb("sumsq_eps", [P, 4, 4])
        rnorm = sb("rnorm", [P, 4, 4])
        smax = sb("smax", [P, 2, 8])
        ssum = sb("ssum", [P, 2, 8])
        srec = sb("srec", [P, 2, 8])
        row_max, row_sum, row_rec = (sb(n, [P, 2, AH]) for n in ("row_max", "row_sum", "row_rec"))
        iota8 = sb("iota8", [P, NE])
        logits = sb("logits", [P, NT, NE])
        top8 = sb("top8", [P, NT, 8])
        top8_at = sb("top8_at", [P, NT, 8], U32)
        top_at = sb("top_at", [P, NT, 2])
        chosen = ffn_scale[:, 0:2 * NE * NT].rearrange("p (j e t) -> p j e t", j=2, e=NE)
        cw = sb("cw", [P, NE * NT])
        cw_now = sb("cw_now", [P, NT])
        wr_raw = sb("wr_raw", [P, KC, NE])
        tiny = sb("tiny", [P, 12, NT])

        xT_h = sb("xT_h", [P, KC, NB * SQ], F32R)
        xT_l = sb("xT_l", [P, KC, NB * SQ], F32R)
        w_r = sb("w_r", [P, 6144], F32R)
        wr_r = sb("wr_r", [P, 2, KC, NE], F32R)
        wr_h, wr_l = wr_r[:, 0, :, :], wr_r[:, 1, :, :]
        act_r = sb("act_r", [P, 8192], F32R)

        wq_raw = reg_a[:, :]
        wk_raw = reg_b[:, :]
        wf_raw = reg_b[:, 0:512]
        wo_raw = reg_c[:, 0:4096]
        wv_raw = reg_c[:, 4096:6144]
        wk1T = reg_c[:, 4096:5120]
        wv1T = reg_c[:, 5120:6144]
        vo0, m1, vo1 = reg_d, reg_d, reg_e
        nb_flat = norm_buf[:, :, :].rearrange("p t d -> p (t d)")
        squares = reg_e[:, 1024:2048].rearrange("p (s g d) -> p s g d", s=2, g=4)
        raw = nb_flat.rearrange("p (s g d) -> p s g d", s=4, g=4)
        qT_v = qT[:, :].rearrange("p (t b h q) -> p t b h q", t=NT, b=2, h=2)
        kT_v = kT[:, :].rearrange("p (t b h q) -> p t b h q", t=NT, b=2, h=2)
        wq_h, wq_l = w_r[:, 0:512].rearrange("p (k n) -> p k n", k=KC), w_r[:, 512:1024].rearrange("p (k n) -> p k n", k=KC)
        wk_h, wk_l = w_r[:, 1024:1280], w_r[:, 1280:1536]
        vo_h, vo_l = w_r[:, 1536:2048].rearrange("p (h n) -> p h n", h=2), w_r[:, 2048:2560].rearrange("p (h n) -> p h n", h=2)
        ctxT_h, ctxT_l = w_r[:, 2560:3584], w_r[:, 3584:4608]
        wf_h, wf_l = w_r[:, 4608:5120].rearrange("p (k n) -> p k n", k=KC), w_r[:, 5120:5632].rearrange("p (k n) -> p k n", k=KC)
        ac_h = act_r[:, 0:2048].rearrange("p (h t n) -> p h t n", h=2, t=NT)
        ac_l = act_r[:, 2048:4096].rearrange("p (h t n) -> p h t n", h=2, t=NT)

        mask_u8 = reg_e[:, 0:256].bitcast(U8)
        x1 = reg_a[:, 0:2048].rearrange("p (t d) -> p t d", t=NT)
        attn_raw = reg_a[:, 2048:4096]
        gu_raw, dn_raw = reg_c[:, 0:2048], reg_c[:, 2048:3072]
        silu_buf = qT[:, 0:1024].rearrange("p (s n) -> p s n", s=2)
        prod_buf = reg_b[:, :].rearrange("p (s n) -> p s n", s=IC)
        nb = norm_buf
        qT2 = qT[:, :].rearrange("p (k n) -> p k n", k=KC)
        kT2 = kT[:, :].rearrange("p (k n) -> p k n", k=KC)
        kexp = reg_e[:, :].rearrange("p (s b k n) -> p s b k n", s=2, b=2, k=KC)
        vexp = reg_d[:, :].rearrange("p (b n) -> p b n", b=NB)
        vexp_v = reg_d[:, :].rearrange("p (b g r d) -> p b g r d", b=NB, g=8, r=2)
        v_sb = reg_c[:, 3072:5120].rearrange("p (t n) -> p t n", t=NT)
        probs2 = reg_b[:, :].rearrange("p (s n) -> p s n", s=2)
        pt2 = [probs[:, :, :].rearrange("p b k -> p (b k)"), probsT[:, :, :, :].rearrange("p j b n -> p (j b n)")]
        aw = act_r[:, 4096:8192].rearrange("p (w s n) -> p w s n", w=4, s=2)
        aw_h = aw[:, :, 0, :].rearrange("p w (k n) -> p w k n", k=KC)
        aw_l = aw[:, :, 1, :].rearrange("p w (k n) -> p w k n", k=KC)
        hT_h = act_r[:, 0:2048].rearrange("p (t k n) -> p t k n", t=NT, k=KC)
        hT_l = act_r[:, 2048:4096].rearrange("p (t k n) -> p t k n", t=NT, k=KC)
        gu_h = w_r[:, 0:2048].rearrange("p (i m k n) -> p i m k n", i=IC, m=2, k=KC)
        gu_l = w_r[:, 2048:4096].rearrange("p (i m k n) -> p i m k n", i=IC, m=2, k=KC)
        dn_h = w_r[:, 4096:5120].rearrange("p (i n) -> p i n", i=IC)
        dn_l = w_r[:, 5120:6144].rearrange("p (i n) -> p i n", i=IC)
        hx_h = act_r[:, 0:4096].rearrange("p (s i n) -> p s i n", s=2, i=IC)
        hx_l = act_r[:, 4096:8192].rearrange("p (s i n) -> p s i n", s=2, i=IC)

        psum = [ctx.enter_context(nc.psum_tensor(f"bank{i}", [P, BANK], F32)) for i in range(8)]
        Y = psum[0:4]
        R = psum[4:8]

        def y_tile(t):
            return Y[t // 2][:, DM * (t % 2):DM * (t % 2 + 1)]

        def f(ap):
            return ap.bitcast(F32)

        ld = {n: sem("ld_" + n) for n in (
            "x0", "x1", "ident", "ctx", "ctx_tok", "gqk", "small", "wq0", "wk0", "wv0", "wo0", "wq0_rest", "wk0_rest", "wf",
            "wq1", "wk1", "wv1", "wo1", "attn", "wr", "gu", "dn")}
        stored = sem("stored")
        S = {n: sem(n) for n in (
            "stats", "var_eps", "rstd", "normed", "rms_var", "rms_rstd",
            "xT_mm", "xT_high", "xT_low",
            "halves", "zeroed", "gates", "gqk", "mask_add", "mask_any", "ctx_high", "ctx_low",
            "vo0_mm", "vo0", "m1_mm", "m1", "vo1_mm", "vo1",
            "wf_high", "wf_low", "wf_scaled", "ffn_mm", "ffn_sumsq", "ffn_len0", "ffn_len", "ffn_tanh",
            "aw_high", "aw_low", "qk2_mm", "q2", "k2", "v2_mm", "v2", "vs_mm", "vs_a", "vs_v",
            "kexp_v", "kexp_p", "s2_mm", "s2_row_max", "s2_sub", "s2_exp", "s2_rec", "s2_prob", "pt2_mm", "pt2",
            "av2_mm", "h2", "hT_mm", "hT_high", "hT_low", "wo2_mm", "x2",
            "wr_high", "wr_low", "route_mm", "top_gap", "top_exp",
            "gu_high", "gu_low", "dn_high", "dn_low", "gu_mm", "silu", "prod", "act_high", "act_low", "y_mm", "y_added",
            "cw_now", "out_ready", "dve_step", "pool_step")}
        LAYER = ("wk_low", "proj", "squares", "sumsq", "sumsq_eps", "rnorm", "scaled", "qk_mm", "qk",
                 "scores", "masked", "smax", "sub", "exp", "ssum", "srec0", "srec", "prob",
                 "pt_mm", "pt_a", "pt_v", "av_mm", "ac_high", "ac_low", "o_mm", "w_high", "w_low", "vo_high", "vo_low")
        L0 = {k: sem("a0_" + k) for k in LAYER}
        L1 = {k: sem("a1_" + k) for k in LAYER if k not in ("wk_low", "squares", "sumsq", "sumsq_eps", "rnorm", "scaled", "qk_mm")}

        class Chain:
            def __init__(self, eng, s):
                self.eng, self.s, self.n = eng, s, 0

            def __call__(self, ins):
                ins.then_inc(self.s, 1)
                self.n += 1
                self.eng.wait_ge(self.s, self.n)

        def v_parts(bank):
            return bank[:, :].rearrange("p (t g r d) -> p t g r d", t=2, g=8, r=2)

        def xT_half(part, k, hf):
            return part[:, k, HALF * hf:HALF * (hf + 1)]

        block = ctx.enter_context(nc.Block())

        @block.sync
        def _(sp):
            def load(name, dst, src):
                sp.dma_start(dst, src).then_inc(ld[name], 16)

            xv = a["x"].rearrange("(t p) d -> p t d", p=P)
            load("x0", x_res[:, 0:4, :], xv[:, 0:4, :])
            load("x1", x_res[:, 4:8, :], xv[:, 4:8, :])
            load("ident", ident[:, :], a["c_ident"])
            load("wq0", wq_raw[:, 0:1024], a["wq0"][:, 0:1024])
            load("wk0", wk_raw[:, 0:512], a["wk0"][:, 0:512])
            load("wv0", wv_raw, a["wv0T"])
            load("wo0", wo_raw, a["wo0"])
            load("wq0_rest", wq_raw[:, 1024:4096], a["wq0"][:, 1024:4096])
            load("wk0_rest", wk_raw[:, 512:2048], a["wk0"][:, 512:2048])
            sp.wait_ge(S["vo0_mm"], 8)
            load("wo1", wo_raw, a["wo1"])
            load("wk1", wk1T, a["wk1T"])
            load("wv1", wv1T, a["wv1T"])
            sp.wait_ge(L0["w_low"], PAIRS)
            load("wq1", wq_raw, a["wq1T"])
            load("wf", wf_raw, a["wf"])
            sp.wait_ge(S["m1_mm"], 8)
            load("attn", attn_raw, a["wattn"])
            sp.wait_ge(S["vo1_mm"], 8)
            load("gu", gu_raw, a["gu"][0])
            load("dn", dn_raw, a["dn"][0])
            with sp.Fori(1, NE) as e:
                sp.wait_ge(S["gu_low"], e * IC)
                load("gu", gu_raw, a["gu"][bass.ds(e, 1)].rearrange("e p n -> (e p) n"))
                sp.wait_ge(S["dn_low"], e)
                load("dn", dn_raw, a["dn"][bass.ds(e, 1)].rearrange("e p n -> (e p) n"))
            ov = a["out"].rearrange("(t p) d -> p t d", p=P)
            for hf in range(2):
                sp.wait_ge(S["out_ready"], hf + 1)
                sp.dma_start(ov[:, 4 * hf:4 * hf + 4, :], norm_buf[:, 4 * hf:4 * hf + 4, :]).then_inc(stored, 16)
            sp.wait_ge(stored, 32)

        class Unit:
            def __init__(self, i, c):
                self.i, self.c = i, c

            def at(self, off):
                return Unit(self.i, self.c + off)

            def there(self):
                return not isinstance(self.i, int) or 0 <= 2 * self.i + self.c < UNITS

            def count(self, per, k):
                return self.i * (2 * per) + (self.c * per + k)

            def after_zero(self, per, k):
                return not isinstance(self.i, int) or self.count(per, k) > 0

            def half(self):
                return self.c % 2

            def first(self):
                return isinstance(self.i, int) and 2 * self.i + self.c in (0, 1)

        def step_is(n, k):
            return isinstance(n.i, int) and 2 * n.i + n.c == k

        def pair_there(j):
            return not isinstance(j, int) or 0 <= j < PAIRS

        def vo_turn(n, j):
            g = 3 * (2 * n.i + n.c + 2) + j if isinstance(n.i, int) else -1
            return g if j < 3 and 0 <= g < PAIRS else None

        def pipeline(eng, step, lead):
            if lead == 3:
                step(Unit(-2, 1))
            for i in (-1, 0, 1):
                for c in (0, 1):
                    step(Unit(i, c))
            with eng.Fori(2, PAIRS - 2) as i:
                for c in (0, 1):
                    step(Unit(i, c))
            for i in (PAIRS - 2, PAIRS - 1, PAIRS):
                for c in (0, 1):
                    step(Unit(i, c))

        @block.tensor
        def _(pe):
            def split_mm(out, lh, ll, rh, rl, start, stop):
                pe.matmul(out, lh, rh, start=start, stop=False, skip_group_check=True)
                pe.matmul(out, lh, rl, start=False, stop=False, skip_group_check=True)
                return pe.matmul(out, ll, rh, start=False, stop=stop, skip_group_check=True)

            def x_transposes(norm, halves=(0, 1), banks=R):
                for hf in halves:
                    for k in range(KC):
                        for t in range(4):
                            pe.wait_ge(S["normed"], 8 * norm + 4 * hf + t + 1)
                            ins = pe.transpose(banks[2 * hf + k][:, P * t:P * (t + 1)],
                                               nb[:, 4 * hf + t, P * k:P * (k + 1)], ident[:, :])
                        ins.then_inc(S["xT_mm"], 1)

            pe.wait_ge(ld["ident"], 16)
            x_transposes(0)

            def probs_T(L, n, bank):
                pe.wait_ge(L["prob"], n.count(1, 1))
                for j in range(4):
                    b = 8 * n.half() + 2 * j
                    ins = pe.transpose(bank[:, P * j:P * (j + 1)],
                                       probs[:, b:b + 2, :].rearrange("p b k -> p (b k)"), ident[:, :])
                ins.then_inc(L["pt_mm"], 1)

            def attend(L, n, part, bank):
                pe.wait_ge(L["pt_a"], n.count(1, 1))
                pe.wait_ge(L["pt_v"], n.count(1, 1))
                for jj in range(2):
                    j = 2 * part + jj
                    ins = pe.matmul(bank[:, 256 * jj:256 * (jj + 1)], ctx_tok[:, 4 * n.half() + j, :],
                                    probsT[:, j, :, :].rearrange("p b (h q) -> p h b q", h=2), start=True, stop=True)
                ins.then_inc(L["av_mm"], 1)

            def project_out(L, n, tiles):
                pe.wait_ge(L["ac_low"], n.count(2, 2))
                pe.wait_ge(L["vo_low"], n.i + (n.c // 2 + 1))
                for j in tiles:
                    t = 4 * n.half() + j
                    for hh in range(2):
                        ins = split_mm(y_tile(t), ac_h[:, hh, t, :], ac_l[:, hh, t, :], vo_h[:, hh, :], vo_l[:, hh, :],
                                       start=n.first() and t % 2 == 0 and hh == 0, stop=False)
                if tiles[-1] == 3:
                    ins.then_inc(L["o_mm"], 1)

            def project_qk(u, j, bank):
                t = 4 * u.half() + j
                if j == 0:
                    pe.wait_ge(L0["w_low"], u.i + (u.c // 2 + 1))
                    pe.wait_ge(L0["wk_low"], u.i + (u.c // 2 + 1))
                for k in range(KC):
                    split_mm(bank[:, 0:256], xT_h[:, k, P * t:P * (t + 1)], xT_l[:, k, P * t:P * (t + 1)],
                             wq_h[:, k, :], wq_l[:, k, :], k == 0, k == KC - 1)
                split_mm(bank[:, 256:512], ctxT_h[:, P * t:P * (t + 1)], ctxT_l[:, P * t:P * (t + 1)],
                         wk_h, wk_l, True, True).then_inc(L0["proj"], 1)

            def qk_T(u, j, bank):
                pe.wait_ge(L0["scaled"], u.count(4, j + 1))
                for g in range(4):
                    ins = pe.transpose(bank[:, P * g:P * (g + 1)], raw[:, j, g, :], ident[:, :])
                ins.then_inc(L0["qk_mm"], 1)

            def vo_product(n, j):
                g = vo_turn(n, j)
                if g is not None:
                    if g == 0:
                        pe.wait_ge(ld["wv0"], 16)
                        pe.wait_ge(ld["wo0"], 16)
                    if g >= 4:
                        pe.wait_ge(S["vo0"], g - 3)
                    for hh in range(2):
                        h = 2 * g + hh
                        ins = pe.matmul(Y[g % 4][:, DM * hh:DM * (hh + 1)], wv_raw[:, CD * h:CD * (h + 1)],
                                        wo_raw[:, DM * h:DM * (h + 1)], start=True, stop=True)
                    ins.then_inc(S["vo0_mm"], 1)

            def step0(n):
                u1, u2, u3, um, um2 = n.at(1), n.at(2), n.at(3), n.at(-1), n.at(-2)
                if u1.there():
                    pe.wait_ge(L0["qk"], u1.count(4, 4))
                    for j in range(4):
                        for b in range(2):
                            for hh in range(2):
                                t = 4 * u1.half() + j
                                ins = pe.matmul(R[0][64 * hh:64 * (hh + 1), 64 * (2 * j + b):64 * (2 * j + b + 1)],
                                                qT_v[:, t, b, hh, :], kT_v[:, t, b, hh, :], start=True, stop=True)
                    ins.then_inc(L0["scores"], 1)
                if u2.there():
                    if um.there():
                        pe.wait_ge(L0["ac_low"], um.count(2, 2))
                    qk_T(u2, 0, R[1])
                    pe.wait_ge(L0["squares"], u2.count(4, 3))
                    qk_T(u2, 1, R[2])
                    pe.wait_ge(L0["squares"], u2.count(4, 4))
                if n.there():
                    probs_T(L0, n, R[3])
                if um2.there():
                    project_out(L0, um2, (3,))
                if u3.there():
                    if u1.there():
                        pe.wait_ge(L0["sub"], u1.count(1, 1))
                    project_qk(u3, 0, R[0])
                    vo_product(n, 0)
                if n.there():
                    if u2.there():
                        pe.wait_ge(L0["qk"], u2.count(4, 2))
                    elif um.there():
                        pe.wait_ge(L0["ac_low"], um.count(2, 2))
                    attend(L0, n, 0, R[2])
                if u2.there():
                    pe.wait_ge(L0["qk"], u2.count(4, 1))
                    qk_T(u2, 2, R[1])
                if u3.there():
                    if n.there():
                        pe.wait_ge(L0["pt_v"], n.count(1, 1))
                    project_qk(u3, 1, R[3])
                    vo_product(n, 1)
                if u2.there():
                    if u3.there():
                        pe.wait_ge(L0["squares"], u3.count(4, 1))
                    else:
                        pe.wait_ge(L0["sub"], u1.count(1, 1))
                    qk_T(u2, 3, R[0])
                if um.there():
                    project_out(L0, um, (0,))
                if n.there():
                    if u2.there():
                        pe.wait_ge(L0["qk"], u2.count(4, 3))
                    attend(L0, n, 1, R[1])
                if um.there():
                    project_out(L0, um, (1,))
                if u3.there():
                    if n.there():
                        pe.wait_ge(L0["ac_low"], n.count(2, 1))
                    project_qk(u3, 2, R[2])
                    vo_product(n, 2)
                if um.there():
                    project_out(L0, um, (2,))
                if u3.there():
                    pe.wait_ge(L0["squares"], u3.count(4, 2))
                    project_qk(u3, 3, R[3])

            pe.wait_ge(S["xT_low"], 4)
            pe.wait_ge(S["ctx_low"], 1)
            pe.wait_ge(ld["ctx_tok"], 16)
            pipeline(pe, step0, 3)

            pe.wait_ge(ld["wq1"], 16)
            pe.wait_ge(ld["wk1"], 16)
            for g in range(PAIRS):
                if g >= 4:
                    pe.wait_ge(S["m1"], g - 3)
                for k in range(KC):
                    for hh in range(2):
                        o = P * (2 * k + hh)
                        w = DM * (2 * g + hh) + P * k
                        ins = pe.matmul(R[g % 4][:, o:o + P], wq_raw[:, w:w + P], wk1T[:, CD * g:CD * (g + 1)],
                                        start=True, stop=True)
                ins.then_inc(S["m1_mm"], 1)
            pe.wait_ge(S["m1"], PAIRS)
            x_transposes(1)
            pe.wait_ge(S["wf_low"], 1)
            for t in range(NT):
                if t % 4 == 0:
                    pe.wait_ge(S["xT_low"], 4 + 2 * (t // 4) + 2)
                for k in range(KC):
                    ins = split_mm(y_tile(t), xT_h[:, k, P * t:P * (t + 1)], xT_l[:, k, P * t:P * (t + 1)],
                                   wf_h[:, k, :], wf_l[:, k, :], k == 0, k == KC - 1)
                ins.then_inc(S["ffn_mm"], 1)
            pe.wait_ge(ld["wv1"], 16)
            pe.wait_ge(ld["wo1"], 16)
            for g in range(PAIRS):
                if g >= 4:
                    pe.wait_ge(S["vo1"], g - 3)
                for hh in range(2):
                    h = 2 * g + hh
                    ins = pe.matmul(R[g % 4][:, DM * hh:DM * (hh + 1)], wv1T[:, CD * g:CD * (g + 1)],
                                    wo_raw[:, DM * h:DM * (h + 1)], start=True, stop=True)
                ins.then_inc(S["vo1_mm"], 1)

            pe.wait_ge(S["vo1"], PAIRS)
            x_transposes(2)

            def project_t(u, hh, bank):
                if hh == 0:
                    pe.wait_ge(L1["w_low"], u.i + (u.c // 2 + 1))
                for k in range(KC):
                    ins = split_mm(bank[:, :], wq_h[:, k, P * hh:P * (hh + 1)], wq_l[:, k, P * hh:P * (hh + 1)],
                                   xT_half(xT_h, k, u.half()), xT_half(xT_l, k, u.half()), k == 0, k == KC - 1)
                ins.then_inc(L1["proj"], 1)

            def step1(n):
                u1, u2, um = n.at(1), n.at(2), n.at(-1)
                B = [R[(2 * n.half() + k) % 4] for k in range(4)]
                if u1.there():
                    pe.wait_ge(L1["qk"], u1.count(2, 2))
                    for j in range(4):
                        for b in range(2):
                            t = 4 * u1.half() + j
                            ins = pe.matmul(B[0][:, 64 * (2 * j + b):64 * (2 * j + b + 1)],
                                            qT_v[:, t, b, :, :].rearrange("p h q -> p (h q)"),
                                            ctxT[:, SQ * (2 * t + b):SQ * (2 * t + b + 1)], start=True, stop=True)
                    ins.then_inc(L1["scores"], 1)
                if u2.there():
                    project_t(u2, 0, B[1])
                if n.there():
                    if um.there():
                        pe.wait_ge(L1["ac_low"], um.count(2, 1))
                    probs_T(L1, n, B[2])
                if um.there():
                    project_out(L1, um, (0, 1))
                if u2.there():
                    project_t(u2, 1, B[3])
                if n.there():
                    if u1.there():
                        pe.wait_ge(L1["masked"], u1.count(1, 1))
                    attend(L1, n, 0, B[0])
                    if u2.there():
                        pe.wait_ge(L1["qk"], u2.count(2, 1))
                    attend(L1, n, 1, B[1])
                if um.there():
                    project_out(L1, um, (2, 3))

            pe.wait_ge(S["xT_low"], 12)
            pipeline(pe, step1, 2)

            x_transposes(3)
            pe.wait_ge(S["aw_low"], 1)
            for hf in range(2):
                pe.wait_ge(S["xT_low"], 12 + 2 * hf + 2)
                for w in range(2):
                    for oc in range(KC):
                        bank = (Y, R)[hf][2 * w + oc]
                        for k in range(KC):
                            ins = split_mm(bank[:, :], aw_h[:, w, k, P * oc:P * (oc + 1)],
                                           aw_l[:, w, k, P * oc:P * (oc + 1)],
                                           xT_half(xT_h, k, hf), xT_half(xT_l, k, hf), k == 0, k == KC - 1)
                        ins.then_inc(S["qk2_mm"], 1)

            def self_scores(t):
                pe.wait_ge(S["kexp_v"], t + 1)
                pe.wait_ge(S["kexp_p"], t + 1)
                pe.wait_ge(S["q2"], 2 * (t // 4) + 2)
                if t >= 2:
                    pe.wait_ge(S["s2_sub"], t - 1)
                for oc in range(KC):
                    bank = Y[2 * (t % 2) + oc]
                    pe.matmul(bank[:, :], ident_b[:, :], causal[:, :].unsqueeze(1).broadcast_to([P, 8, SQ]),
                              start=True, stop=False, skip_group_check=True)
                    for b in range(2):
                        c = SQ * (2 * t + b)
                        ins = pe.matmul(bank[64 * b:64 * (b + 1), :], qT2[:, oc, c:c + SQ],
                                        kexp[:, t % 2, b, oc, :], start=False, stop=True, skip_group_check=True)
                ins.then_inc(S["s2_mm"], 1)

            pe.wait_ge(ld["small"], SMALL)
            self_scores(0)
            for g in range(4):
                pe.wait_ge(*((S["q2"], 3 + g) if g < 2 else (S["k2"], 1 + g)))
                for tt in range(2):
                    c = P * (2 * g + tt)
                    for k in range(KC):
                        ins = split_mm(R[g][:, DM * tt:DM * (tt + 1)], xT_h[:, k, c:c + P], xT_l[:, k, c:c + P],
                                       aw_h[:, 2, k, :], aw_l[:, 2, k, :], k == 0, k == KC - 1)
                ins.then_inc(S["v2_mm"], 1)
            for g in range(4):
                pe.wait_ge(S["v2"], g + 1)
                pe.matmul(R[g][:, :], swap[:, :], v_sb[:, 2 * g:2 * g + 2, :].rearrange("p t n -> p (t n)"),
                          start=True, stop=True).then_inc(S["vs_mm"], 1)
            self_scores(1)
            pe.wait_ge(S["vs_a"], 4)
            pe.wait_ge(S["vs_v"], 4)

            def self_out(t):
                pe.wait_ge(S["h2"], t + 1)
                if t >= 1:
                    pe.wait_ge(S["x2"], t)
                for k in range(KC):
                    ins = pe.transpose(R[3][:, P * k:P * (k + 1)], nb[:, t, P * k:P * (k + 1)], ident[:, :])
                ins.then_inc(S["hT_mm"], 1)

            def self_proj(t):
                pe.wait_ge(S["hT_low"], t + 1)
                for k in range(KC):
                    ins = split_mm(R[3][:, DM:2 * DM], hT_h[:, t, k, :], hT_l[:, t, k, :],
                                   aw_h[:, 3, k, :], aw_l[:, 3, k, :], k == 0, k == KC - 1)
                ins.then_inc(S["wo2_mm"], 1)

            for t in range(NT + 1):
                if t < NT:
                    pe.wait_ge(S["s2_prob"], t + 1)
                    if t >= 1:
                        pe.wait_ge(S["pt2"], t)
                    for g in range(8):
                        ins = pe.transpose(R[g // 4][:, P * (g % 4):P * (g % 4 + 1)],
                                           probs2[:, t % 2, P * g:P * (g + 1)], ident[:, :])
                    ins.then_inc(S["pt2_mm"], 1)
                if t >= 1:
                    self_out(t - 1)
                if t + 2 < NT:
                    self_scores(t + 2)
                if t < NT:
                    pe.wait_ge(S["pt2"], t + 1)
                    for b in range(2):
                        for g in range(8):
                            ins = pe.matmul(R[2][64 * b:64 * (b + 1), 32 * g:32 * (g + 1)],
                                            pt2[t % 2][:, P * g + 64 * b:P * g + 64 * (b + 1)],
                                            vexp[:, 2 * t + b, 32 * g:32 * (g + 1)], start=True, stop=True)
                    ins.then_inc(S["av2_mm"], 1)
                if t == NT - 1:
                    pe.wait_ge(S["s2_sub"], NT - 1)
                    x_transposes(4, (0,), Y)
                if t >= 1:
                    self_proj(t - 1)

            def gate_up(u, chunks=range(IC)):
                for ic in chunks:
                    pe.wait_ge(S["gu_low"], u.i * IC + (u.c // 2 * IC + ic + 1))
                    if u.after_zero(4, ic - 1):
                        pe.wait_ge(S["prod"], u.count(4, ic - 1))
                    for m in range(2):
                        for k in range(KC):
                            ins = split_mm(R[2 * (ic % 2) + m][:, :], gu_h[:, ic, m, k, :], gu_l[:, ic, m, k, :],
                                           xT_half(xT_h, k, u.half()), xT_half(xT_l, k, u.half()), k == 0, k == KC - 1)
                        ins.then_inc(S["gu_mm"], 1)

            def down(u):
                pe.wait_ge(S["dn_low"], u.i + 1)
                pe.wait_ge(S["act_low"], u.count(4, 4))
                if u.after_zero(4, -4):
                    pe.wait_ge(S["y_added"], u.count(4, -4))
                for j in range(4):
                    t = 4 * u.half() + j
                    for ic in range(IC):
                        ins = split_mm(y_tile(t), hx_h[:, u.half(), ic, P * j:P * (j + 1)],
                                       hx_l[:, u.half(), ic, P * j:P * (j + 1)], dn_h[:, ic, :], dn_l[:, ic, :],
                                       ic == 0, ic == IC - 1)
                    ins.then_inc(S["y_mm"], 1)

            pe.wait_ge(S["xT_low"], 18)
            gate_up(Unit(0, 0), (0,))
            pe.wait_ge(S["x2"], NT)
            gate_up(Unit(0, 0), (1,))
            pe.wait_ge(S["s2_sub"], NT)
            x_transposes(4, (1,), Y)
            gate_up(Unit(0, 0), (2, 3))
            pe.wait_ge(S["xT_low"], 20)
            pe.wait_ge(S["wr_low"], 1)
            for t in range(NT):
                both = Y[3][:, 2 * NE * t:2 * NE * (t + 1)]
                for k in range(KC):
                    pe.matmul(both.rearrange("p (s e) -> p s e", s=2), xT_h[:, k, P * t:P * (t + 1)], wr_r[:, :, k, :],
                              start=k == 0, stop=False, skip_group_check=True)
                    ins = pe.matmul(both[:, 0:NE], xT_l[:, k, P * t:P * (t + 1)], wr_h[:, k, :],
                                    start=False, stop=k == KC - 1, skip_group_check=True)
            ins.then_inc(S["route_mm"], 1)
            gate_up(Unit(0, 1))
            pe.wait_ge(S["top_gap"], 1)
            down(Unit(0, 0))
            gate_up(Unit(1, 0))
            down(Unit(0, 1))
            with pe.Fori(1, NE - 1) as e:
                for c in range(2):
                    gate_up(Unit(e, c + 1))
                    down(Unit(e, c))
            gate_up(Unit(NE - 1, 1))
            down(Unit(NE - 1, 0))
            down(Unit(NE - 1, 1))

        @block.scalar
        def _(act):
            def copy(out, in_, scale=None):
                if scale is None:
                    return act.activation(out, in_, ACT.Copy)
                return act.activation(out, in_, ACT.Copy, scale=scale)

            def load(name, dst, src):
                act.dma_start(dst, src).then_inc(ld[name], 16)

            def x_high(turn, w=None, halves=(0, 1), banks=R):
                for hf in halves:
                    for k in range(KC):
                        act.wait_ge(S["xT_mm"], 4 * turn + 2 * hf + k + 1)
                        copy(xT_half(xT_h, k, hf), banks[2 * hf + k][:, :],
                             None if w is None else w_ln[:, w, k:k + 1]).then_inc(S["xT_high"], 1)

            load("ctx", ctxT[:, :], a["ctxT"])
            load("gqk", gq_gk[:, :], a["gqk"])
            load("ctx_tok", ctx_tok[:, :, :], a["ctx"].rearrange("(t p) c -> p t c", p=P))
            for dst, src in ((gates[:, :], a["gates"].unsqueeze(0).broadcast_to([P, 4])),
                             (causal[:, :], a["c_causal"]),
                             (ident_b[:, :], a["c_ident_b"]), (head_mask[:, :], a["c_heads"]),
                             (iota8[:, :], a["c_iota"]), (swap[:, :], a["c_swap"]), (w_ln[:, :, :], a["w_ln"]),
                             (ffn_scale[:, :], a["ffn_scale"].unsqueeze(0).broadcast_to([P, DM])),
                             (mask_u8[:, :], a["mask"].unsqueeze(0).broadcast_to([P, NB * SQ]))):
                load("small", dst, src)
            load("wr", wr_raw[:, :, :], a["wr"])
            x_high(0)
            act.wait_ge(ld["ctx"], 16)
            copy(ctxT_h, ctxT[:, :]).then_inc(S["ctx_high"], 1)

            def vo_out(n, j):
                g = vo_turn(n, j)
                if g is not None:
                    act.wait_ge(S["vo0_mm"], g + 1)
                    copy(vo0[:, 512 * g:512 * (g + 1)], Y[g % 4][:, :]).then_inc(S["vo0"], 1)

            def vo_high(L, src, n):
                if n.c == 1 and pair_there(n.i):
                    if not isinstance(n.i, int) or n.i > 0:
                        act.wait_ge(L["o_mm"], n.i * 2)
                    copy(vo_h.rearrange("p h n -> p (h n)"), src[:, bass.ds(n.i * 512, 512)]).then_inc(L["vo_high"], 1)

            def split_exp(L, u1):
                act.wait_ge(L["sub"], u1.count(1, 1))
                p = probs[:, 8 * u1.half():8 * u1.half() + 8, :]
                act.activation(p, p, ACT.Exp, scale=float(HD) ** -0.5).then_inc(L["exp"], 1)

            def probs_T(L, n, bank):
                act.wait_ge(L["pt_mm"], n.count(1, 1))
                copy(probsT[0:64, :, 0, :], bank[0:64, :].rearrange("p (j n) -> p j n", j=4)).then_inc(L["pt_a"], 1)

            def attended(L, n, part, bank):
                act.wait_ge(L["av_mm"], n.count(2, part + 1))
                t = 4 * n.half() + 2 * part
                copy(ac_h[:, :, t:t + 2, :].rearrange("p h t n -> p t h n"),
                     bank[:, :].rearrange("p (t h n) -> p t h n", t=2, h=2)).then_inc(L["ac_high"], 1)

            def w_high0(j):
                if isinstance(j, int) and j == 2:
                    act.wait_ge(ld["wq0_rest"], 16)
                    act.wait_ge(ld["wk0_rest"], 16)
                copy(w_r[:, 0:512], wq_raw[:, bass.ds(j * 512, 512)])
                copy(wk_h, wk_raw[:, bass.ds(j * 256, 256)]).then_inc(L0["w_high"], 1)

            def step0(n):
                u1, u2, u3 = n.at(1), n.at(2), n.at(3)

                def take(j, bank):
                    act.wait_ge(L0["proj"], u3.count(4, j + 1))
                    copy(raw[:, j, :, :].rearrange("p g d -> p (g d)"), bank[:, :])
                    if u3.after_zero(4, j - 1):
                        act.wait_ge(L0["sumsq"], u3.count(4, j - 1))
                    act.activation(squares[:, j % 2, :, :].rearrange("p g d -> p (g d)"), bank[:, :],
                                   ACT.Square, scale=float(HD) ** -0.5).then_inc(L0["squares"], 1)

                def qk_out(j, bank):
                    act.wait_ge(L0["qk_mm"], u2.count(4, j + 1))
                    t = 4 * u2.half() + j
                    for g, dst, scale in ((0, qT_v, gqk[:, 0:1]), (1, kT_v, None)):
                        ins = copy(dst[:, t, :, :, :].rearrange("p b h q -> p h b q"),
                                   bank[:, 256 * g:256 * (g + 1)].rearrange("p (h b q) -> p h b q", h=2, b=2), scale)
                    ins.then_inc(L0["qk"], 1)

                if u2.there():
                    qk_out(0, R[1])
                    qk_out(1, R[2])
                if n.there():
                    probs_T(L0, n, R[3])
                if u1.there():
                    split_exp(L0, u1)
                if u3.there():
                    take(0, R[0])
                vo_out(n, 0)
                vo_high(L0, vo0, n)
                if n.there():
                    attended(L0, n, 0, R[2])
                if u2.there():
                    qk_out(2, R[1])
                if u3.there():
                    take(1, R[3])
                vo_out(n, 1)
                if u2.there():
                    qk_out(3, R[0])
                if n.there():
                    attended(L0, n, 1, R[1])
                if u3.there():
                    take(2, R[2])
                    vo_out(n, 2)
                    take(3, R[3])
                if step_is(n, 3):
                    act.wait_ge(ld["small"], SMALL)
                    act.activation(tgates[:, :], gates[:, :], ACT.Tanh).then_inc(S["gates"], 1)
                if n.c == 0 and pair_there(n.i + 2):
                    w_high0(n.i + 2)

            act.wait_ge(ld["wq0"], 16)
            act.wait_ge(ld["wk0"], 16)
            act.wait_ge(S["gqk"], 1)
            w_high0(0)
            pipeline(act, step0, 3)

            act.wait_ge(S["wf_scaled"], 1)
            copy(w_r[:, 4608:5120], wf_raw).then_inc(S["wf_high"], 1)
            act.wait_ge(L0["vo_low"], PAIRS)
            for g in range(PAIRS):
                act.wait_ge(S["m1_mm"], g + 1)
                copy(m1[:, 512 * g:512 * (g + 1)], R[g % 4][:, :]).then_inc(S["m1"], 1)
            def ffn_tanh():
                act.wait_ge(S["ffn_len"], 1)
                act.activation(tiny[:, 2, :], tiny[:, 1, :], ACT.Tanh).then_inc(S["ffn_tanh"], 1)

            x_high(1)
            for t in range(NT):
                act.wait_ge(S["ffn_mm"], t // 2 * 2 + 2)
                act.activation(qT[:, DM * t:DM * (t + 1)], y_tile(t), ACT.Square,
                               accum_out=tiny[:, 0, t:t + 1]).then_inc(S["ffn_sumsq"], 1)
            for g in range(PAIRS):
                act.wait_ge(S["vo1_mm"], g + 1)
                copy(vo1[:, 512 * g:512 * (g + 1)], R[g % 4][:, :]).then_inc(S["vo1"], 1)
                if g == 3:
                    ffn_tanh()
            act.wait_ge(ld["attn"], 16)
            copy(aw[:, :, 0, :], attn_raw.rearrange("p (w n) -> p w n", w=4)).then_inc(S["aw_high"], 1)
            x_high(2)

            def w_high1(j):
                copy(w_r[:, 0:512], m1[:, bass.ds(j * 512, 512)]).then_inc(L1["w_high"], 1)

            def step1(n):
                u1, u2, um = n.at(1), n.at(2), n.at(-1)
                B = [R[(2 * n.half() + k) % 4] for k in range(4)]
                vo_high(L1, vo1, n)

                def t_out(hh, bank):
                    act.wait_ge(L1["proj"], u2.count(2, hh + 1))
                    t = 4 * u2.half()
                    copy(qT_v[:, t:t + 4, :, hh, :].rearrange("p t b q -> p (t b) q"),
                         bank[:, :].rearrange("p (tb q) -> p tb q", q=SQ)).then_inc(L1["qk"], 1)

                if u2.there():
                    t_out(0, B[1])
                if u1.there():
                    split_exp(L1, u1)
                if n.there():
                    probs_T(L1, n, B[2])
                if u2.there():
                    t_out(1, B[3])
                if n.c == 1 and pair_there(n.i + 2):
                    act.wait_ge(L1["proj"], u2.count(2, 2))
                    w_high1(n.i + 2)
                if n.there():
                    attended(L1, n, 0, B[0])
                    attended(L1, n, 1, B[1])

            act.wait_ge(S["vo1"], PAIRS)
            w_high1(0)
            pipeline(act, step1, 2)

            x_high(3, 0)
            for hf in range(2):
                for oc in range(KC):
                    act.wait_ge(S["qk2_mm"], 4 * hf + oc + 1)
                    copy(qT2[:, oc, HALF * hf:HALF * (hf + 1)], (Y, R)[hf][oc][:, :]).then_inc(S["q2"], 1)

            def self_exp(t):
                act.wait_ge(S["s2_sub"], t + 1)
                act.activation(probs2[:, t % 2, :], probs2[:, t % 2, :], ACT.Exp,
                               scale=float(AD) ** -0.5).then_inc(S["s2_exp"], 1)

            for g in range(4):
                act.wait_ge(S["v2_mm"], g + 1)
                copy(v_sb[:, 2 * g:2 * g + 2, :].rearrange("p t n -> p (t n)"), R[g][:, :]).then_inc(S["v2"], 1)
                if g == 1:
                    self_exp(0)
            act.wait_ge(S["zeroed"], 3)
            for g in range(4):
                act.wait_ge(S["vs_mm"], g + 1)
                copy(vexp_v[0:64, 4 * g + 1:4 * g + 4:2, :, 0, :], v_parts(R[g])[0:64, :, :, 0, :]).then_inc(S["vs_a"], 1)
            act.wait_ge(ld["gu"], 16)
            act.wait_ge(L1["o_mm"], UNITS)
            for ic in range(IC):
                copy(w_r[:, 512 * ic:512 * (ic + 1)], gu_raw[:, 512 * ic:512 * (ic + 1)]).then_inc(S["gu_high"], 1)
            act.wait_ge(ld["wr"], 16)
            copy(wr_h.rearrange("p k n -> p (k n)"), wr_raw[:, :, :].rearrange("p k n -> p (k n)")).then_inc(S["wr_high"], 1)

            def rms_normed(hf):
                act.wait_ge(S["rstd"], 2 * 4 + hf + 1)
                for t in range(4 * hf, 4 * hf + 4):
                    copy(nb[:, t, :], x1[:, t, :], rstd[:, t:t + 1]).then_inc(S["normed"], 1)

            for t in range(NT + 1):
                if t < NT:
                    act.wait_ge(S["pt2_mm"], t + 1)
                    copy(pt2[t % 2][:, 0:512], R[0][:, :])
                    copy(pt2[t % 2][:, 512:1024], R[1][:, :]).then_inc(S["pt2"], 1)
                if t >= 1:
                    act.wait_ge(S["hT_mm"], t)
                    copy(hT_h[:, t - 1, :, :].rearrange("p k n -> p (k n)"), R[3][:, 0:DM]).then_inc(S["hT_high"], 1)
                if t + 1 < NT:
                    self_exp(t + 1)
                if t < NT:
                    act.wait_ge(S["av2_mm"], t + 1)
                    copy(nb[:, t, :], R[2][:, 0:DM]).then_inc(S["h2"], 1)
                if t == NT - 2:
                    rms_normed(0)

            x_high(4, 1, (0,), Y)
            rms_normed(1)
            def expert_unit(u, splits, between=None):
                def silu(ic):
                    act.wait_ge(S["gu_mm"], u.count(8, 2 * ic + 1))
                    if u.after_zero(4, ic - 1):
                        act.wait_ge(S["prod"], u.count(4, ic - 1))
                    act.activation(silu_buf[:, ic % 2, :], R[2 * (ic % 2)][:, :], ACT.Silu).then_inc(S["silu"], 1)

                def high(ic):
                    act.wait_ge(S["prod"], u.count(4, ic + 1))
                    copy(hx_h[:, u.half(), ic, :], prod_buf[:, ic, :]).then_inc(S["act_high"], 1)
                    if splits:
                        act.wait_ge(S["gu_mm"], u.count(8, 2 * ic + 2))
                        if ic == 0:
                            act.wait_ge(ld["gu"], u.i * 16 + 32)
                        copy(w_r[:, 512 * ic:512 * (ic + 1)], gu_raw[:, 512 * ic:512 * (ic + 1)]).then_inc(S["gu_high"], 1)

                for ic in range(IC):
                    silu(ic)
                    if ic >= 1:
                        high(ic - 1)
                    if ic == 1 and between:
                        between()
                high(IC - 1)

            def down_high(e):
                act.wait_ge(ld["dn"], e * 16 + 16)
                if not isinstance(e, int) or e > 0:
                    act.wait_ge(S["y_mm"], e * 8)
                copy(w_r[:, 4096:5120], dn_raw).then_inc(S["dn_high"], 1)

            def top_exp():
                act.wait_ge(S["top_gap"], 1)
                act.activation(tiny[:, 1, :], tiny[:, 0, :], ACT.Exp).then_inc(S["top_exp"], 1)

            expert_unit(Unit(0, 0), False, lambda: x_high(4, 1, (1,), Y))
            down_high(0)
            expert_unit(Unit(0, 1), True, top_exp)
            with act.Fori(1, NE - 1) as e:
                expert_unit(Unit(e, 0), False)
                down_high(e)
                expert_unit(Unit(e, 1), True)
            expert_unit(Unit(NE - 1, 0), False)
            down_high(NE - 1)
            expert_unit(Unit(NE - 1, 1), False)

        @block.vector
        def _(dve):
            link = Chain(dve, S["dve_step"])

            def norm_stats(hf, src, before=None):
                if before:
                    before(hf)
                for t in range(4 * hf, 4 * hf + 4):
                    ins = dve.bn_stats(bn6[:, t, :], src[:, t, :])
                link(ins)
                for t in range(4 * hf, 4 * hf + 4):
                    ins = dve.bn_aggr(mean_var[:, t, :], bn6[:, t, :])
                ins.then_inc(S["stats"], 1)

            def normalise(hf, src, dst, scale=rstd):
                for t in range(4 * hf, 4 * hf + 4):
                    dve.tensor_scalar(dst[:, t, :], src[:, t, :], mean_var[:, t, 0:1], scale[:, t:t + 1],
                                      ALU.subtract, ALU.mult).then_inc(S["normed"], 1)

            def norm(k, src, dst, before=None):
                for hf in range(2):
                    norm_stats(hf, src, before)
                for hf in range(2):
                    dve.wait_ge(S["rstd"], 2 * k + hf + 1)
                    normalise(hf, src, dst)

            def x_low(turn, w=None, halves=(0, 1), banks=R):
                for hf in halves:
                    for k in range(KC):
                        dve.wait_ge(S["xT_high"], 4 * turn + 2 * hf + k + 1)
                        bank = banks[2 * hf + k][:, :]
                        if w is None:
                            ins = dve.tensor_tensor(xT_half(xT_l, k, hf), bank, f(xT_half(xT_h, k, hf)), ALU.subtract)
                        else:
                            ins = dve.scalar_tensor_tensor(out=xT_half(xT_l, k, hf), in0=bank, scalar=w_ln[:, w, k:k + 1],
                                                           in1=f(xT_half(xT_h, k, hf)), op0=ALU.mult, op1=ALU.subtract)
                        ins.then_inc(S["xT_low"], 1)

            def add_gated(L, g):
                def go(hf):
                    dve.wait_ge(L["o_mm"], UNITS - 1 + hf)
                    for t in range(4 * hf, 4 * hf + 4):
                        ins = dve.scalar_tensor_tensor(out=x_res[:, t, :], in0=y_tile(t), scalar=tgates[:, g:g + 1],
                                                       in1=x_res[:, t, :], op0=ALU.mult, op1=ALU.add)
                    link(ins)
                return go

            norm(0, x_res, nb, before=lambda hf: dve.wait_ge(ld[f"x{hf}"], 16))
            dve.wait_ge(ld["gqk"], 16)
            dve.tensor_tensor(gqk[:, :], gq_gk[:, 0:1], gq_gk[:, 1:2], ALU.mult).then_inc(S["gqk"], 1)
            x_low(0)
            dve.wait_ge(S["ctx_high"], 1)
            dve.tensor_tensor(ctxT_l, ctxT[:, :], f(ctxT_h), ALU.subtract).then_inc(S["ctx_low"], 1)
            dve.wait_ge(S["zeroed"], 1)

            def sub_max(L, u1, src):
                c = u1.half()
                dve.tensor_reduce(smax[:, c, :], src, AX.X, ALU.max).then_inc(L["smax"], 1)
                dve.wait_ge(L["smax"], u1.count(1, 1))
                dve.tensor_tensor(probs[:, 8 * c:8 * c + 8, :], src,
                                  smax[:, c, :].unsqueeze(2).broadcast_to([P, 8, SQ]), ALU.subtract).then_inc(L["sub"], 1)

            def sum_exp(L, u1):
                c = u1.half()
                dve.wait_ge(L["exp"], u1.count(1, 1))
                dve.tensor_reduce(ssum[:, c, :], probs[:, 8 * c:8 * c + 8, :], AX.X, ALU.add).then_inc(L["ssum"], 1)
                dve.wait_ge(L["ssum"], u1.count(1, 1))

            def probs_T(L, n, bank):
                dve.wait_ge(L["pt_mm"], n.count(1, 1))
                dve.tensor_copy(probsT[64:128, :, 1, :],
                                bank[64:128, :].rearrange("p (j n) -> p j n", j=4)).then_inc(L["pt_v"], 1)

            def attended(L, n, part, bank):
                dve.wait_ge(L["ac_high"], n.count(2, part + 1))
                t = 4 * n.half() + 2 * part
                dve.tensor_tensor(ac_l[:, :, t:t + 2, :].rearrange("p h t n -> p t h n"),
                                  bank[:, :].rearrange("p (t h n) -> p t h n", t=2, h=2),
                                  f(ac_h[:, :, t:t + 2, :]).rearrange("p h t n -> p t h n"),
                                  ALU.subtract).then_inc(L["ac_low"], 1)

            def wk_low(j):
                dve.wait_ge(L0["w_high"], j + 1)
                dve.tensor_tensor(wk_l, wk_raw[:, bass.ds(j * 256, 256)], f(wk_h), ALU.subtract).then_inc(L0["wk_low"], 1)

            def step0(n):
                u1, u2, u3 = n.at(1), n.at(2), n.at(3)

                def sum_squares(u, j):
                    dve.wait_ge(L0["squares"], u.count(4, j + 1))
                    dve.tensor_reduce(sumsq[:, j, :], squares[:, j % 2, :, :], AX.X, ALU.add).then_inc(L0["sumsq"], 1)

                def scale(u, j):
                    dve.wait_ge(L0["rnorm"], u.count(2, j // 2 + 1))
                    dve.tensor_tensor(raw[:, j, :, :], raw[:, j, :, :],
                                      rnorm[:, j, :].unsqueeze(2).broadcast_to([P, 4, HD]),
                                      ALU.mult).then_inc(L0["scaled"], 1)

                if u1.there():
                    dve.wait_ge(L0["scores"], u1.count(1, 1))
                    sub_max(L0, u1, R[0][:, :].rearrange("p (b k) -> p b k", b=8))
                if n.c == 1 and pair_there(n.i + 2):
                    wk_low(n.i + 2)
                if n.there():
                    probs_T(L0, n, R[3])
                if u2.there():
                    scale(u2, 2)
                    scale(u2, 3)
                if n.c == 1 and pair_there(n.i):
                    dve.wait_ge(L0["vo_high"], n.i + 1)
                    dve.tensor_tensor(vo_l.rearrange("p h n -> p (h n)"), vo0[:, bass.ds(n.i * 512, 512)],
                                      f(vo_h.rearrange("p h n -> p (h n)")), ALU.subtract).then_inc(L0["vo_low"], 1)
                if u1.there():
                    sum_exp(L0, u1)
                    dve.reciprocal(srec[:, u1.half(), :], ssum[:, u1.half(), :]).then_inc(L0["srec"], 1)
                if u3.there():
                    sum_squares(u3, 0)
                if n.there():
                    attended(L0, n, 0, R[2])
                if u3.there():
                    sum_squares(u3, 1)
                if n.there():
                    attended(L0, n, 1, R[1])
                if u3.there():
                    scale(u3, 0)
                    scale(u3, 1)
                    sum_squares(u3, 2)
                    sum_squares(u3, 3)
                if step_is(n, 3):
                    dve.wait_ge(ld["small"], SMALL)
                    dve.tensor_reduce(mask_any[:, :], mask_u8[:, :].rearrange("p (b k) -> p b k", b=NB), AX.X,
                                      ALU.max).then_inc(S["mask_any"], 1)
                    dve.tensor_scalar(mask_add[:, :, :].rearrange("p b k -> p (b k)"), mask_u8[:, :], 1.0, BIG,
                                      ALU.subtract, ALU.mult).then_inc(S["mask_add"], 1)

            pipeline(dve, step0, 3)

            dve.wait_ge(S["gates"], 1)
            dve.wait_ge(ld["wf"], 16)
            wf_k = wf_raw.rearrange("p (k n) -> p k n", k=KC)
            dve.tensor_tensor(wf_k, wf_k, ffn_scale[:, :].unsqueeze(1).broadcast_to([P, KC, DM]),
                              ALU.mult).then_inc(S["wf_scaled"], 1)
            norm(1, x_res, nb, before=add_gated(L0, 0))
            dve.wait_ge(S["wf_high"], 1)
            dve.tensor_tensor(w_r[:, 5120:5632], wf_raw, f(w_r[:, 4608:5120]), ALU.subtract).then_inc(S["wf_low"], 1)
            x_low(1)
            dve.wait_ge(S["ffn_len0"], 1)
            dve.tensor_scalar(tiny[:, 1, :], tiny[:, 3, :], 1e-7, None, ALU.max).then_inc(S["ffn_len"], 1)
            dve.wait_ge(S["ffn_tanh"], 1)
            link(dve.tensor_scalar(tiny[:, 4, :], tiny[:, 1, :], 1e-7, None, ALU.add))
            link(dve.reciprocal(tiny[:, 5, :], tiny[:, 4, :]))
            link(dve.tensor_tensor(tiny[:, 6, :], tiny[:, 2, :], tiny[:, 5, :], ALU.mult))
            link(dve.tensor_tensor(tiny[:, 7, :], tiny[:, 6, :], tiny[:, 3, :], ALU.mult))
            link(dve.tensor_scalar(tiny[:, 7, :], tiny[:, 7, :], 1e-7, None, ALU.max))
            link(dve.reciprocal(tiny[:, 8, :], tiny[:, 7, :]))
            link(dve.tensor_scalar(tiny[:, 8, :], tiny[:, 8, :], 0.99, 1.0, ALU.mult, ALU.min))
            link(dve.tensor_tensor(tiny[:, 9, :], tiny[:, 6, :], tiny[:, 8, :], ALU.mult))
            link(dve.tensor_scalar(tiny[:, 10, :], tiny[:, 9, :], tgates[:, 2:3], None, ALU.mult))

            def add_ffn(hf):
                for t in range(4 * hf, 4 * hf + 4):
                    ins = dve.scalar_tensor_tensor(out=x_res[:, t, :], in0=y_tile(t), scalar=tiny[:, 10, t:t + 1],
                                                   in1=x_res[:, t, :], op0=ALU.mult, op1=ALU.add)
                link(ins)

            norm(2, x_res, nb, before=add_ffn)
            x_low(2)

            def step1(n):
                u1, u2 = n.at(1), n.at(2)
                B = [R[(2 * n.half() + k) % 4] for k in range(4)]
                if u1.there():
                    c = u1.half()
                    p = probs[:, 8 * c:8 * c + 8, :]
                    dve.wait_ge(L1["scores"], u1.count(1, 1))
                    dve.tensor_tensor(p, B[0][:, :].rearrange("p (b k) -> p b k", b=8), mask_add[:, 8 * c:8 * c + 8, :],
                                      ALU.add).then_inc(L1["masked"], 1)
                    dve.wait_ge(L1["masked"], u1.count(1, 1))
                    sub_max(L1, u1, p)
                if n.there():
                    probs_T(L1, n, B[2])
                if u1.there():
                    sum_exp(L1, u1)
                    dve.reciprocal(srec[:, c, :], ssum[:, c, :]).then_inc(L1["srec0"], 1)
                    dve.wait_ge(L1["srec0"], u1.count(1, 1))
                    dve.tensor_tensor(srec[:, c, :], srec[:, c, :], mask_any[:, 8 * c:8 * c + 8],
                                      ALU.mult).then_inc(L1["srec"], 1)
                if n.there():
                    attended(L1, n, 0, B[0])
                    attended(L1, n, 1, B[1])

            pipeline(dve, step1, 2)

            for hf in range(2):
                norm_stats(hf, x_res, add_gated(L1, 1))
            for hf in range(2):
                dve.wait_ge(S["rms_rstd"], hf + 1)
                normalise(hf, x_res, nb, rms_rstd)
            x_low(3, 0)
            for hf in range(2):
                dve.wait_ge(S["rstd"], 2 * 3 + hf + 1)
                for t in range(4 * hf, 4 * hf + 4):
                    ins = dve.tensor_scalar(x1[:, t, :], x_res[:, t, :], mean_var[:, t, 0:1], rstd[:, t:t + 1],
                                            ALU.subtract, ALU.mult)
            link(ins)

            def key_blocks(t):
                if t >= 2:
                    dve.wait_ge(S["s2_mm"], t - 1)
                for oc in range(KC):
                    c = SQ * 2 * t
                    ins = dve.tensor_tensor(kexp[:, t % 2, 0, oc, :].rearrange("p (h k) -> p h k", h=8),
                                            kT2[:, oc, c:c + SQ].unsqueeze(1).broadcast_to([P, 8, SQ]),
                                            head_mask[:, :].unsqueeze(2).broadcast_to([P, 8, SQ]), ALU.mult)
                ins.then_inc(S["kexp_v"], 1)

            def self_softmax(t):
                p = probs2[:, t % 2, :].rearrange("p (h k) -> p h k", k=SQ)
                scores = [Y[2 * (t % 2) + oc][:, :].rearrange("p (h k) -> p h k", k=SQ) for oc in range(KC)]
                dve.wait_ge(S["s2_mm"], t + 1)
                for oc in range(KC):
                    ins = dve.tensor_reduce(row_max[:, t % 2, 8 * oc:8 * oc + 8], scores[oc], AX.X, ALU.max)
                ins.then_inc(S["s2_row_max"], 1)
                dve.wait_ge(S["s2_row_max"], t + 1)
                if t >= 2:
                    dve.wait_ge(S["pt2_mm"], t - 1)
                for oc in range(KC):
                    ins = dve.tensor_tensor(p[:, 8 * oc:8 * oc + 8, :], scores[oc],
                                            row_max[:, t % 2, 8 * oc:8 * oc + 8].unsqueeze(2).broadcast_to([P, 8, SQ]),
                                            ALU.subtract)
                ins.then_inc(S["s2_sub"], 1)

            def self_sum(t):
                p = probs2[:, t % 2, :].rearrange("p (h k) -> p h k", k=SQ)
                dve.wait_ge(S["s2_exp"], t + 1)
                link(dve.tensor_reduce(row_sum[:, t % 2, :], p, AX.X, ALU.add))
                dve.reciprocal(row_rec[:, t % 2, :], row_sum[:, t % 2, :]).then_inc(S["s2_rec"], 1)

            for hf in range(2):
                for oc in range(KC):
                    dve.wait_ge(S["qk2_mm"], 4 * hf + 2 + oc + 1)
                    dve.tensor_copy(kT2[:, oc, HALF * hf:HALF * (hf + 1)], (Y, R)[hf][2 + oc][:, :]).then_inc(S["k2"], 1)
                dve.wait_ge(S["k2"], 2 * hf + 2)
                if hf == 0:
                    key_blocks(0)
                    key_blocks(1)
            self_softmax(0)
            dve.wait_ge(S["zeroed"], 3)
            dve.wait_ge(S["v2"], 4)
            v_all = v_sb[:, :, :].rearrange("p t (g r d) -> p t g r d", g=8, r=2)
            dve.tensor_copy(vexp_v[0:64, 0:NB:2, :, 0, :], v_all[0:64, :, :, 0, :])
            dve.tensor_copy(vexp_v[64:128, 1:NB:2, :, 1, :], v_all[64:128, :, :, 1, :])
            self_sum(0)
            for g in range(4):
                dve.wait_ge(S["vs_mm"], g + 1)
                dve.tensor_copy(vexp_v[64:128, 4 * g:4 * g + 3:2, :, 1, :],
                                v_parts(R[g])[64:128, :, :, 1, :]).then_inc(S["vs_v"], 1)
            key_blocks(2)

            def self_add(t):
                dve.wait_ge(S["wo2_mm"], t + 1)
                dve.tensor_tensor(x1[:, t, :], R[3][:, DM:2 * DM], x1[:, t, :], ALU.add).then_inc(S["x2"], 1)
                dve.wait_ge(S["x2"], t + 1)
                link(dve.bn_stats(bn6[:, t, :], x1[:, t, :]))
                link(dve.bn_aggr(mean_var[:, t, :], bn6[:, t, :]))
                if t % 4 == 3:
                    m, v = mean_var[:, t - 3:t + 1, 0], mean_var[:, t - 3:t + 1, 1]
                    link(dve.tensor_tensor(m, m, m, ALU.mult))
                    dve.tensor_tensor(v, v, m, ALU.add).then_inc(S["stats"], 1)

            for t in range(NT + 1):
                if t >= 2:
                    self_add(t - 2)
                if t + 1 < NT:
                    self_softmax(t + 1)
                if t >= 1:
                    dve.wait_ge(S["hT_high"], t)
                    dve.tensor_tensor(hT_l[:, t - 1, :, :].rearrange("p k n -> p (k n)"), R[3][:, 0:DM],
                                      f(hT_h[:, t - 1, :, :].rearrange("p k n -> p (k n)")),
                                      ALU.subtract).then_inc(S["hT_low"], 1)
                if t + 1 < NT:
                    self_sum(t + 1)
                if t + 3 < NT:
                    key_blocks(t + 3)

            dve.wait_ge(S["wr_high"], 1)
            dve.tensor_tensor(wr_l, wr_raw[:, :, :], f(wr_h), ALU.subtract).then_inc(S["wr_low"], 1)
            x_low(4, 1, (0,), Y)
            self_add(NT - 1)

            def top_two():
                dve.wait_ge(S["route_mm"], 1)
                both = Y[3][:, 0:2 * NT * NE].rearrange("p (t s e) -> p t s e", t=NT, s=2)
                link(dve.tensor_copy(logits[:, :, :], both[:, :, 0, :]))
                link(dve.tensor_tensor(logits[:, :, :], both[:, :, 1, :], logits[:, :, :], ALU.add))
                for t in range(NT):
                    ins = dve.max(top8[:, t, :], logits[:, t, :])
                link(ins)
                for t in range(NT):
                    ins = dve.max_index(top8_at[:, t, :], top8[:, t, :], logits[:, t, :])
                link(ins)
                link(dve.tensor_copy(top_at[:, :, :], top8_at[:, :, 0:2]))
                dve.tensor_tensor(tiny[:, 0, :], top8[:, :, 1], top8[:, :, 0], ALU.subtract).then_inc(S["top_gap"], 1)

            def expert_weights():
                dve.wait_ge(S["top_exp"], 1)
                link(dve.tensor_scalar(tiny[:, 2, :], tiny[:, 1, :], 1.0, None, ALU.add))
                link(dve.reciprocal(tiny[:, 3, :], tiny[:, 2, :]))
                link(dve.tensor_tensor(tiny[:, 4, :], tiny[:, 1, :], tiny[:, 3, :], ALU.mult))
                for j in range(2):
                    link(dve.tensor_tensor(chosen[:, j, :, :], iota8[:, :].unsqueeze(2).broadcast_to([P, NE, NT]),
                                           top_at[:, :, j].unsqueeze(1).broadcast_to([P, NE, NT]), ALU.is_equal))
                    link(dve.tensor_tensor(chosen[:, j, :, :], chosen[:, j, :, :],
                                           tiny[:, 3 + j, :].unsqueeze(1).broadcast_to([P, NE, NT]), ALU.mult))
                link(dve.tensor_tensor(cw[:, :].rearrange("p (e t) -> p e t", e=NE), chosen[:, 0, :, :], chosen[:, 1, :, :],
                                       ALU.add))

            def products(u, between=None):
                def product(ic):
                    dve.wait_ge(S["silu"], u.count(4, ic + 1))
                    dve.wait_ge(S["gu_mm"], u.count(8, 2 * ic + 2))
                    if u.after_zero(4, ic - 3):
                        dve.wait_ge(S["act_low"], u.count(4, ic - 3))
                    dve.tensor_tensor(prod_buf[:, ic, :], R[2 * (ic % 2) + 1][:, :], silu_buf[:, ic % 2, :],
                                      ALU.mult).then_inc(S["prod"], 1)

                def low(ic):
                    dve.wait_ge(S["act_high"], u.count(4, ic + 1))
                    dve.tensor_tensor(hx_l[:, u.half(), ic, :], prod_buf[:, ic, :], f(hx_h[:, u.half(), ic, :]),
                                      ALU.subtract).then_inc(S["act_low"], 1)

                for ic in range(IC):
                    product(ic)
                    if ic >= 1:
                        low(ic - 1)
                    if ic == 1 and between:
                        between()
                low(IC - 1)

            def add_expert(u):
                if u.half() == 0:
                    dve.tensor_copy(cw_now[:, :], cw[:, bass.ds(u.i * NT, NT)]).then_inc(S["cw_now"], 1)
                    dve.wait_ge(S["cw_now"], u.i + 1)
                for j in range(4):
                    t = 4 * u.half() + j
                    dve.wait_ge(S["y_mm"], u.count(4, j // 2 * 2 + 2))
                    dve.scalar_tensor_tensor(out=x1[:, t, :], in0=y_tile(t), scalar=cw_now[:, t:t + 1],
                                             in1=x1[:, t, :], op0=ALU.mult, op1=ALU.add).then_inc(S["y_added"], 1)

            products(Unit(0, 0), lambda: x_low(4, 1, (1,), Y))
            top_two()
            products(Unit(0, 1), expert_weights)
            add_expert(Unit(0, 0))
            products(Unit(1, 0))
            add_expert(Unit(0, 1))
            with dve.Fori(1, NE - 1) as e:
                for c in range(2):
                    products(Unit(e, c + 1))
                    add_expert(Unit(e, c))
            products(Unit(NE - 1, 1))
            add_expert(Unit(NE - 1, 0))
            add_expert(Unit(NE - 1, 1))
            dve.wait_ge(S["y_added"], 4 * UNITS)
            for hf in range(2):
                for t in range(4 * hf, 4 * hf + 4):
                    ins = dve.scalar_tensor_tensor(out=nb[:, t, :], in0=x1[:, t, :], scalar=tgates[:, 3:4],
                                                   in1=x_res[:, t, :], op0=ALU.mult, op1=ALU.add)
                ins.then_inc(S["out_ready"], 1)

        @block.gpsimd
        def _(pool):
            def rstd_of(k, halves=(0, 1)):
                for hf in halves:
                    s = slice(4 * hf, 4 * hf + 4)
                    pool.wait_ge(S["stats"], 2 * k + hf + 1)
                    pool.tensor_scalar(var_eps[:, s], mean_var[:, s, 1], EPS, None, ALU.add).then_inc(S["var_eps"], 1)
                    pool.wait_ge(S["var_eps"], 2 * k + hf + 1)
                    pool.tensor_tensor(rstd[:, s], var_eps[:, s], neg_half[:, 0:4], ALU.pow).then_inc(S["rstd"], 1)

            pool.memset(neg_half[:, :], -0.5)
            pool.memset(eps8[:, :], EPS)
            pool.memset(pos_half[:, :], 0.5).then_inc(S["halves"], 1)
            pool.wait_ge(S["halves"], 1)
            rstd_of(0)
            pool.memset(probsT[:, :, :, :], 0.0).then_inc(S["zeroed"], 1)

            def probabilities(L, u1):
                c = u1.half()
                pool.wait_ge(L["srec"], u1.count(1, 1))
                p = probs[:, 8 * c:8 * c + 8, :]
                pool.tensor_tensor(p, p, srec[:, c, :].unsqueeze(2).broadcast_to([P, 8, SQ]),
                                   ALU.mult).then_inc(L["prob"], 1)

            def vo_low(L, src, n):
                if n.c == 1 and pair_there(n.i):
                    pool.wait_ge(L["vo_high"], n.i + 1)
                    pool.tensor_tensor(vo_l.rearrange("p h n -> p (h n)"), src[:, bass.ds(n.i * 512, 512)],
                                       f(vo_h.rearrange("p h n -> p (h n)")), ALU.subtract).then_inc(L["vo_low"], 1)

            def w_low0(j):
                pool.wait_ge(L0["w_high"], j + 1)
                pool.tensor_tensor(w_r[:, 512:1024], wq_raw[:, bass.ds(j * 512, 512)], f(w_r[:, 0:512]),
                                   ALU.subtract).then_inc(L0["w_low"], 1)

            def step0(n):
                u1, u3 = n.at(1), n.at(3)
                def norms(j):
                    pool.wait_ge(L0["sumsq"], u3.count(4, j + 2))
                    pool.tensor_tensor(sumsq_eps[:, j:j + 2, :].rearrange("p j g -> p (j g)"),
                                       sumsq[:, j:j + 2, :].rearrange("p j g -> p (j g)"), eps8[:, :],
                                       ALU.add).then_inc(L0["sumsq_eps"], 1)
                    pool.wait_ge(L0["sumsq_eps"], u3.count(2, j // 2 + 1))
                    pool.tensor_tensor(rnorm[:, j:j + 2, :].rearrange("p j g -> p (j g)"),
                                       sumsq_eps[:, j:j + 2, :].rearrange("p j g -> p (j g)"), neg_half[:, 0:8],
                                       ALU.pow).then_inc(L0["rnorm"], 1)

                if u1.there():
                    probabilities(L0, u1)
                if u3.there():
                    norms(0)
                if n.c == 0 and pair_there(n.i + 2):
                    w_low0(n.i + 2)
                if u3.there():
                    norms(2)

            w_low0(0)
            pipeline(pool, step0, 3)
            rstd_of(1)
            pool.wait_ge(S["ffn_sumsq"], NT)
            pool.tensor_tensor(tiny[:, 3, :], tiny[:, 0, :], pos_half[:, :], ALU.pow).then_inc(S["ffn_len0"], 1)
            rstd_of(2)
            pool.wait_ge(S["aw_high"], 1)
            pool.tensor_tensor(aw[:, :, 1, :], attn_raw.rearrange("p (w n) -> p w n", w=4), f(aw[:, :, 0, :]),
                               ALU.subtract).then_inc(S["aw_low"], 1)

            def w_low1(j):
                pool.wait_ge(L1["w_high"], j + 1)
                pool.tensor_tensor(w_r[:, 512:1024], m1[:, bass.ds(j * 512, 512)], f(w_r[:, 0:512]),
                                   ALU.subtract).then_inc(L1["w_low"], 1)

            def step1(n):
                u1 = n.at(1)
                vo_low(L1, vo1, n)
                if u1.there():
                    probabilities(L1, u1)
                if n.c == 1 and pair_there(n.i + 2):
                    w_low1(n.i + 2)

            w_low1(0)
            pipeline(pool, step1, 2)
            pool.memset(reg_d[:, 0:2048], 0.0).then_inc(S["zeroed"], 1)
            pool.memset(reg_d[:, 2048:4096], 0.0).then_inc(S["zeroed"], 1)
            for hf in range(2):
                s = slice(4 * hf, 4 * hf + 4)
                pool.wait_ge(S["stats"], 2 * 3 + hf + 1)
                pool.tensor_scalar(rms_var[:, s], mean_var[:, s, 1], 1.0 + EPS, EPS * EPS, ALU.mult,
                                   ALU.add).then_inc(S["rms_var"], 1)
                pool.wait_ge(S["rms_var"], hf + 1)
                pool.tensor_tensor(rms_rstd[:, s], rms_var[:, s], neg_half[:, 0:4], ALU.pow).then_inc(S["rms_rstd"], 1)
            rstd_of(3)

            def key_blocks(t):
                if t % 4 == 0:
                    pool.wait_ge(S["k2"], 2 * (t // 4) + 2)
                if t >= 2:
                    pool.wait_ge(S["s2_mm"], t - 1)
                for oc in range(KC):
                    c = SQ * (2 * t + 1)
                    ins = pool.tensor_tensor(kexp[:, t % 2, 1, oc, :].rearrange("p (h k) -> p h k", h=8),
                                             kT2[:, oc, c:c + SQ].unsqueeze(1).broadcast_to([P, 8, SQ]),
                                             head_mask[:, :].unsqueeze(2).broadcast_to([P, 8, SQ]), ALU.mult)
                ins.then_inc(S["kexp_p"], 1)

            def self_probabilities(t):
                pool.wait_ge(S["s2_rec"], t + 1)
                p = probs2[:, t % 2, :].rearrange("p (h k) -> p h k", k=SQ)
                pool.tensor_tensor(p, p, row_rec[:, t % 2, :].unsqueeze(2).broadcast_to([P, AH, SQ]),
                                   ALU.mult).then_inc(S["s2_prob"], 1)

            def gate_up_low(j, ic):
                pool.wait_ge(S["gu_high"], j * IC + (ic + 1))
                s = slice(512 * ic, 512 * (ic + 1))
                pool.tensor_tensor(w_r[:, 2048 + 512 * ic:2048 + 512 * (ic + 1)], gu_raw[:, s], f(w_r[:, s]),
                                   ALU.subtract).then_inc(S["gu_low"], 1)

            def down_low(e):
                pool.wait_ge(S["dn_high"], e + 1)
                pool.tensor_tensor(w_r[:, 5120:6144], dn_raw, f(w_r[:, 4096:5120]), ALU.subtract).then_inc(S["dn_low"], 1)

            key_blocks(0)
            key_blocks(1)
            key_blocks(2)
            self_probabilities(0)
            for t in range(NT - 1):
                self_probabilities(t + 1)
                if t + 3 < NT:
                    key_blocks(t + 3)
                if t < IC:
                    gate_up_low(0, t)
                if t == 5:
                    rstd_of(4, (0,))
            rstd_of(4, (1,))
            with pool.Fori(0, NE - 1) as e:
                down_low(e)
                for ic in range(IC):
                    gate_up_low(e + 1, ic)
            down_low(NE - 1)


def kernel(x, ctx_1024, mask_BxS2_bf1, g_xattn, g_ffn, L0_xattn_Wq, L0_xattn_Wk, L0_xattn_Wv, L0_xattn_Wo,
           L0_xattn_gq, L0_xattn_gk, L0_ffn_weight, L0_ffn_scale, L1_xattn_Wq, L1_xattn_Wk, L1_xattn_Wv, L1_xattn_Wo,
           L1_ffn_Wq, L1_ffn_Wk, L1_ffn_Wv, L1_ffn_Wo, L1_ffn_w_ln1, L1_ffn_w_ln2, L1_ffn_Wr, L1_ffn_Wg, L1_ffn_Wu,
           L1_ffn_Wd):
    import ml_dtypes
    import numpy as np
    import concourse.bacc as bacc
    from concourse import mybir as mb
    from concourse.bass_utils import run_bass_kernel_spmd

    def arr(v):
        return np.asarray(v)

    def rows(w, chunks):
        return arr(w).reshape(chunks, 128, -1).transpose(1, 0, 2)

    def inner_first(w, heads):
        return arr(w).reshape(arr(w).shape[0], heads, 128).transpose(2, 1, 0)

    x2 = arr(x).reshape(1024, 256)
    c2 = arr(ctx_1024).reshape(1024, 128)
    gu = np.stack([arr(L1_ffn_Wg), arr(L1_ffn_Wu)])
    gu = gu.reshape(2, 8, 4, 128, 2, 128).transpose(1, 5, 2, 0, 4, 3)
    dn = arr(L1_ffn_Wd).transpose(0, 2, 1).reshape(8, 4, 128, 256).transpose(0, 2, 1, 3)
    wattn = np.stack([arr(w).T.reshape(2, 128, 256) for w in (L1_ffn_Wq, L1_ffn_Wk, L1_ffn_Wv, L1_ffn_Wo)])
    key, q = np.arange(64)[None, :], np.arange(128)[:, None] % 64
    data = {
        "x": x2, "ctx": c2, "ctxT": c2.T, "mask": arr(mask_BxS2_bf1).reshape(-1).view(np.uint8),
        "gates": np.concatenate([arr(g_xattn), arr(g_ffn)]),
        "gqk": np.stack([arr(L0_xattn_gq), arr(L0_xattn_gk)], axis=1),
        "wq0": rows(L0_xattn_Wq, 2).reshape(128, 2, 8, 256).transpose(0, 2, 1, 3).reshape(128, 4096),
        "wk0": arr(L0_xattn_Wk), "wv0T": inner_first(L0_xattn_Wv, 16).reshape(128, 2048),
        "wo0": rows(L0_xattn_Wo, 16).reshape(128, 4096),
        "wf": rows(L0_ffn_weight, 2).reshape(128, 512), "ffn_scale": arr(L0_ffn_scale),
        "wq1T": inner_first(L1_xattn_Wq, 16).reshape(128, 4096), "wk1T": inner_first(L1_xattn_Wk, 8).reshape(128, 1024),
        "wv1T": inner_first(L1_xattn_Wv, 8).reshape(128, 1024), "wo1": rows(L1_xattn_Wo, 16).reshape(128, 4096),
        "wattn": wattn.transpose(2, 0, 1, 3).reshape(128, 2048),
        "w_ln": np.stack([arr(L1_ffn_w_ln1), arr(L1_ffn_w_ln2)]).reshape(2, 2, 128).transpose(2, 0, 1),
        "wr": arr(L1_ffn_Wr).T.reshape(2, 128, 8).transpose(1, 0, 2),
        "gu": gu.reshape(8, 128, 2048),
        "dn": dn.reshape(8, 128, 1024),
        "c_ident": np.eye(128, dtype=np.float32),
        "c_swap": np.roll(np.eye(128, dtype=np.float32), 64, axis=1),
        "c_causal": np.where(key <= q, 0.0, -1e30).astype(ml_dtypes.bfloat16),
        "c_ident_b": np.eye(128, dtype=ml_dtypes.bfloat16),
        "c_heads": (np.arange(128)[:, None] // 16 == np.arange(8)[None, :]).astype(np.float32),
        "c_iota": np.tile(np.arange(8, dtype=np.float32), (128, 1)),
    }
    nc = bacc.Bacc("TRN2", target_bir_lowering=False, num_devices=1)
    arrays, aps = {}, {}
    for name, v in data.items():
        v = np.ascontiguousarray(v)
        arrays["in_" + name] = v
        aps[name] = nc.dram_tensor("in_" + name, v.shape, mb.dt.from_np(v.dtype), kind="ExternalInput").ap()
    aps["out"] = nc.dram_tensor("out_x", (1024, 256), mb.dt.float32, kind="ExternalOutput").ap()
    build(nc, aps)
    r = run_bass_kernel_spmd(nc, [arrays], core_ids=[0])
    return r.results[0]["out_x"].reshape(16, 64, 256)
```

```python
from contextlib import ExitStack

import concourse.bass as bass
from concourse import mybir

F32 = mybir.dt.float32
F32R = mybir.dt.float32r
BF16 = mybir.dt.bfloat16
I32 = mybir.dt.int32
U32 = mybir.dt.uint32
U8 = mybir.dt.uint8
ALU = mybir.AluOpType
ACT = mybir.ActivationFunctionType
AX = mybir.AxisListType

P = 128
NB, SQ, DM = 16, 64, 256
CD, HD = 128, 128
NH, NKV = 16, 8
NT = NB * SQ // P
KC = DM // P
HALF = NB * SQ // 2
PAIRS = NH // 2
UNITS = 2 * PAIRS
NE, INTER = 8, 512
IC = INTER // P
AH, AD = 16, 16
BANK = 512
BIG = 1e30
EPS = 1e-5
SMALL = 9 * 16


def build(nc, a):
    with ExitStack() as ctx:
        def sb(name, shape, dt=F32):
            return ctx.enter_context(nc.sbuf_tensor(name, shape, dt))

        def sem(name):
            return ctx.enter_context(nc.semaphore(name))

        x_res = sb("x_res", [P, NT, DM])
        ctxT = sb("ctxT", [P, NB * SQ])
        ctx_tok = sb("ctx_tok", [P, NT, CD])
        reg_a = sb("reg_a", [P, 4096])
        reg_b = sb("reg_b", [P, 2048])
        reg_c = sb("reg_c", [P, 6144])
        reg_d = sb("reg_d", [P, 4096])
        reg_e = sb("reg_e", [P, 4096])
        norm_buf = sb("norm_buf", [P, NT, DM])
        qT = sb("qT", [P, 2048])
        kT = sb("kT", [P, 2048])
        probs = sb("probs", [P, NB, SQ])
        probsT = sb("probsT", [P, 4, 2, P])
        ident = sb("ident", [P, P])
        swap = sb("swap", [P, P])
        causal = sb("causal", [P, SQ], BF16)
        ident_b = sb("ident_b", [P, P], BF16)
        head_mask = sb("head_mask", [P, 8])
        mask_add = sb("mask_add", [P, NB, SQ], BF16)
        mask_any = sb("mask_any", [P, NB])
        gates = sb("gates", [P, 4])
        tgates = sb("tgates", [P, 4])
        gq_gk = sb("gq_gk", [P, 2])
        gqk = sb("gqk", [P, 1])
        ffn_scale = sb("ffn_scale", [P, DM])
        w_ln = sb("w_ln", [P, 2, KC])
        bn6 = sb("bn6", [P, NT, 6])
        mean_var = sb("mean_var", [P, NT, 2])
        var_eps = sb("var_eps", [P, NT])
        rstd = sb("rstd", [P, NT])
        rms_var, rms_rstd = sb("rms_var", [P, NT]), sb("rms_rstd", [P, NT])
        neg_half = sb("neg_half", [P, 8])
        eps8 = sb("eps8", [P, 8])
        pos_half = sb("pos_half", [P, 8])
        sumsq = sb("sumsq", [P, 4, 4])
        sumsq_eps = sb("sumsq_eps", [P, 4, 4])
        rnorm = sb("rnorm", [P, 4, 4])
        smax = sb("smax", [P, 2, 8])
        ssum = sb("ssum", [P, 2, 8])
        srec = sb("srec", [P, 2, 8])
        row_max, row_sum, row_rec = (sb(n, [P, 2, AH]) for n in ("row_max", "row_sum", "row_rec"))
        iota8 = sb("iota8", [P, NE])
        logits = sb("logits", [P, NT, NE])
        top8 = sb("top8", [P, NT, 8])
        top8_at = sb("top8_at", [P, NT, 8], U32)
        top_at = sb("top_at", [P, NT, 2])
        chosen = ffn_scale[:, 0:2 * NE * NT].rearrange("p (j e t) -> p j e t", j=2, e=NE)
        cw = sb("cw", [P, NE * NT])
        cw_now = sb("cw_now", [P, NT])
        wr_raw = sb("wr_raw", [P, KC, NE])
        tiny = sb("tiny", [P, 12, NT])

        xT_h = sb("xT_h", [P, KC, NB * SQ], F32R)
        xT_l = sb("xT_l", [P, KC, NB * SQ], F32R)
        w_r = sb("w_r", [P, 6144], F32R)
        wr_r = sb("wr_r", [P, 2, KC, NE], F32R)
        wr_h, wr_l = wr_r[:, 0, :, :], wr_r[:, 1, :, :]
        act_r = sb("act_r", [P, 8192], F32R)

        wq_raw = reg_a[:, :]
        wk_raw = reg_b[:, :]
        wf_raw = reg_b[:, 0:512]
        wo_raw = reg_c[:, 0:4096]
        wv_raw = reg_c[:, 4096:6144]
        wk1T = reg_c[:, 4096:5120]
        wv1T = reg_c[:, 5120:6144]
        vo0, m1, vo1 = reg_d, reg_d, reg_e
        nb_flat = norm_buf[:, :, :].rearrange("p t d -> p (t d)")
        squares = reg_e[:, 1024:2048].rearrange("p (s g d) -> p s g d", s=2, g=4)
        raw = nb_flat.rearrange("p (s g d) -> p s g d", s=4, g=4)
        qT_v = qT[:, :].rearrange("p (t b h q) -> p t b h q", t=NT, b=2, h=2)
        kT_v = kT[:, :].rearrange("p (t b h q) -> p t b h q", t=NT, b=2, h=2)
        wq_h, wq_l = w_r[:, 0:512].rearrange("p (k n) -> p k n", k=KC), w_r[:, 512:1024].rearrange("p (k n) -> p k n", k=KC)
        wk_h, wk_l = w_r[:, 1024:1280], w_r[:, 1280:1536]
        vo_h, vo_l = w_r[:, 1536:2048].rearrange("p (h n) -> p h n", h=2), w_r[:, 2048:2560].rearrange("p (h n) -> p h n", h=2)
        ctxT_h, ctxT_l = w_r[:, 2560:3584], w_r[:, 3584:4608]
        wf_h, wf_l = w_r[:, 4608:5120].rearrange("p (k n) -> p k n", k=KC), w_r[:, 5120:5632].rearrange("p (k n) -> p k n", k=KC)
        ac_h = act_r[:, 0:2048].rearrange("p (h t n) -> p h t n", h=2, t=NT)
        ac_l = act_r[:, 2048:4096].rearrange("p (h t n) -> p h t n", h=2, t=NT)

        mask_u8 = reg_e[:, 0:256].bitcast(U8)
        x1 = reg_a[:, 0:2048].rearrange("p (t d) -> p t d", t=NT)
        attn_raw = reg_a[:, 2048:4096]
        gu_raw, dn_raw = reg_c[:, 0:2048], reg_c[:, 2048:3072]
        silu_buf = qT[:, 0:1024].rearrange("p (s n) -> p s n", s=2)
        prod_buf = reg_b[:, :].rearrange("p (s n) -> p s n", s=IC)
        nb = norm_buf
        qT2 = qT[:, :].rearrange("p (k n) -> p k n", k=KC)
        kT2 = kT[:, :].rearrange("p (k n) -> p k n", k=KC)
        kexp = reg_e[:, :].rearrange("p (s b k n) -> p s b k n", s=2, b=2, k=KC)
        vexp = reg_d[:, :].rearrange("p (b n) -> p b n", b=NB)
        vexp_v = reg_d[:, :].rearrange("p (b g r d) -> p b g r d", b=NB, g=8, r=2)
        v_sb = reg_c[:, 3072:5120].rearrange("p (t n) -> p t n", t=NT)
        probs2 = reg_b[:, :].rearrange("p (s n) -> p s n", s=2)
        pt2 = [probs[:, :, :].rearrange("p b k -> p (b k)"), probsT[:, :, :, :].rearrange("p j b n -> p (j b n)")]
        aw = act_r[:, 4096:8192].rearrange("p (w s n) -> p w s n", w=4, s=2)
        aw_h = aw[:, :, 0, :].rearrange("p w (k n) -> p w k n", k=KC)
        aw_l = aw[:, :, 1, :].rearrange("p w (k n) -> p w k n", k=KC)
        hT_h = act_r[:, 0:2048].rearrange("p (t k n) -> p t k n", t=NT, k=KC)
        hT_l = act_r[:, 2048:4096].rearrange("p (t k n) -> p t k n", t=NT, k=KC)
        gu_h = w_r[:, 0:2048].rearrange("p (i m k n) -> p i m k n", i=IC, m=2, k=KC)
        gu_l = w_r[:, 2048:4096].rearrange("p (i m k n) -> p i m k n", i=IC, m=2, k=KC)
        dn_h = w_r[:, 4096:5120].rearrange("p (i n) -> p i n", i=IC)
        dn_l = w_r[:, 5120:6144].rearrange("p (i n) -> p i n", i=IC)
        hx_h = act_r[:, 0:4096].rearrange("p (s i n) -> p s i n", s=2, i=IC)
        hx_l = act_r[:, 4096:8192].rearrange("p (s i n) -> p s i n", s=2, i=IC)

        psum = [ctx.enter_context(nc.psum_tensor(f"bank{i}", [P, BANK], F32)) for i in range(8)]
        Y = psum[0:4]
        R = psum[4:8]

        def y_tile(t):
            return Y[t // 2][:, DM * (t % 2):DM * (t % 2 + 1)]

        def f(ap):
            return ap.bitcast(F32)

        ld = {n: sem("ld_" + n) for n in (
            "x0", "x1", "ident", "ctx", "ctx_tok", "gqk", "small", "wq0", "wk0", "wv0", "wo0", "wq0_rest", "wk0_rest", "wf",
            "wq1", "wk1", "wv1", "wo1", "attn", "wr", "gu", "dn")}
        stored = sem("stored")
        S = {n: sem(n) for n in (
            "stats", "var_eps", "rstd", "normed", "rms_var", "rms_rstd",
            "xT_mm", "xT_high", "xT_low",
            "halves", "zeroed", "gates", "gqk", "mask_add", "mask_any", "ctx_high", "ctx_low",
            "vo0_mm", "vo0", "m1_mm", "m1", "vo1_mm", "vo1",
            "wf_high", "wf_low", "wf_scaled", "ffn_mm", "ffn_sumsq", "ffn_len0", "ffn_len", "ffn_tanh",
            "aw_high", "aw_low", "qk2_mm", "q2", "k2", "v2_mm", "v2", "vs_mm", "vs_a", "vs_v",
            "kexp_v", "kexp_p", "s2_mm", "s2_row_max", "s2_sub", "s2_exp", "s2_rec", "x1", "pt2_mm", "pt2",
            "av2_mm", "h2", "hT_mm", "hT_high", "hT_low", "wo2_mm", "x2",
            "wr_high", "wr_low", "route_mm", "top_gap", "top_exp",
            "gu_high", "gu_low", "dn_high", "dn_low", "gu_mm", "silu", "prod", "act_high", "act_low", "y_mm", "y_added",
            "cw_now", "out_ready", "dve_step", "pool_step")}
        LAYER = ("wk_low", "proj", "squares", "sumsq", "sumsq_eps", "rnorm", "scaled", "qk_mm", "qk",
                 "scores", "masked", "smax", "sub", "exp", "ssum", "srec0", "srec", "prob",
                 "pt_mm", "pt_a", "pt_v", "av_mm", "ac_high", "ac_low", "o_mm", "w_high", "w_low", "vo_high", "vo_low")
        L0 = {k: sem("a0_" + k) for k in LAYER}
        L1 = {k: sem("a1_" + k) for k in LAYER if k not in ("wk_low", "squares", "sumsq", "sumsq_eps", "rnorm", "scaled", "qk_mm")}

        class Chain:
            def __init__(self, eng, s):
                self.eng, self.s, self.n = eng, s, 0

            def __call__(self, ins):
                ins.then_inc(self.s, 1)
                self.n += 1
                self.eng.wait_ge(self.s, self.n)

        def v_parts(bank):
            return bank[:, :].rearrange("p (t g r d) -> p t g r d", t=2, g=8, r=2)

        def xT_half(part, k, hf):
            return part[:, k, HALF * hf:HALF * (hf + 1)]

        block = ctx.enter_context(nc.Block())

        @block.sync
        def _(sp):
            def load(name, dst, src):
                sp.dma_start(dst, src).then_inc(ld[name], 16)

            xv = a["x"].rearrange("(t p) d -> p t d", p=P)
            load("x0", x_res[:, 0:4, :], xv[:, 0:4, :])
            load("x1", x_res[:, 4:8, :], xv[:, 4:8, :])
            load("ident", ident[:, :], a["c_ident"])
            load("wq0", wq_raw[:, 0:1024], a["wq0"][:, 0:1024])
            load("wk0", wk_raw[:, 0:512], a["wk0"][:, 0:512])
            load("wv0", wv_raw, a["wv0T"])
            load("wo0", wo_raw, a["wo0"])
            load("wq0_rest", wq_raw[:, 1024:4096], a["wq0"][:, 1024:4096])
            load("wk0_rest", wk_raw[:, 512:2048], a["wk0"][:, 512:2048])
            for dst, src in ((gates[:, :], a["gates"].unsqueeze(0).broadcast_to([P, 4])),
                             (causal[:, :], a["c_causal"]),
                             (ident_b[:, :], a["c_ident_b"]), (head_mask[:, :], a["c_heads"]),
                             (iota8[:, :], a["c_iota"]), (swap[:, :], a["c_swap"]), (w_ln[:, :, :], a["w_ln"]),
                             (ffn_scale[:, :], a["ffn_scale"].unsqueeze(0).broadcast_to([P, DM])),
                             (mask_u8[:, :], a["mask"].unsqueeze(0).broadcast_to([P, NB * SQ]))):
                load("small", dst, src)
            load("wr", wr_raw[:, :, :], a["wr"])
            sp.wait_ge(S["vo0_mm"], 8)
            load("wo1", wo_raw, a["wo1"])
            load("wk1", wk1T, a["wk1T"])
            load("wv1", wv1T, a["wv1T"])
            sp.wait_ge(L0["w_low"], PAIRS)
            load("wq1", wq_raw, a["wq1T"])
            load("wf", wf_raw, a["wf"])
            sp.wait_ge(S["m1_mm"], 8)
            load("attn", attn_raw, a["wattn"])
            sp.wait_ge(S["vo1_mm"], 8)
            load("gu", gu_raw, a["gu"][0])
            load("dn", dn_raw, a["dn"][0])
            with sp.Fori(1, NE) as e:
                sp.wait_ge(S["gu_low"], e * IC)
                load("gu", gu_raw, a["gu"][bass.ds(e, 1)].rearrange("e p n -> (e p) n"))
                sp.wait_ge(S["dn_low"], e)
                load("dn", dn_raw, a["dn"][bass.ds(e, 1)].rearrange("e p n -> (e p) n"))
            ov = a["out"].rearrange("(t p) d -> p t d", p=P)
            for g in range(NT // 2):
                sp.wait_ge(S["out_ready"], g + 1)
                sp.dma_start(ov[:, 2 * g:2 * g + 2, :], norm_buf[:, 2 * g:2 * g + 2, :]).then_inc(stored, 16)
            sp.wait_ge(stored, 16 * NT // 2)

        class Unit:
            def __init__(self, i, c):
                self.i, self.c = i, c

            def at(self, off):
                return Unit(self.i, self.c + off)

            def there(self):
                return not isinstance(self.i, int) or 0 <= 2 * self.i + self.c < UNITS

            def count(self, per, k):
                return self.i * (2 * per) + (self.c * per + k)

            def after_zero(self, per, k):
                return not isinstance(self.i, int) or self.count(per, k) > 0

            def half(self):
                return self.c % 2

            def first(self):
                return isinstance(self.i, int) and 2 * self.i + self.c in (0, 1)

        def step_is(n, k):
            return isinstance(n.i, int) and 2 * n.i + n.c == k

        def pair_there(j):
            return not isinstance(j, int) or 0 <= j < PAIRS

        def aw_part(n):
            part = {2: 0, 3: 1}.get(2 * n.i + n.c) if isinstance(n.i, int) else None
            if part is None:
                return None
            w = slice(2 * part, 2 * part + 2)
            return part, aw[:, w, 0, :], aw[:, w, 1, :], attn_raw.rearrange("p (w n) -> p w n", w=4)[:, w, :]

        def vo_turn(n, j):
            g = 3 * (2 * n.i + n.c + 2) + j if isinstance(n.i, int) else -1
            return g if j < 3 and 0 <= g < PAIRS else None

        def pipeline(eng, step, lead):
            if lead == 3:
                step(Unit(-2, 1))
            for i in (-1, 0, 1):
                for c in (0, 1):
                    step(Unit(i, c))
            with eng.Fori(2, PAIRS - 2) as i:
                for c in (0, 1):
                    step(Unit(i, c))
            for i in (PAIRS - 2, PAIRS - 1, PAIRS):
                for c in (0, 1):
                    step(Unit(i, c))

        @block.tensor
        def _(pe):
            def split_mm(out, lh, ll, rh, rl, start, stop):
                pe.matmul(out, lh, rh, start=start, stop=False, skip_group_check=True)
                pe.matmul(out, lh, rl, start=False, stop=False, skip_group_check=True)
                return pe.matmul(out, ll, rh, start=False, stop=stop, skip_group_check=True)

            def x_transposes(norm, halves=(0, 1), banks=R):
                for hf in halves:
                    for k in range(KC):
                        for t in range(4):
                            pe.wait_ge(S["normed"], 8 * norm + 4 * hf + t + 1)
                            ins = pe.transpose(banks[2 * hf + k][:, P * t:P * (t + 1)],
                                               nb[:, 4 * hf + t, P * k:P * (k + 1)], ident[:, :])
                        ins.then_inc(S["xT_mm"], 1)

            pe.wait_ge(ld["ident"], 16)
            x_transposes(0)

            def probs_T(L, n, bank):
                pe.wait_ge(L["prob"], n.count(1, 1))
                for j in range(4):
                    b = 8 * n.half() + 2 * j
                    ins = pe.transpose(bank[:, P * j:P * (j + 1)],
                                       probs[:, b:b + 2, :].rearrange("p b k -> p (b k)"), ident[:, :])
                ins.then_inc(L["pt_mm"], 1)

            def attend(L, n, part, bank):
                pe.wait_ge(L["pt_a"], n.count(1, 1))
                pe.wait_ge(L["pt_v"], n.count(1, 1))
                for jj in range(2):
                    j = 2 * part + jj
                    ins = pe.matmul(bank[:, 256 * jj:256 * (jj + 1)], ctx_tok[:, 4 * n.half() + j, :],
                                    probsT[:, j, :, :].rearrange("p b (h q) -> p h b q", h=2), start=True, stop=True)
                ins.then_inc(L["av_mm"], 1)

            def project_out(L, n, tiles):
                pe.wait_ge(L["ac_low"], n.count(2, 2))
                pe.wait_ge(L["vo_low"], n.i + (n.c // 2 + 1))
                for j in tiles:
                    t = 4 * n.half() + j
                    for hh in range(2):
                        ins = split_mm(y_tile(t), ac_h[:, hh, t, :], ac_l[:, hh, t, :], vo_h[:, hh, :], vo_l[:, hh, :],
                                       start=n.first() and t % 2 == 0 and hh == 0, stop=False)
                if tiles[-1] == 3:
                    ins.then_inc(L["o_mm"], 1)

            def project_qk(u, j, bank):
                t = 4 * u.half() + j
                if j == 0:
                    pe.wait_ge(L0["w_low"], u.i + (u.c // 2 + 1))
                    pe.wait_ge(L0["wk_low"], u.i + (u.c // 2 + 1))
                for k in range(KC):
                    split_mm(bank[:, 0:256], xT_h[:, k, P * t:P * (t + 1)], xT_l[:, k, P * t:P * (t + 1)],
                             wq_h[:, k, :], wq_l[:, k, :], k == 0, k == KC - 1)
                split_mm(bank[:, 256:512], ctxT_h[:, P * t:P * (t + 1)], ctxT_l[:, P * t:P * (t + 1)],
                         wk_h, wk_l, True, True).then_inc(L0["proj"], 1)

            def qk_T(u, j, bank):
                pe.wait_ge(L0["scaled"], u.count(4, j + 1))
                for g in range(4):
                    ins = pe.transpose(bank[:, P * g:P * (g + 1)], raw[:, j, g, :], ident[:, :])
                ins.then_inc(L0["qk_mm"], 1)

            def vo_product(n, j):
                g = vo_turn(n, j)
                if g is not None:
                    if g == 0:
                        pe.wait_ge(ld["wv0"], 16)
                        pe.wait_ge(ld["wo0"], 16)
                    if g >= 4:
                        pe.wait_ge(S["vo0"], g - 3)
                    for hh in range(2):
                        h = 2 * g + hh
                        ins = pe.matmul(Y[g % 4][:, DM * hh:DM * (hh + 1)], wv_raw[:, CD * h:CD * (h + 1)],
                                        wo_raw[:, DM * h:DM * (h + 1)], start=True, stop=True)
                    ins.then_inc(S["vo0_mm"], 1)

            def step0(n):
                u1, u2, u3, um, um2 = n.at(1), n.at(2), n.at(3), n.at(-1), n.at(-2)
                if u1.there():
                    pe.wait_ge(L0["qk"], u1.count(4, 4))
                    for j in range(4):
                        for b in range(2):
                            for hh in range(2):
                                t = 4 * u1.half() + j
                                ins = pe.matmul(R[0][64 * hh:64 * (hh + 1), 64 * (2 * j + b):64 * (2 * j + b + 1)],
                                                qT_v[:, t, b, hh, :], kT_v[:, t, b, hh, :], start=True, stop=True)
                    ins.then_inc(L0["scores"], 1)
                if u2.there():
                    if um.there():
                        pe.wait_ge(L0["ac_low"], um.count(2, 2))
                    qk_T(u2, 0, R[1])
                    pe.wait_ge(L0["squares"], u2.count(4, 3))
                    qk_T(u2, 1, R[2])
                    pe.wait_ge(L0["squares"], u2.count(4, 4))
                if n.there():
                    probs_T(L0, n, R[3])
                if um2.there():
                    project_out(L0, um2, (3,))
                if u3.there():
                    if u1.there():
                        pe.wait_ge(L0["sub"], u1.count(1, 1))
                    project_qk(u3, 0, R[0])
                    vo_product(n, 0)
                if n.there():
                    if u2.there():
                        pe.wait_ge(L0["qk"], u2.count(4, 2))
                    elif um.there():
                        pe.wait_ge(L0["ac_low"], um.count(2, 2))
                    attend(L0, n, 0, R[2])
                if u2.there():
                    pe.wait_ge(L0["qk"], u2.count(4, 1))
                    qk_T(u2, 2, R[1])
                if u3.there():
                    if n.there():
                        pe.wait_ge(L0["pt_v"], n.count(1, 1))
                    if step_is(n, -3):
                        pe.wait_ge(S["xT_low"], 4)
                    project_qk(u3, 1, R[3])
                    vo_product(n, 1)
                if u2.there():
                    if u3.there():
                        pe.wait_ge(L0["squares"], u3.count(4, 1))
                    else:
                        pe.wait_ge(L0["sub"], u1.count(1, 1))
                    qk_T(u2, 3, R[0])
                if um.there():
                    project_out(L0, um, (0,))
                if n.there():
                    if u2.there():
                        pe.wait_ge(L0["qk"], u2.count(4, 3))
                    attend(L0, n, 1, R[1])
                if um.there():
                    project_out(L0, um, (1,))
                if u3.there():
                    if n.there():
                        pe.wait_ge(L0["ac_low"], n.count(2, 1))
                    project_qk(u3, 2, R[2])
                    vo_product(n, 2)
                if um.there():
                    project_out(L0, um, (2,))
                if u3.there():
                    pe.wait_ge(L0["squares"], u3.count(4, 2))
                    project_qk(u3, 3, R[3])

            pe.wait_ge(S["xT_low"], 2)
            pe.wait_ge(S["ctx_low"], 1)
            pe.wait_ge(ld["ctx_tok"], 16)
            pipeline(pe, step0, 3)

            pe.wait_ge(ld["wq1"], 16)
            pe.wait_ge(ld["wk1"], 16)
            def m1_product(g):
                for k in range(KC):
                    for hh in range(2):
                        o = P * (2 * k + hh)
                        w = DM * (2 * g + hh) + P * k
                        ins = pe.matmul(R[g % 4][:, o:o + P], wq_raw[:, w:w + P], wk1T[:, CD * g:CD * (g + 1)],
                                        start=True, stop=True)
                ins.then_inc(S["m1_mm"], 1)

            for g in range(4):
                m1_product(g)
            pe.wait_ge(S["m1"], 4)
            x_transposes(1, (0,))
            pe.wait_ge(S["wf_low"], 1)
            for t in range(NT):
                if t == 2:
                    x_transposes(1, (1,))
                if t % 4 == 0:
                    pe.wait_ge(S["xT_low"], 4 + 2 * (t // 4) + 2)
                for k in range(KC):
                    ins = split_mm(y_tile(t), xT_h[:, k, P * t:P * (t + 1)], xT_l[:, k, P * t:P * (t + 1)],
                                   wf_h[:, k, :], wf_l[:, k, :], k == 0, k == KC - 1)
                ins.then_inc(S["ffn_mm"], 1)
            for g in range(4, PAIRS):
                m1_product(g)
            pe.wait_ge(ld["wv1"], 16)
            pe.wait_ge(ld["wo1"], 16)
            for g in range(PAIRS):
                pe.wait_ge(*((S["m1"], g + 5) if g < 4 else (S["vo1"], g - 3)))
                for hh in range(2):
                    h = 2 * g + hh
                    ins = pe.matmul(R[g % 4][:, DM * hh:DM * (hh + 1)], wv1T[:, CD * g:CD * (g + 1)],
                                    wo_raw[:, DM * h:DM * (h + 1)], start=True, stop=True)
                ins.then_inc(S["vo1_mm"], 1)

            pe.wait_ge(S["vo1"], PAIRS)
            x_transposes(2, (0,))

            def project_t(u, hh, bank):
                if hh == 0:
                    pe.wait_ge(L1["w_low"], u.i + (u.c // 2 + 1))
                for k in range(KC):
                    ins = split_mm(bank[:, :], wq_h[:, k, P * hh:P * (hh + 1)], wq_l[:, k, P * hh:P * (hh + 1)],
                                   xT_half(xT_h, k, u.half()), xT_half(xT_l, k, u.half()), k == 0, k == KC - 1)
                ins.then_inc(L1["proj"], 1)

            def step1(n):
                u1, u2, um = n.at(1), n.at(2), n.at(-1)
                B = [R[(2 * n.half() + k) % 4] for k in range(4)]
                if u1.there():
                    pe.wait_ge(L1["qk"], u1.count(2, 2))
                    for j in range(4):
                        for b in range(2):
                            t = 4 * u1.half() + j
                            ins = pe.matmul(B[0][:, 64 * (2 * j + b):64 * (2 * j + b + 1)],
                                            qT_v[:, t, b, :, :].rearrange("p h q -> p (h q)"),
                                            ctxT[:, SQ * (2 * t + b):SQ * (2 * t + b + 1)], start=True, stop=True)
                    ins.then_inc(L1["scores"], 1)
                if u2.there():
                    project_t(u2, 0, B[1])
                if n.there():
                    if um.there():
                        pe.wait_ge(L1["ac_low"], um.count(2, 1))
                    probs_T(L1, n, B[2])
                if um.there():
                    project_out(L1, um, (0, 1))
                if u2.there():
                    if step_is(n, -2):
                        x_transposes(2, (1,))
                        pe.wait_ge(S["xT_low"], 12)
                    project_t(u2, 1, B[3])
                if n.there():
                    if u1.there():
                        pe.wait_ge(L1["masked"], u1.count(1, 1))
                    attend(L1, n, 0, B[0])
                    if u2.there():
                        pe.wait_ge(L1["qk"], u2.count(2, 1))
                    attend(L1, n, 1, B[1])
                if um.there():
                    project_out(L1, um, (2, 3))

            pe.wait_ge(S["xT_low"], 10)
            pipeline(pe, step1, 2)

            x_transposes(3, (0,))
            pe.wait_ge(S["aw_low"], 2)
            for hf in range(2):
                pe.wait_ge(S["xT_low"], 12 + 2 * hf + 2)
                for w in range(2):
                    if hf == 0 and w == 1:
                        x_transposes(3, (1,))
                    for oc in range(KC):
                        bank = (Y, R)[hf][2 * w + oc]
                        for k in range(KC):
                            ins = split_mm(bank[:, :], aw_h[:, w, k, P * oc:P * (oc + 1)],
                                           aw_l[:, w, k, P * oc:P * (oc + 1)],
                                           xT_half(xT_h, k, hf), xT_half(xT_l, k, hf), k == 0, k == KC - 1)
                        ins.then_inc(S["qk2_mm"], 1)

            def self_scores(t):
                pe.wait_ge(S["kexp_v"], min(t + 1, 3))
                pe.wait_ge(S["kexp_p"], t + 1)
                pe.wait_ge(S["q2"], 2 * (t // 4) + 2)
                if t >= 2:
                    pe.wait_ge(S["s2_sub"], t - 1)
                for oc in range(KC):
                    bank = Y[2 * (t % 2) + oc]
                    pe.matmul(bank[:, :], ident_b[:, :], causal[:, :].unsqueeze(1).broadcast_to([P, 8, SQ]),
                              start=True, stop=False, skip_group_check=True)
                    for b in range(2):
                        c = SQ * (2 * t + b)
                        ins = pe.matmul(bank[64 * b:64 * (b + 1), :], qT2[:, oc, c:c + SQ],
                                        kexp[:, t % 2, b, oc, :], start=False, stop=True, skip_group_check=True)
                ins.then_inc(S["s2_mm"], 1)

            pe.wait_ge(ld["small"], SMALL)
            self_scores(0)
            for g in range(4):
                pe.wait_ge(*((S["q2"], 3 + g) if g < 2 else (S["k2"], 1 + g)))
                for tt in range(2):
                    c = P * (2 * g + tt)
                    for k in range(KC):
                        ins = split_mm(R[g][:, DM * tt:DM * (tt + 1)], xT_h[:, k, c:c + P], xT_l[:, k, c:c + P],
                                       aw_h[:, 2, k, :], aw_l[:, 2, k, :], k == 0, k == KC - 1)
                ins.then_inc(S["v2_mm"], 1)
                if g == 1:
                    self_scores(1)
            for g in range(4):
                pe.wait_ge(S["v2"], g + 1)
                pe.matmul(R[g][:, :], swap[:, :], v_sb[:, 2 * g:2 * g + 2, :].rearrange("p t n -> p (t n)"),
                          start=True, stop=True).then_inc(S["vs_mm"], 1)
            pe.wait_ge(S["vs_a"], 4)
            pe.wait_ge(S["vs_v"], 4)

            def gate_up(u, chunks=range(IC), between=None):
                for ic in chunks:
                    pe.wait_ge(S["gu_low"], u.i * IC + (u.c // 2 * IC + ic + 1))
                    if u.after_zero(4, ic - 1):
                        pe.wait_ge(S["prod"], u.count(4, ic - 1))
                    for m in range(2):
                        for k in range(KC):
                            ins = split_mm(R[2 * (ic % 2) + m][:, :], gu_h[:, ic, m, k, :], gu_l[:, ic, m, k, :],
                                           xT_half(xT_h, k, u.half()), xT_half(xT_l, k, u.half()), k == 0, k == KC - 1)
                        ins.then_inc(S["gu_mm"], 1)
                        if between and m == 0:
                            between()

            def self_out(t):
                pe.wait_ge(S["h2"], t + 1)
                if t >= 1:
                    pe.wait_ge(S["x2"], t)
                for k in range(KC):
                    ins = pe.transpose(R[3][:, P * k:P * (k + 1)], nb[:, t, P * k:P * (k + 1)], ident[:, :])
                ins.then_inc(S["hT_mm"], 1)

            def self_proj(t):
                pe.wait_ge(S["hT_low"], t + 1)
                for k in range(KC):
                    ins = split_mm(R[3][:, DM:2 * DM], hT_h[:, t, k, :], hT_l[:, t, k, :],
                                   aw_h[:, 3, k, :], aw_l[:, 3, k, :], k == 0, k == KC - 1)
                ins.then_inc(S["wo2_mm"], 1)

            for t in range(NT + 1):
                if t < NT:
                    pe.wait_ge(S["s2_exp"], t + 1)
                    if t >= 1:
                        pe.wait_ge(S["pt2"], t)
                    for g in range(8):
                        ins = pe.transpose(R[g // 4][:, P * (g % 4):P * (g % 4 + 1)],
                                           probs2[:, t % 2, P * g:P * (g + 1)], ident[:, :])
                    ins.then_inc(S["pt2_mm"], 1)
                if 1 <= t < NT:
                    self_out(t - 1)
                if t + 2 < NT:
                    self_scores(t + 2)
                if t < NT:
                    pe.wait_ge(S["pt2"], t + 1)
                    for b in range(2):
                        for g in range(8):
                            ins = pe.matmul(R[2][64 * b:64 * (b + 1), 32 * g:32 * (g + 1)],
                                            pt2[t % 2][:, P * g + 64 * b:P * g + 64 * (b + 1)],
                                            vexp[:, 2 * t + b, 32 * g:32 * (g + 1)], start=True, stop=True)
                    ins.then_inc(S["av2_mm"], 1)
                if t == NT - 2:
                    pe.wait_ge(S["s2_sub"], NT - 1)
                    x_transposes(4, (0,), Y)
                if t >= 1:
                    self_proj(t - 1)
                if t == NT - 1:
                    pe.wait_ge(S["xT_low"], 18)
                    gate_up(Unit(0, 0), (0,), lambda: self_out(NT - 1))

            def down(u):
                pe.wait_ge(S["dn_low"], u.i + 1)
                pe.wait_ge(S["act_low"], u.count(4, 4))
                if u.after_zero(4, -4):
                    pe.wait_ge(S["y_added"], u.count(4, -4))
                for j in range(4):
                    t = 4 * u.half() + j
                    for ic in range(IC):
                        ins = split_mm(y_tile(t), hx_h[:, u.half(), ic, P * j:P * (j + 1)],
                                       hx_l[:, u.half(), ic, P * j:P * (j + 1)], dn_h[:, ic, :], dn_l[:, ic, :],
                                       ic == 0, ic == IC - 1)
                    ins.then_inc(S["y_mm"], 1)

            pe.wait_ge(S["x2"], NT)
            gate_up(Unit(0, 0), (1,))
            pe.wait_ge(S["s2_sub"], NT)
            gate_up(Unit(0, 0), (2,))
            x_transposes(4, (1,), Y)
            gate_up(Unit(0, 0), (3,))
            pe.wait_ge(S["xT_low"], 20)
            pe.wait_ge(S["wr_low"], 1)
            for t in range(NT):
                both = Y[3][:, 2 * NE * t:2 * NE * (t + 1)]
                for k in range(KC):
                    pe.matmul(both.rearrange("p (s e) -> p s e", s=2), xT_h[:, k, P * t:P * (t + 1)], wr_r[:, :, k, :],
                              start=k == 0, stop=False, skip_group_check=True)
                    ins = pe.matmul(both[:, 0:NE], xT_l[:, k, P * t:P * (t + 1)], wr_h[:, k, :],
                                    start=False, stop=k == KC - 1, skip_group_check=True)
            ins.then_inc(S["route_mm"], 1)
            gate_up(Unit(0, 1))
            pe.wait_ge(S["top_gap"], 1)
            down(Unit(0, 0))
            gate_up(Unit(1, 0))
            down(Unit(0, 1))
            with pe.Fori(1, NE - 1) as e:
                for c in range(2):
                    gate_up(Unit(e, c + 1))
                    down(Unit(e, c))
            gate_up(Unit(NE - 1, 1))
            down(Unit(NE - 1, 0))
            down(Unit(NE - 1, 1))

        @block.scalar
        def _(act):
            def copy(out, in_, scale=None):
                if scale is None:
                    return act.activation(out, in_, ACT.Copy)
                return act.activation(out, in_, ACT.Copy, scale=scale)

            def load(name, dst, src):
                act.dma_start(dst, src).then_inc(ld[name], 16)

            def x_high(turn, w=None, halves=(0, 1), banks=R):
                for hf in halves:
                    for k in range(KC):
                        act.wait_ge(S["xT_mm"], 4 * turn + 2 * hf + k + 1)
                        copy(xT_half(xT_h, k, hf), banks[2 * hf + k][:, :],
                             None if w is None else w_ln[:, w, k:k + 1]).then_inc(S["xT_high"], 1)

            load("ctx", ctxT[:, :], a["ctxT"])
            load("gqk", gq_gk[:, :], a["gqk"])
            load("ctx_tok", ctx_tok[:, :, :], a["ctx"].rearrange("(t p) c -> p t c", p=P))
            act.wait_ge(ld["ctx"], 16)
            copy(ctxT_h, ctxT[:, :]).then_inc(S["ctx_high"], 1)

            def vo_out(n, j):
                g = vo_turn(n, j)
                if g is not None:
                    act.wait_ge(S["vo0_mm"], g + 1)
                    copy(vo0[:, 512 * g:512 * (g + 1)], Y[g % 4][:, :]).then_inc(S["vo0"], 1)

            def vo_high(L, src, n):
                if n.c == 1 and pair_there(n.i):
                    if not isinstance(n.i, int) or n.i > 0:
                        act.wait_ge(L["o_mm"], n.i * 2)
                    copy(vo_h.rearrange("p h n -> p (h n)"), src[:, bass.ds(n.i * 512, 512)]).then_inc(L["vo_high"], 1)

            def split_exp(L, u1):
                act.wait_ge(L["sub"], u1.count(1, 1))
                p = probs[:, 8 * u1.half():8 * u1.half() + 8, :]
                act.activation(p, p, ACT.Exp, scale=float(HD) ** -0.5).then_inc(L["exp"], 1)

            def probs_T(L, n, bank):
                act.wait_ge(L["pt_mm"], n.count(1, 1))
                copy(probsT[0:64, :, 0, :], bank[0:64, :].rearrange("p (j n) -> p j n", j=4)).then_inc(L["pt_a"], 1)

            def attended(L, n, part, bank):
                act.wait_ge(L["av_mm"], n.count(2, part + 1))
                t = 4 * n.half() + 2 * part
                copy(ac_h[:, :, t:t + 2, :].rearrange("p h t n -> p t h n"),
                     bank[:, :].rearrange("p (t h n) -> p t h n", t=2, h=2)).then_inc(L["ac_high"], 1)

            def w_high0(j):
                if isinstance(j, int) and j == 0:
                    act.wait_ge(ld["wq0"], 16)
                    act.wait_ge(ld["wk0"], 16)
                if isinstance(j, int) and j == 2:
                    act.wait_ge(ld["wq0_rest"], 16)
                    act.wait_ge(ld["wk0_rest"], 16)
                copy(w_r[:, 0:512], wq_raw[:, bass.ds(j * 512, 512)])
                copy(wk_h, wk_raw[:, bass.ds(j * 256, 256)]).then_inc(L0["w_high"], 1)

            def step0(n):
                u1, u2, u3 = n.at(1), n.at(2), n.at(3)

                def take(j, bank):
                    act.wait_ge(L0["proj"], u3.count(4, j + 1))
                    copy(raw[:, j, :, :].rearrange("p g d -> p (g d)"), bank[:, :])
                    if u3.after_zero(4, j - 1):
                        act.wait_ge(L0["sumsq"], u3.count(4, j - 1))
                    act.activation(squares[:, j % 2, :, :].rearrange("p g d -> p (g d)"), bank[:, :],
                                   ACT.Square, scale=float(HD) ** -0.5).then_inc(L0["squares"], 1)

                def qk_out(j, bank):
                    act.wait_ge(L0["qk_mm"], u2.count(4, j + 1))
                    t = 4 * u2.half() + j
                    for g, dst, scale in ((0, qT_v, gqk[:, 0:1]), (1, kT_v, None)):
                        ins = copy(dst[:, t, :, :, :].rearrange("p b h q -> p h b q"),
                                   bank[:, 256 * g:256 * (g + 1)].rearrange("p (h b q) -> p h b q", h=2, b=2), scale)
                    ins.then_inc(L0["qk"], 1)

                if u2.there():
                    qk_out(0, R[1])
                    qk_out(1, R[2])
                if n.there():
                    probs_T(L0, n, R[3])
                if u1.there():
                    split_exp(L0, u1)
                if u3.there():
                    take(0, R[0])
                vo_out(n, 0)
                vo_high(L0, vo0, n)
                if n.there():
                    attended(L0, n, 0, R[2])
                if u2.there():
                    qk_out(2, R[1])
                if u3.there():
                    take(1, R[3])
                vo_out(n, 1)
                if u2.there():
                    qk_out(3, R[0])
                if n.there():
                    attended(L0, n, 1, R[1])
                if u3.there():
                    take(2, R[2])
                    vo_out(n, 2)
                    if n.c == 0 and pair_there(n.i + 2):
                        act.wait_ge(L0["proj"], u3.count(4, 4))
                        w_high0(n.i + 2)
                    take(3, R[3])
                if step_is(n, 3):
                    act.wait_ge(ld["small"], SMALL)
                    act.activation(tgates[:, :], gates[:, :], ACT.Tanh).then_inc(S["gates"], 1)

            x_high(0, halves=(0,))
            w_high0(0)
            x_high(0, halves=(1,))
            act.wait_ge(S["gqk"], 1)
            pipeline(act, step0, 3)

            act.wait_ge(S["wf_scaled"], 1)
            copy(w_r[:, 4608:5120], wf_raw).then_inc(S["wf_high"], 1)
            act.wait_ge(L0["vo_low"], PAIRS)
            def m1_out(g):
                act.wait_ge(S["m1_mm"], g + 1)
                copy(m1[:, 512 * g:512 * (g + 1)], R[g % 4][:, :]).then_inc(S["m1"], 1)

            def w_high1(j):
                copy(w_r[:, 0:512], m1[:, bass.ds(j * 512, 512)]).then_inc(L1["w_high"], 1)

            def ffn_tanh(hf):
                act.wait_ge(S["ffn_len"], hf + 1)
                act.activation(tiny[:, 2, 4 * hf:4 * hf + 4], tiny[:, 1, 4 * hf:4 * hf + 4],
                               ACT.Tanh).then_inc(S["ffn_tanh"], 1)

            for g in range(4):
                m1_out(g)
            x_high(1)
            for t in range(NT):
                act.wait_ge(S["ffn_mm"], t // 2 * 2 + 2)
                act.activation(qT[:, DM * t:DM * (t + 1)], y_tile(t), ACT.Square,
                               accum_out=tiny[:, 0, t:t + 1]).then_inc(S["ffn_sumsq"], 1)
                if t == 5:
                    ffn_tanh(0)
            for g in range(4, PAIRS):
                m1_out(g)
            w_high1(0)
            ffn_tanh(1)
            for g in range(PAIRS):
                act.wait_ge(S["vo1_mm"], g + 1)
                copy(vo1[:, 512 * g:512 * (g + 1)], R[g % 4][:, :]).then_inc(S["vo1"], 1)
            x_high(2)

            def step1(n):
                u1, u2, um = n.at(1), n.at(2), n.at(-1)
                B = [R[(2 * n.half() + k) % 4] for k in range(4)]
                vo_high(L1, vo1, n)

                def t_out(hh, bank):
                    act.wait_ge(L1["proj"], u2.count(2, hh + 1))
                    t = 4 * u2.half()
                    copy(qT_v[:, t:t + 4, :, hh, :].rearrange("p t b q -> p (t b) q"),
                         bank[:, :].rearrange("p (tb q) -> p tb q", q=SQ)).then_inc(L1["qk"], 1)

                if u2.there():
                    t_out(0, B[1])
                if u1.there():
                    split_exp(L1, u1)
                if n.there():
                    probs_T(L1, n, B[2])
                if u2.there():
                    t_out(1, B[3])
                if n.c == 1 and pair_there(n.i + 2):
                    act.wait_ge(L1["proj"], u2.count(2, 2))
                    w_high1(n.i + 2)
                if n.there():
                    attended(L1, n, 0, B[0])
                    attended(L1, n, 1, B[1])
                if aw_part(n):
                    part, high, _, raw_w = aw_part(n)
                    act.wait_ge(ld["attn"], 16)
                    copy(high, raw_w).then_inc(S["aw_high"], 1)

            act.wait_ge(S["vo1"], PAIRS)
            pipeline(act, step1, 2)

            x_high(3, 0)
            for hf in range(2):
                for oc in range(KC):
                    act.wait_ge(S["qk2_mm"], 4 * hf + oc + 1)
                    copy(qT2[:, oc, HALF * hf:HALF * (hf + 1)], (Y, R)[hf][oc][:, :]).then_inc(S["q2"], 1)

            def self_exp(t):
                act.wait_ge(S["s2_sub"], t + 1)
                act.activation(probs2[:, t % 2, :], probs2[:, t % 2, :], ACT.Exp,
                               scale=float(AD) ** -0.5).then_inc(S["s2_exp"], 1)

            for g in range(4):
                act.wait_ge(S["v2_mm"], g + 1)
                copy(v_sb[:, 2 * g:2 * g + 2, :].rearrange("p t n -> p (t n)"), R[g][:, :]).then_inc(S["v2"], 1)
                if g == 1:
                    self_exp(0)
            act.wait_ge(S["zeroed"], 3)
            act.wait_ge(S["v2"], 4)
            v_all = v_sb[:, :, :].rearrange("p t (g r d) -> p t g r d", g=8, r=2)
            copy(vexp_v[0:64, 0:NB:2, :, 0, :], v_all[0:64, :, :, 0, :])
            copy(vexp_v[64:128, 1:NB:2, :, 1, :], v_all[64:128, :, :, 1, :])
            for g in range(4):
                act.wait_ge(S["vs_mm"], g + 1)
                copy(vexp_v[0:64, 4 * g + 1:4 * g + 4:2, :, 0, :], v_parts(R[g])[0:64, :, :, 0, :]).then_inc(S["vs_a"], 1)
            act.wait_ge(ld["gu"], 16)
            act.wait_ge(L1["o_mm"], UNITS)
            for ic in range(IC):
                copy(w_r[:, 512 * ic:512 * (ic + 1)], gu_raw[:, 512 * ic:512 * (ic + 1)]).then_inc(S["gu_high"], 1)
            act.wait_ge(ld["wr"], 16)
            copy(wr_h.rearrange("p k n -> p (k n)"), wr_raw[:, :, :].rearrange("p k n -> p (k n)")).then_inc(S["wr_high"], 1)

            def rms_normed(hf):
                act.wait_ge(S["rstd"], 2 * 4 + hf + 1)
                for t in range(4 * hf, 4 * hf + 4):
                    copy(nb[:, t, :], x1[:, t, :], rstd[:, t:t + 1]).then_inc(S["normed"], 1)

            for t in range(NT + 1):
                if t < NT:
                    act.wait_ge(S["pt2_mm"], t + 1)
                    copy(pt2[t % 2][:, 0:512], R[0][:, :])
                    copy(pt2[t % 2][:, 512:1024], R[1][:, :]).then_inc(S["pt2"], 1)
                if t >= 1:
                    act.wait_ge(S["hT_mm"], t)
                    copy(hT_h[:, t - 1, :, :].rearrange("p k n -> p (k n)"), R[3][:, 0:DM]).then_inc(S["hT_high"], 1)
                if t + 1 < NT:
                    self_exp(t + 1)
                if t == NT - 2:
                    x_high(4, 1, (0,), Y)
                if t == NT - 3:
                    rms_normed(0)

            def expert_unit(u, splits, between=None):
                def silu(ic):
                    act.wait_ge(S["gu_mm"], u.count(8, 2 * ic + 1))
                    if u.after_zero(4, ic - 1):
                        act.wait_ge(S["prod"], u.count(4, ic - 1))
                    act.activation(silu_buf[:, ic % 2, :], R[2 * (ic % 2)][:, :], ACT.Silu).then_inc(S["silu"], 1)

                def high(ic):
                    act.wait_ge(S["prod"], u.count(4, ic + 1))
                    copy(hx_h[:, u.half(), ic, :], prod_buf[:, ic, :]).then_inc(S["act_high"], 1)
                    if splits:
                        act.wait_ge(S["gu_mm"], u.count(8, 2 * ic + 2))
                        if ic == 0:
                            act.wait_ge(ld["gu"], u.i * 16 + 32)
                        copy(w_r[:, 512 * ic:512 * (ic + 1)], gu_raw[:, 512 * ic:512 * (ic + 1)]).then_inc(S["gu_high"], 1)

                for ic in range(IC):
                    silu(ic)
                    if ic >= 1:
                        high(ic - 1)
                    if between and ic in between:
                        between[ic]()
                high(IC - 1)

            def down_high(e):
                act.wait_ge(ld["dn"], e * 16 + 16)
                if not isinstance(e, int) or e > 0:
                    act.wait_ge(S["y_mm"], e * 8)
                copy(w_r[:, 4096:5120], dn_raw).then_inc(S["dn_high"], 1)

            def top_exp():
                act.wait_ge(S["top_gap"], 1)
                act.activation(tiny[:, 1, :], tiny[:, 0, :], ACT.Exp).then_inc(S["top_exp"], 1)

            expert_unit(Unit(0, 0), False, {0: lambda: rms_normed(1), 2: lambda: x_high(4, 1, (1,), Y)})
            down_high(0)
            expert_unit(Unit(0, 1), True, {1: top_exp})
            with act.Fori(1, NE - 1) as e:
                expert_unit(Unit(e, 0), False)
                down_high(e)
                expert_unit(Unit(e, 1), True)
            expert_unit(Unit(NE - 1, 0), False)
            down_high(NE - 1)
            expert_unit(Unit(NE - 1, 1), False)

        @block.vector
        def _(dve):
            link = Chain(dve, S["dve_step"])

            def norm_stats(hf, src):
                for t in range(4 * hf, 4 * hf + 4):
                    ins = dve.bn_stats(bn6[:, t, :], src[:, t, :])
                link(ins)
                for t in range(4 * hf, 4 * hf + 4):
                    ins = dve.bn_aggr(mean_var[:, t, :], bn6[:, t, :])
                ins.then_inc(S["stats"], 1)

            def normalise(hf, src, dst, scale=rstd):
                for t in range(4 * hf, 4 * hf + 4):
                    dve.tensor_scalar(dst[:, t, :], src[:, t, :], mean_var[:, t, 0:1], scale[:, t:t + 1],
                                      ALU.subtract, ALU.mult).then_inc(S["normed"], 1)

            def x_low(turn, w=None, halves=(0, 1), banks=R):
                for hf in halves:
                    for k in range(KC):
                        dve.wait_ge(S["xT_high"], 4 * turn + 2 * hf + k + 1)
                        bank = banks[2 * hf + k][:, :]
                        if w is None:
                            ins = dve.tensor_tensor(xT_half(xT_l, k, hf), bank, f(xT_half(xT_h, k, hf)), ALU.subtract)
                        else:
                            ins = dve.scalar_tensor_tensor(out=xT_half(xT_l, k, hf), in0=bank, scalar=w_ln[:, w, k:k + 1],
                                                           in1=f(xT_half(xT_h, k, hf)), op0=ALU.mult, op1=ALU.subtract)
                        ins.then_inc(S["xT_low"], 1)

            def norm_in(turn, before, scale=rstd, ready=None, w=None):
                sem, base = ready or (S["rstd"], 2 * turn)
                before(0)
                norm_stats(0, x_res)
                before(1)
                dve.wait_ge(sem, base + 1)
                normalise(0, x_res, nb, scale)
                norm_stats(1, x_res)
                x_low(turn, w, (0,))
                dve.wait_ge(sem, base + 2)
                normalise(1, x_res, nb, scale)
                x_low(turn, w, (1,))

            def add_gated(L, g):
                def go(hf):
                    dve.wait_ge(L["o_mm"], UNITS - 1 + hf)
                    for t in range(4 * hf, 4 * hf + 4):
                        ins = dve.scalar_tensor_tensor(out=x_res[:, t, :], in0=y_tile(t), scalar=tgates[:, g:g + 1],
                                                       in1=x_res[:, t, :], op0=ALU.mult, op1=ALU.add)
                    link(ins)
                return go

            norm_in(0, lambda hf: dve.wait_ge(ld[f"x{hf}"], 16))
            dve.wait_ge(ld["gqk"], 16)
            dve.tensor_tensor(gqk[:, :], gq_gk[:, 0:1], gq_gk[:, 1:2], ALU.mult).then_inc(S["gqk"], 1)
            dve.wait_ge(S["zeroed"], 1)

            def sub_max(L, u1, src):
                c = u1.half()
                dve.tensor_reduce(smax[:, c, :], src, AX.X, ALU.max).then_inc(L["smax"], 1)
                dve.wait_ge(L["smax"], u1.count(1, 1))
                dve.tensor_tensor(probs[:, 8 * c:8 * c + 8, :], src,
                                  smax[:, c, :].unsqueeze(2).broadcast_to([P, 8, SQ]), ALU.subtract).then_inc(L["sub"], 1)

            def sum_exp(L, u1):
                c = u1.half()
                dve.wait_ge(L["exp"], u1.count(1, 1))
                dve.tensor_reduce(ssum[:, c, :], probs[:, 8 * c:8 * c + 8, :], AX.X, ALU.add).then_inc(L["ssum"], 1)
                dve.wait_ge(L["ssum"], u1.count(1, 1))

            def probs_T(L, n, bank):
                dve.wait_ge(L["pt_mm"], n.count(1, 1))
                dve.tensor_copy(probsT[64:128, :, 1, :],
                                bank[64:128, :].rearrange("p (j n) -> p j n", j=4)).then_inc(L["pt_v"], 1)

            def attended(L, n, part, bank):
                dve.wait_ge(L["ac_high"], n.count(2, part + 1))
                t = 4 * n.half() + 2 * part
                dve.tensor_tensor(ac_l[:, :, t:t + 2, :].rearrange("p h t n -> p t h n"),
                                  bank[:, :].rearrange("p (t h n) -> p t h n", t=2, h=2),
                                  f(ac_h[:, :, t:t + 2, :]).rearrange("p h t n -> p t h n"),
                                  ALU.subtract).then_inc(L["ac_low"], 1)

            def wk_low(j):
                dve.wait_ge(L0["w_high"], j + 1)
                dve.tensor_tensor(wk_l, wk_raw[:, bass.ds(j * 256, 256)], f(wk_h), ALU.subtract).then_inc(L0["wk_low"], 1)

            def step0(n):
                u1, u2, u3 = n.at(1), n.at(2), n.at(3)

                def sum_squares(u, j):
                    dve.wait_ge(L0["squares"], u.count(4, j + 1))
                    dve.tensor_reduce(sumsq[:, j, :], squares[:, j % 2, :, :], AX.X, ALU.add).then_inc(L0["sumsq"], 1)

                def scale(u, j):
                    dve.wait_ge(L0["rnorm"], u.count(3, (1, 1, 2, 3)[j]))
                    dve.tensor_tensor(raw[:, j, :, :], raw[:, j, :, :],
                                      rnorm[:, j, :].unsqueeze(2).broadcast_to([P, 4, HD]),
                                      ALU.mult).then_inc(L0["scaled"], 1)

                if u1.there():
                    dve.wait_ge(L0["scores"], u1.count(1, 1))
                    sub_max(L0, u1, R[0][:, :].rearrange("p (b k) -> p b k", b=8))
                if u2.there():
                    sum_squares(u2, 3)
                if n.c == 1 and pair_there(n.i + 2) and not step_is(n, -3):
                    wk_low(n.i + 2)
                if n.there():
                    probs_T(L0, n, R[3])
                if u2.there():
                    scale(u2, 2)
                    scale(u2, 3)
                if n.c == 1 and pair_there(n.i):
                    dve.wait_ge(L0["vo_high"], n.i + 1)
                    dve.tensor_tensor(vo_l.rearrange("p h n -> p (h n)"), vo0[:, bass.ds(n.i * 512, 512)],
                                      f(vo_h.rearrange("p h n -> p (h n)")), ALU.subtract).then_inc(L0["vo_low"], 1)
                if u1.there():
                    sum_exp(L0, u1)
                    dve.reciprocal(srec[:, u1.half(), :], ssum[:, u1.half(), :]).then_inc(L0["srec"], 1)
                if u3.there():
                    sum_squares(u3, 0)
                if n.there():
                    attended(L0, n, 0, R[2])
                if u3.there():
                    sum_squares(u3, 1)
                if n.there():
                    attended(L0, n, 1, R[1])
                if u3.there():
                    scale(u3, 0)
                    scale(u3, 1)
                    sum_squares(u3, 2)
                if step_is(n, 3):
                    dve.wait_ge(ld["small"], SMALL)
                    dve.tensor_reduce(mask_any[:, :], mask_u8[:, :].rearrange("p (b k) -> p b k", b=NB), AX.X,
                                      ALU.max).then_inc(S["mask_any"], 1)
                    dve.tensor_scalar(mask_add[:, :, :].rearrange("p b k -> p (b k)"), mask_u8[:, :], 1.0, BIG,
                                      ALU.subtract, ALU.mult).then_inc(S["mask_add"], 1)

            pipeline(dve, step0, 3)

            dve.wait_ge(S["gates"], 1)
            norm_in(1, add_gated(L0, 0))
            def add_ffn(hf):
                v = [tiny[:, i, 4 * hf:4 * hf + 4] for i in range(12)]
                dve.wait_ge(S["ffn_len0"], hf + 1)
                dve.tensor_scalar(v[1], v[3], 1e-7, None, ALU.max).then_inc(S["ffn_len"], 1)
                dve.wait_ge(S["ffn_len"], hf + 1)
                link(dve.tensor_scalar(v[4], v[1], 1e-7, None, ALU.add))
                link(dve.reciprocal(v[5], v[4]))
                dve.wait_ge(S["ffn_tanh"], hf + 1)
                link(dve.tensor_tensor(v[6], v[2], v[5], ALU.mult))
                link(dve.tensor_tensor(v[7], v[6], v[3], ALU.mult))
                link(dve.tensor_scalar(v[7], v[7], 1e-7, None, ALU.max))
                link(dve.reciprocal(v[8], v[7]))
                link(dve.tensor_scalar(v[8], v[8], 0.99, 1.0, ALU.mult, ALU.min))
                link(dve.scalar_tensor_tensor(out=v[10], in0=v[8], scalar=tgates[:, 2:3], in1=v[6],
                                              op0=ALU.mult, op1=ALU.mult))
                for t in range(4 * hf, 4 * hf + 4):
                    ins = dve.scalar_tensor_tensor(out=x_res[:, t, :], in0=y_tile(t), scalar=tiny[:, 10, t:t + 1],
                                                   in1=x_res[:, t, :], op0=ALU.mult, op1=ALU.add)
                link(ins)

            norm_in(2, add_ffn)

            def step1(n):
                u1, u2 = n.at(1), n.at(2)
                B = [R[(2 * n.half() + k) % 4] for k in range(4)]
                if u1.there():
                    c = u1.half()
                    p = probs[:, 8 * c:8 * c + 8, :]
                    dve.wait_ge(L1["scores"], u1.count(1, 1))
                    dve.tensor_tensor(p, B[0][:, :].rearrange("p (b k) -> p b k", b=8), mask_add[:, 8 * c:8 * c + 8, :],
                                      ALU.add).then_inc(L1["masked"], 1)
                    dve.wait_ge(L1["masked"], u1.count(1, 1))
                    sub_max(L1, u1, p)
                if n.there():
                    probs_T(L1, n, B[2])
                if u1.there():
                    sum_exp(L1, u1)
                    dve.reciprocal(srec[:, c, :], ssum[:, c, :]).then_inc(L1["srec0"], 1)
                    dve.wait_ge(L1["srec0"], u1.count(1, 1))
                    dve.tensor_tensor(srec[:, c, :], srec[:, c, :], mask_any[:, 8 * c:8 * c + 8],
                                      ALU.mult).then_inc(L1["srec"], 1)
                if n.there():
                    attended(L1, n, 0, B[0])
                    attended(L1, n, 1, B[1])

            pipeline(dve, step1, 2)

            norm_in(3, add_gated(L1, 1), rms_rstd, (S["rms_rstd"], 0), 0)
            def key_blocks(t):
                if t >= 2:
                    dve.wait_ge(S["s2_mm"], t - 1)
                for oc in range(KC):
                    c = SQ * 2 * t
                    ins = dve.tensor_tensor(kexp[:, t % 2, 0, oc, :].rearrange("p (h k) -> p h k", h=8),
                                            kT2[:, oc, c:c + SQ].unsqueeze(1).broadcast_to([P, 8, SQ]),
                                            head_mask[:, :].unsqueeze(2).broadcast_to([P, 8, SQ]), ALU.mult)
                ins.then_inc(S["kexp_v"], 1)

            def self_softmax(t):
                p = probs2[:, t % 2, :].rearrange("p (h k) -> p h k", k=SQ)
                scores = [Y[2 * (t % 2) + oc][:, :].rearrange("p (h k) -> p h k", k=SQ) for oc in range(KC)]
                dve.wait_ge(S["s2_mm"], t + 1)
                for oc in range(KC):
                    ins = dve.tensor_reduce(row_max[:, t % 2, 8 * oc:8 * oc + 8], scores[oc], AX.X, ALU.max)
                ins.then_inc(S["s2_row_max"], 1)
                dve.wait_ge(S["s2_row_max"], t + 1)
                if t >= 2:
                    dve.wait_ge(S["pt2_mm"], t - 1)
                for oc in range(KC):
                    ins = dve.tensor_tensor(p[:, 8 * oc:8 * oc + 8, :], scores[oc],
                                            row_max[:, t % 2, 8 * oc:8 * oc + 8].unsqueeze(2).broadcast_to([P, 8, SQ]),
                                            ALU.subtract)
                ins.then_inc(S["s2_sub"], 1)

            def self_sum(t):
                p = probs2[:, t % 2, :].rearrange("p (h k) -> p h k", k=SQ)
                dve.wait_ge(S["s2_exp"], t + 1)
                link(dve.tensor_reduce(row_sum[:, t % 2, :], p, AX.X, ALU.add))
                dve.reciprocal(row_rec[:, t % 2, :], row_sum[:, t % 2, :]).then_inc(S["s2_rec"], 1)

            for hf in range(2):
                for oc in range(KC):
                    dve.wait_ge(S["qk2_mm"], 4 * hf + 2 + oc + 1)
                    dve.tensor_copy(kT2[:, oc, HALF * hf:HALF * (hf + 1)], (Y, R)[hf][2 + oc][:, :]).then_inc(S["k2"], 1)
                dve.wait_ge(S["k2"], 2 * hf + 2)
                if hf == 0:
                    key_blocks(0)
                    key_blocks(1)
            self_softmax(0)
            dve.wait_ge(S["zeroed"], 3)
            self_sum(0)
            for g in range(4):
                dve.wait_ge(S["vs_mm"], g + 1)
                dve.tensor_copy(vexp_v[64:128, 4 * g:4 * g + 3:2, :, 1, :],
                                v_parts(R[g])[64:128, :, :, 1, :]).then_inc(S["vs_v"], 1)
            key_blocks(2)

            def self_add(t):
                dve.wait_ge(S["wo2_mm"], t + 1)
                dve.wait_ge(S["x1"], t // 4 + 1)
                dve.tensor_tensor(x1[:, t, :], R[3][:, DM:2 * DM], x1[:, t, :], ALU.add).then_inc(S["x2"], 1)
                dve.wait_ge(S["x2"], t + 1)
                link(dve.bn_stats(bn6[:, t, :], x1[:, t, :]))
                link(dve.bn_aggr(mean_var[:, t, :], bn6[:, t, :]))
                if t % 4 == 3:
                    m, v = mean_var[:, t - 3:t + 1, 0], mean_var[:, t - 3:t + 1, 1]
                    link(dve.tensor_tensor(m, m, m, ALU.mult))
                    dve.tensor_tensor(v, v, m, ALU.add).then_inc(S["stats"], 1)

            for t in range(NT + 1):
                if t + 1 < NT:
                    self_softmax(t + 1)
                if t >= 1:
                    dve.wait_ge(S["hT_high"], t)
                    dve.tensor_tensor(hT_l[:, t - 1, :, :].rearrange("p k n -> p (k n)"), R[3][:, 0:DM],
                                      f(hT_h[:, t - 1, :, :].rearrange("p k n -> p (k n)")),
                                      ALU.subtract).then_inc(S["hT_low"], 1)
                if t == NT - 1:
                    x_low(4, 1, (0,), Y)
                if t < NT:
                    dve.wait_ge(S["s2_rec"], t + 1)
                    dve.wait_ge(S["av2_mm"], t + 1)
                    dve.tensor_tensor(nb[:, t, :].rearrange("p (h d) -> p h d", h=AH),
                                      R[2][:, 0:DM].rearrange("p (h d) -> p h d", h=AH),
                                      row_rec[:, t % 2, :].unsqueeze(2).broadcast_to([P, AH, AD]),
                                      ALU.mult).then_inc(S["h2"], 1)
                if 1 <= t < NT:
                    self_add(t - 1)
                if t + 1 < NT:
                    self_sum(t + 1)

            dve.wait_ge(S["wr_high"], 1)
            dve.tensor_tensor(wr_l, wr_raw[:, :, :], f(wr_h), ALU.subtract).then_inc(S["wr_low"], 1)
            self_add(NT - 1)

            def top_two():
                dve.wait_ge(S["route_mm"], 1)
                both = Y[3][:, 0:2 * NT * NE].rearrange("p (t s e) -> p t s e", t=NT, s=2)
                link(dve.tensor_copy(logits[:, :, :], both[:, :, 0, :]))
                link(dve.tensor_tensor(logits[:, :, :], both[:, :, 1, :], logits[:, :, :], ALU.add))
                for t in range(NT):
                    ins = dve.max(top8[:, t, :], logits[:, t, :])
                link(ins)
                for t in range(NT):
                    ins = dve.max_index(top8_at[:, t, :], top8[:, t, :], logits[:, t, :])
                link(ins)
                link(dve.tensor_copy(top_at[:, :, :], top8_at[:, :, 0:2]))
                dve.tensor_tensor(tiny[:, 0, :], top8[:, :, 1], top8[:, :, 0], ALU.subtract).then_inc(S["top_gap"], 1)

            def expert_weights():
                dve.wait_ge(S["top_exp"], 1)
                link(dve.tensor_scalar(tiny[:, 2, :], tiny[:, 1, :], 1.0, None, ALU.add))
                link(dve.reciprocal(tiny[:, 3, :], tiny[:, 2, :]))
                link(dve.tensor_tensor(tiny[:, 4, :], tiny[:, 1, :], tiny[:, 3, :], ALU.mult))
                for j in range(2):
                    link(dve.tensor_tensor(chosen[:, j, :, :], iota8[:, :].unsqueeze(2).broadcast_to([P, NE, NT]),
                                           top_at[:, :, j].unsqueeze(1).broadcast_to([P, NE, NT]), ALU.is_equal))
                    link(dve.tensor_tensor(chosen[:, j, :, :], chosen[:, j, :, :],
                                           tiny[:, 3 + j, :].unsqueeze(1).broadcast_to([P, NE, NT]), ALU.mult))
                link(dve.tensor_tensor(cw[:, :].rearrange("p (e t) -> p e t", e=NE), chosen[:, 0, :, :], chosen[:, 1, :, :],
                                       ALU.add))

            def products(u, between=None):
                def product(ic):
                    dve.wait_ge(S["silu"], u.count(4, ic + 1))
                    dve.wait_ge(S["gu_mm"], u.count(8, 2 * ic + 2))
                    if u.after_zero(4, ic - 3):
                        dve.wait_ge(S["act_low"], u.count(4, ic - 3))
                    dve.tensor_tensor(prod_buf[:, ic, :], R[2 * (ic % 2) + 1][:, :], silu_buf[:, ic % 2, :],
                                      ALU.mult).then_inc(S["prod"], 1)

                def low(ic):
                    dve.wait_ge(S["act_high"], u.count(4, ic + 1))
                    dve.tensor_tensor(hx_l[:, u.half(), ic, :], prod_buf[:, ic, :], f(hx_h[:, u.half(), ic, :]),
                                      ALU.subtract).then_inc(S["act_low"], 1)

                for ic in range(IC):
                    product(ic)
                    if ic >= 1:
                        low(ic - 1)
                    if between and ic in between:
                        between[ic]()
                low(IC - 1)

            def add_expert(u):
                if u.half() == 0:
                    dve.tensor_copy(cw_now[:, :], cw[:, bass.ds(u.i * NT, NT)]).then_inc(S["cw_now"], 1)
                    dve.wait_ge(S["cw_now"], u.i + 1)
                for j in range(4):
                    t = 4 * u.half() + j
                    dve.wait_ge(S["y_mm"], u.count(4, j // 2 * 2 + 2))
                    dve.scalar_tensor_tensor(out=x1[:, t, :], in0=y_tile(t), scalar=cw_now[:, t:t + 1],
                                             in1=x1[:, t, :], op0=ALU.mult, op1=ALU.add).then_inc(S["y_added"], 1)

            products(Unit(0, 0), {2: lambda: x_low(4, 1, (1,), Y)})
            top_two()
            products(Unit(0, 1), {1: expert_weights})
            add_expert(Unit(0, 0))
            products(Unit(1, 0))
            add_expert(Unit(0, 1))
            with dve.Fori(1, NE - 1) as e:
                for c in range(2):
                    products(Unit(e, c + 1))
                    add_expert(Unit(e, c))
            products(Unit(NE - 1, 1))
            dve.wait_ge(S["y_added"], 4 * (UNITS - 2))
            link(dve.tensor_scalar(cw_now[:, :], cw[:, (NE - 1) * NT:NE * NT], tgates[:, 3:4], None, ALU.mult))
            for t in range(NT):
                ins = dve.scalar_tensor_tensor(out=nb[:, t, :], in0=x1[:, t, :], scalar=tgates[:, 3:4],
                                               in1=x_res[:, t, :], op0=ALU.mult, op1=ALU.add)
            link(ins)
            for t in range(NT):
                dve.wait_ge(S["y_mm"], 8 * (NE - 1) + t // 2 * 2 + 2)
                ins = dve.scalar_tensor_tensor(out=nb[:, t, :], in0=y_tile(t), scalar=cw_now[:, t:t + 1],
                                               in1=nb[:, t, :], op0=ALU.mult, op1=ALU.add)
                if t % 2 == 1:
                    ins.then_inc(S["out_ready"], 1)

        @block.gpsimd
        def _(pool):
            def rstd_of(k, halves=(0, 1)):
                for hf in halves:
                    s = slice(4 * hf, 4 * hf + 4)
                    pool.wait_ge(S["stats"], 2 * k + hf + 1)
                    pool.tensor_scalar(var_eps[:, s], mean_var[:, s, 1], EPS, None, ALU.add).then_inc(S["var_eps"], 1)
                    pool.wait_ge(S["var_eps"], 2 * k + hf + 1)
                    pool.tensor_tensor(rstd[:, s], var_eps[:, s], neg_half[:, 0:4], ALU.pow).then_inc(S["rstd"], 1)

            pool.memset(neg_half[:, :], -0.5)
            pool.memset(eps8[:, :], EPS)
            pool.memset(pos_half[:, :], 0.5).then_inc(S["halves"], 1)
            pool.wait_ge(S["halves"], 1)
            rstd_of(0, (0,))
            pool.wait_ge(S["ctx_high"], 1)
            pool.tensor_tensor(ctxT_l, ctxT[:, :], f(ctxT_h), ALU.subtract).then_inc(S["ctx_low"], 1)
            rstd_of(0, (1,))

            def probabilities(L, u1):
                c = u1.half()
                pool.wait_ge(L["srec"], u1.count(1, 1))
                p = probs[:, 8 * c:8 * c + 8, :]
                pool.tensor_tensor(p, p, srec[:, c, :].unsqueeze(2).broadcast_to([P, 8, SQ]),
                                   ALU.mult).then_inc(L["prob"], 1)

            def vo_low(L, src, n):
                if n.c == 1 and pair_there(n.i):
                    pool.wait_ge(L["vo_high"], n.i + 1)
                    pool.tensor_tensor(vo_l.rearrange("p h n -> p (h n)"), src[:, bass.ds(n.i * 512, 512)],
                                       f(vo_h.rearrange("p h n -> p (h n)")), ALU.subtract).then_inc(L["vo_low"], 1)

            def w_low0(j):
                pool.wait_ge(L0["w_high"], j + 1)
                pool.tensor_tensor(w_r[:, 512:1024], wq_raw[:, bass.ds(j * 512, 512)], f(w_r[:, 0:512]),
                                   ALU.subtract).then_inc(L0["w_low"], 1)

            def step0(n):
                u1, u3 = n.at(1), n.at(3)
                def norms(k, tiles):
                    j, n = tiles[0], len(tiles)
                    pool.wait_ge(L0["sumsq"], u3.count(4, tiles[-1] + 1))
                    pool.tensor_tensor(sumsq_eps[:, j:j + n, :].rearrange("p j g -> p (j g)"),
                                       sumsq[:, j:j + n, :].rearrange("p j g -> p (j g)"), eps8[:, 0:4 * n],
                                       ALU.add).then_inc(L0["sumsq_eps"], 1)
                    pool.wait_ge(L0["sumsq_eps"], u3.count(3, k))
                    pool.tensor_tensor(rnorm[:, j:j + n, :].rearrange("p j g -> p (j g)"),
                                       sumsq_eps[:, j:j + n, :].rearrange("p j g -> p (j g)"), neg_half[:, 0:4 * n],
                                       ALU.pow).then_inc(L0["rnorm"], 1)

                if u1.there():
                    probabilities(L0, u1)
                if u3.there():
                    norms(1, (0, 1))
                if n.c == 0 and pair_there(n.i + 2):
                    w_low0(n.i + 2)
                if u3.there():
                    norms(2, (2,))
                    norms(3, (3,))

            w_low0(0)
            pool.tensor_tensor(wk_l, wk_raw[:, 0:256], f(wk_h), ALU.subtract).then_inc(L0["wk_low"], 1)
            pool.memset(probsT[:, :, :, :], 0.0).then_inc(S["zeroed"], 1)
            pipeline(pool, step0, 3)
            def w_low1(j):
                pool.wait_ge(L1["w_high"], j + 1)
                pool.tensor_tensor(w_r[:, 512:1024], m1[:, bass.ds(j * 512, 512)], f(w_r[:, 0:512]),
                                   ALU.subtract).then_inc(L1["w_low"], 1)

            pool.wait_ge(ld["wf"], 16)
            wf_k = wf_raw.rearrange("p (k n) -> p k n", k=KC)
            pool.tensor_tensor(wf_k, wf_k, ffn_scale[:, :].unsqueeze(1).broadcast_to([P, KC, DM]),
                               ALU.mult).then_inc(S["wf_scaled"], 1)
            rstd_of(1, (0,))
            pool.wait_ge(S["wf_high"], 1)
            pool.tensor_tensor(w_r[:, 5120:5632], wf_raw, f(w_r[:, 4608:5120]), ALU.subtract).then_inc(S["wf_low"], 1)
            rstd_of(1, (1,))
            for hf in range(2):
                s = slice(4 * hf, 4 * hf + 4)
                pool.wait_ge(S["ffn_sumsq"], 4 * hf + 4)
                pool.tensor_tensor(tiny[:, 3, s], tiny[:, 0, s], pos_half[:, 0:4], ALU.pow).then_inc(S["ffn_len0"], 1)
            w_low1(0)
            rstd_of(2)

            def step1(n):
                u1 = n.at(1)
                vo_low(L1, vo1, n)
                if u1.there():
                    probabilities(L1, u1)
                if n.c == 1 and pair_there(n.i + 2):
                    w_low1(n.i + 2)
                if aw_part(n):
                    part, high, low, raw_w = aw_part(n)
                    pool.wait_ge(S["aw_high"], part + 1)
                    pool.tensor_tensor(low, raw_w, f(high), ALU.subtract).then_inc(S["aw_low"], 1)

            pipeline(pool, step1, 2)
            pool.memset(reg_d[:, 0:2048], 0.0).then_inc(S["zeroed"], 1)
            pool.memset(reg_d[:, 2048:4096], 0.0).then_inc(S["zeroed"], 1)
            for hf in range(2):
                s = slice(4 * hf, 4 * hf + 4)
                pool.wait_ge(S["stats"], 2 * 3 + hf + 1)
                pool.tensor_scalar(rms_var[:, s], mean_var[:, s, 1], 1.0 + EPS, EPS * EPS, ALU.mult,
                                   ALU.add).then_inc(S["rms_var"], 1)
                pool.wait_ge(S["rms_var"], hf + 1)
                pool.tensor_tensor(rms_rstd[:, s], rms_var[:, s], neg_half[:, 0:4], ALU.pow).then_inc(S["rms_rstd"], 1)
            rstd_of(3)
            def key_blocks(t):
                if t % 4 == 0:
                    pool.wait_ge(S["k2"], 2 * (t // 4) + 2)
                if t >= 2:
                    pool.wait_ge(S["s2_mm"], t - 1)
                for b in (1,) if t < 3 else (0, 1):
                    for oc in range(KC):
                        c = SQ * (2 * t + b)
                        ins = pool.tensor_tensor(kexp[:, t % 2, b, oc, :].rearrange("p (h k) -> p h k", h=8),
                                                 kT2[:, oc, c:c + SQ].unsqueeze(1).broadcast_to([P, 8, SQ]),
                                                 head_mask[:, :].unsqueeze(2).broadcast_to([P, 8, SQ]), ALU.mult)
                ins.then_inc(S["kexp_p"], 1)

            def gate_up_low(j, ic):
                pool.wait_ge(S["gu_high"], j * IC + (ic + 1))
                s = slice(512 * ic, 512 * (ic + 1))
                pool.tensor_tensor(w_r[:, 2048 + 512 * ic:2048 + 512 * (ic + 1)], gu_raw[:, s], f(w_r[:, s]),
                                   ALU.subtract).then_inc(S["gu_low"], 1)

            def down_low(e):
                pool.wait_ge(S["dn_high"], e + 1)
                pool.tensor_tensor(w_r[:, 5120:6144], dn_raw, f(w_r[:, 4096:5120]), ALU.subtract).then_inc(S["dn_low"], 1)

            key_blocks(0)
            key_blocks(1)
            key_blocks(2)
            for hf in range(2):
                pool.wait_ge(S["rstd"], 2 * 3 + hf + 1)
                for t in range(4 * hf, 4 * hf + 4):
                    ins = pool.tensor_scalar(x1[:, t, :], x_res[:, t, :], mean_var[:, t, 0:1], rstd[:, t:t + 1],
                                             ALU.subtract, ALU.mult)
                ins.then_inc(S["x1"], 1)
            for t in range(NT - 1):
                if t + 3 < NT:
                    key_blocks(t + 3)
                if t < IC:
                    gate_up_low(0, t)
                if t == 4:
                    rstd_of(4, (0,))
            rstd_of(4, (1,))
            with pool.Fori(0, NE - 1) as e:
                down_low(e)
                for ic in range(IC):
                    gate_up_low(e + 1, ic)
            down_low(NE - 1)


def kernel(x, ctx_1024, mask_BxS2_bf1, g_xattn, g_ffn, L0_xattn_Wq, L0_xattn_Wk, L0_xattn_Wv, L0_xattn_Wo,
           L0_xattn_gq, L0_xattn_gk, L0_ffn_weight, L0_ffn_scale, L1_xattn_Wq, L1_xattn_Wk, L1_xattn_Wv, L1_xattn_Wo,
           L1_ffn_Wq, L1_ffn_Wk, L1_ffn_Wv, L1_ffn_Wo, L1_ffn_w_ln1, L1_ffn_w_ln2, L1_ffn_Wr, L1_ffn_Wg, L1_ffn_Wu,
           L1_ffn_Wd):
    import ml_dtypes
    import numpy as np
    import concourse.bacc as bacc
    from concourse import mybir as mb
    from concourse.bass_utils import run_bass_kernel_spmd

    def arr(v):
        return np.asarray(v)

    def rows(w, chunks):
        return arr(w).reshape(chunks, 128, -1).transpose(1, 0, 2)

    def inner_first(w, heads):
        return arr(w).reshape(arr(w).shape[0], heads, 128).transpose(2, 1, 0)

    x2 = arr(x).reshape(1024, 256)
    c2 = arr(ctx_1024).reshape(1024, 128)
    gu = np.stack([arr(L1_ffn_Wg), arr(L1_ffn_Wu)])
    gu = gu.reshape(2, 8, 4, 128, 2, 128).transpose(1, 5, 2, 0, 4, 3)
    dn = arr(L1_ffn_Wd).transpose(0, 2, 1).reshape(8, 4, 128, 256).transpose(0, 2, 1, 3)
    wattn = np.stack([arr(w).T.reshape(2, 128, 256) for w in (L1_ffn_Wq, L1_ffn_Wk, L1_ffn_Wv, L1_ffn_Wo)])
    key, q = np.arange(64)[None, :], np.arange(128)[:, None] % 64
    data = {
        "x": x2, "ctx": c2, "ctxT": c2.T, "mask": arr(mask_BxS2_bf1).reshape(-1).view(np.uint8),
        "gates": np.concatenate([arr(g_xattn), arr(g_ffn)]),
        "gqk": np.stack([arr(L0_xattn_gq), arr(L0_xattn_gk)], axis=1),
        "wq0": rows(L0_xattn_Wq, 2).reshape(128, 2, 8, 256).transpose(0, 2, 1, 3).reshape(128, 4096),
        "wk0": arr(L0_xattn_Wk), "wv0T": inner_first(L0_xattn_Wv, 16).reshape(128, 2048),
        "wo0": rows(L0_xattn_Wo, 16).reshape(128, 4096),
        "wf": rows(L0_ffn_weight, 2).reshape(128, 512), "ffn_scale": arr(L0_ffn_scale),
        "wq1T": inner_first(L1_xattn_Wq, 16).reshape(128, 4096), "wk1T": inner_first(L1_xattn_Wk, 8).reshape(128, 1024),
        "wv1T": inner_first(L1_xattn_Wv, 8).reshape(128, 1024), "wo1": rows(L1_xattn_Wo, 16).reshape(128, 4096),
        "wattn": wattn.transpose(2, 0, 1, 3).reshape(128, 2048),
        "w_ln": np.stack([arr(L1_ffn_w_ln1), arr(L1_ffn_w_ln2)]).reshape(2, 2, 128).transpose(2, 0, 1),
        "wr": arr(L1_ffn_Wr).T.reshape(2, 128, 8).transpose(1, 0, 2),
        "gu": gu.reshape(8, 128, 2048),
        "dn": dn.reshape(8, 128, 1024),
        "c_ident": np.eye(128, dtype=np.float32),
        "c_swap": np.roll(np.eye(128, dtype=np.float32), 64, axis=1),
        "c_causal": np.where(key <= q, 0.0, -1e30).astype(ml_dtypes.bfloat16),
        "c_ident_b": np.eye(128, dtype=ml_dtypes.bfloat16),
        "c_heads": (np.arange(128)[:, None] // 16 == np.arange(8)[None, :]).astype(np.float32),
        "c_iota": np.tile(np.arange(8, dtype=np.float32), (128, 1)),
    }
    nc = bacc.Bacc("TRN2", target_bir_lowering=False, num_devices=1)
    arrays, aps = {}, {}
    for name, v in data.items():
        v = np.ascontiguousarray(v)
        arrays["in_" + name] = v
        aps[name] = nc.dram_tensor("in_" + name, v.shape, mb.dt.from_np(v.dtype), kind="ExternalInput").ap()
    aps["out"] = nc.dram_tensor("out_x", (1024, 256), mb.dt.float32, kind="ExternalOutput").ap()
    build(nc, aps)
    r = run_bass_kernel_spmd(nc, [arrays], core_ids=[0])
    return r.results[0]["out_x"].reshape(16, 64, 256)
```
